# Optimizing a Trainium2 kernel written in Bass

```python
import numpy as np
import jax
import jax.numpy as jnp

def _softmax(x, axis=-1):
    return jax.nn.softmax(x, axis=axis)

def _gelu(x):
    return jax.nn.gelu(x, approximate=True)

def _silu(x):
    return jax.nn.silu(x)

def _sigmoid(x):
    return jax.nn.sigmoid(x)

def _layernorm(x, axis=-1, eps=1e-05):
    m = jnp.mean(x, axis=axis, keepdims=True)
    v = jnp.var(x, axis=axis, keepdims=True)
    return (x - m) / jnp.sqrt(v + eps)

def _scatter_add(tgt, idx, src, axis=0):
    return tgt.at[idx].add(src)

def _segment_sum(src, seg, n):
    return jax.ops.segment_sum(src, seg, n)
kernel_name = 'mk_perceiver_d2_seqx_r4_6f8087'

def setup_inputs(seed: int=0):
    np.random.seed(seed)
    _w = jnp.asarray

    def _rec_inputs():
        import jax
        import jax.numpy as jnp
        _rk = jax.random.key(seed)
        x = -0.0002928 + 1 * jax.random.normal(jax.random.fold_in(_rk, 1), (64, 32, 256), jnp.float32)
        _lenS = 32 - jax.random.randint(jax.random.fold_in(_rk, 7), (64,), 0, max(1, 32 // 4) + 1, jnp.int32)
        _lenS2 = 257 - jax.random.randint(jax.random.fold_in(_rk, 8), (64,), 0, max(1, 257 // 4) + 1, jnp.int32)
        _ctx_1024P = jax.random.normal(jax.random.fold_in(_rk, 11), (64, 16, 256), jnp.float32)
        _ctx_1024c = jax.random.dirichlet(jax.random.fold_in(_rk, 511), 0.3 * jnp.ones((16,), jnp.float32), (64, 257))
        _ctx_1024t = jnp.einsum('bsk,bkd->bsd', _ctx_1024c, _ctx_1024P)
        _ctx_1024t = _ctx_1024t * jax.lax.rsqrt(jnp.mean(jnp.square(_ctx_1024t)) + 1e-12) * 0.953939
        ctx_1024 = -1.39393e-06 + 0.999914 * (_ctx_1024t + 0.3 * jax.random.normal(jax.random.fold_in(_rk, 611), (64, 257, 256), jnp.float32))
        return (x, ctx_1024)
    x, ctx_1024 = _rec_inputs()

    def _L0_xattn_setup():
        import jax, jax.numpy as jnp
        import numpy as np
        import math
        D_MODEL = 256
        N_HEADS = 16
        key = jax.random.key(seed)
        ks = jax.random.split(key, 11)
        N, L, S = (2, 512, 512)
        d = D_MODEL
        s = 1.0 / math.sqrt(d)
        return {'queries': jax.random.normal(ks[0], (N, L, d), dtype=jnp.float32), 'keys': jax.random.normal(ks[1], (N, S, d), dtype=jnp.float32), 'values': jax.random.normal(ks[2], (N, S, d), dtype=jnp.float32), 'Wq': jax.random.normal(ks[3], (d, d), dtype=jnp.float32) * s, 'bq': jax.random.normal(ks[4], (d,), dtype=jnp.float32) * s, 'Wk': jax.random.normal(ks[5], (d, d), dtype=jnp.float32) * s, 'bk': jax.random.normal(ks[6], (d,), dtype=jnp.float32) * s, 'Wv': jax.random.normal(ks[7], (d, d), dtype=jnp.float32) * s, 'bv': jax.random.normal(ks[8], (d,), dtype=jnp.float32) * s, 'Wo': jax.random.normal(ks[9], (d, d), dtype=jnp.float32) * s, 'bo': jax.random.normal(ks[10], (d,), dtype=jnp.float32) * s}
    _L0_xattn_all = _L0_xattn_setup()
    _L0_xattn_in = {k: v for k, v in _L0_xattn_all.items() if k in ('Wq', 'bq', 'Wk', 'bk', 'Wv', 'bv', 'Wo', 'bo')}
    del _L0_xattn_all

    def _L0_attn_setup():
        import jax, jax.numpy as jnp
        import numpy as np
        N_HEAD = 16
        ROPE_BASE = 10000.0

        def rotate_half(x):
            half = x.shape[-1] // 2
            return jnp.concatenate((-x[..., half:], x[..., :half]), axis=-1)

        def rope_freqs(T, head_dim, dtype):
            inv_freq = 1.0 / ROPE_BASE ** (jnp.arange(0, head_dim, 2, dtype=jnp.float32) / head_dim)
            t = jnp.arange(T, dtype=jnp.float32)
            freqs = t[:, None] * inv_freq[None, :]
            emb = jnp.concatenate((freqs, freqs), axis=-1)
            return emb.astype(dtype)
        key = jax.random.key(seed)
        ks = jax.random.split(key, 9)
        B, T, C = (2, 512, 256)
        s = 1.0 / np.sqrt(C)
        return {'x': jax.random.normal(ks[0], (B, T, C), jnp.float32), 'Wq': jax.random.normal(ks[1], (C, C), jnp.float32) * s, 'bq': jnp.zeros((C,), jnp.float32), 'Wk': jax.random.normal(ks[2], (C, C), jnp.float32) * s, 'bk': jnp.zeros((C,), jnp.float32), 'Wv': jax.random.normal(ks[3], (C, C), jnp.float32) * s, 'bv': jnp.zeros((C,), jnp.float32), 'Wp': jax.random.normal(ks[4], (C, C), jnp.float32) * s, 'bp': jnp.zeros((C,), jnp.float32)}
    _L0_attn_all = _L0_attn_setup()
    _L0_attn_in = {k: v for k, v in _L0_attn_all.items() if k in ('Wq', 'bq', 'Wk', 'bk', 'Wv', 'bv', 'Wp', 'bp')}
    del _L0_attn_all

    def _L0_ffn_setup():
        import jax, jax.numpy as jnp
        import numpy as np
        B, K, D = (128, 32, 256)
        E = 32
        H = int(D * 0.25)

        def _rsqrt_uniform(key, shape, d):
            bound = d ** (-0.5)
            return jax.random.uniform(key, shape, jnp.float32, -bound, bound)
        key = jax.random.key(seed)
        ks = jax.random.split(key, 7)
        return {'x': jax.random.normal(ks[0], (B, K, D), jnp.float32), 'router_w': _rsqrt_uniform(ks[1], (E, D), D), 'router_b': _rsqrt_uniform(ks[2], (E,), D), 'weights1': _rsqrt_uniform(ks[3], (E, D, H), H), 'bias1': _rsqrt_uniform(ks[4], (E, H), H), 'weights2': _rsqrt_uniform(ks[5], (E, H, D), D), 'bias2': _rsqrt_uniform(ks[6], (E, D), D)}
    _L0_ffn_all = _L0_ffn_setup()
    _L0_ffn_in = {k: v for k, v in _L0_ffn_all.items() if k in ('router_w', 'router_b', 'weights1', 'bias1', 'weights2', 'bias2')}
    del _L0_ffn_all

    def _L1_xattn_setup():
        import jax, jax.numpy as jnp
        import numpy as np
        N, L, E, H, D = (4, 512, 256, 16, 64)
        key = jax.random.key(seed)
        ks = jax.random.split(key, 8)
        s = 1.0 / np.sqrt(E)
        return {'Q': jax.random.normal(ks[0], (N, L, E), jnp.float32), 'K': jax.random.normal(ks[1], (N, L, E), jnp.float32), 'V': jax.random.normal(ks[2], (N, L, E), jnp.float32), 'Wq': jax.random.normal(ks[3], (H * D, E), jnp.float32) * s, 'bq': jnp.zeros((H * D,), jnp.float32), 'Wk': jax.random.normal(ks[4], (H * D, E), jnp.float32) * s, 'bk': jnp.zeros((H * D,), jnp.float32), 'Wv': jax.random.normal(ks[5], (H * D, E), jnp.float32) * s, 'bv': jnp.zeros((H * D,), jnp.float32), 'Wo': jax.random.normal(ks[6], (E, H * D), jnp.float32) * s, 'bo': jnp.zeros((E,), jnp.float32)}
    _L1_xattn_all = _L1_xattn_setup()
    _L1_xattn_in = {k: v for k, v in _L1_xattn_all.items() if k in ('Wq', 'bq', 'Wk', 'bk', 'Wv', 'bv', 'Wo', 'bo')}
    del _L1_xattn_all

    def _L1_attn_setup():
        import jax, jax.numpy as jnp
        import numpy as np
        N_HEADS = 16
        key = jax.random.key(seed)
        ks = jax.random.split(key, 9)
        B, S, E = (2, 512, 256)
        s = 1.0 / np.sqrt(E)
        return {'x': jax.random.normal(ks[0], (B, S, E), jnp.float32), 'Wq': jax.random.normal(ks[1], (E, E), jnp.float32) * s, 'bq': jax.random.normal(ks[2], (E,), jnp.float32) * 0.01, 'Wk': jax.random.normal(ks[3], (E, E), jnp.float32) * s, 'bk': jax.random.normal(ks[4], (E,), jnp.float32) * 0.01, 'Wv': jax.random.normal(ks[5], (E, E), jnp.float32) * s, 'bv': jax.random.normal(ks[6], (E,), jnp.float32) * 0.01, 'Wo': jax.random.normal(ks[7], (E, E), jnp.float32) * s, 'bo': jax.random.normal(ks[8], (E,), jnp.float32) * 0.01}
    _L1_attn_all = _L1_attn_setup()
    _L1_attn_in = {k: v for k, v in _L1_attn_all.items() if k in ('Wq', 'bq', 'Wk', 'bk', 'Wv', 'bv', 'Wo', 'bo')}
    del _L1_attn_all

    def _L1_ffn_setup():
        import jax, jax.numpy as jnp
        import numpy as np
        H = 256
        F = 1024
        E = 8
        TOP_K = 2
        B, S = (1, 512)
        key = jax.random.key(seed)
        k0, k1, k2, k3 = jax.random.split(key, 4)
        hidden_states = jax.random.normal(k0, (B, S, H), dtype=jnp.float32)
        gate_w = jax.random.normal(k1, (E, H), dtype=jnp.float32) * 0.02
        gate_up_w = jax.random.normal(k2, (E, 2 * F, H), dtype=jnp.float32) * 0.02
        down_w = jax.random.normal(k3, (E, H, F), dtype=jnp.float32) * 0.02
        return {'hidden_states': hidden_states, 'gate_w': gate_w, 'gate_up_w': gate_up_w, 'down_w': down_w}
    _L1_ffn_all = _L1_ffn_setup()
    _L1_ffn_in = {k: v for k, v in _L1_ffn_all.items() if k in ('gate_w', 'gate_up_w', 'down_w')}
    del _L1_ffn_all
    return {'x': x, 'ctx_1024': ctx_1024, 'L0_xattn_Wq': _L0_xattn_in['Wq'], 'L0_xattn_bq': _L0_xattn_in['bq'], 'L0_xattn_Wk': _L0_xattn_in['Wk'], 'L0_xattn_bk': _L0_xattn_in['bk'], 'L0_xattn_Wv': _L0_xattn_in['Wv'], 'L0_xattn_bv': _L0_xattn_in['bv'], 'L0_xattn_Wo': _L0_xattn_in['Wo'], 'L0_xattn_bo': _L0_xattn_in['bo'], 'L0_attn_Wq': _L0_attn_in['Wq'], 'L0_attn_bq': _L0_attn_in['bq'], 'L0_attn_Wk': _L0_attn_in['Wk'], 'L0_attn_bk': _L0_attn_in['bk'], 'L0_attn_Wv': _L0_attn_in['Wv'], 'L0_attn_bv': _L0_attn_in['bv'], 'L0_attn_Wp': _L0_attn_in['Wp'], 'L0_attn_bp': _L0_attn_in['bp'], 'L0_ffn_router_w': _L0_ffn_in['router_w'], 'L0_ffn_router_b': _L0_ffn_in['router_b'], 'L0_ffn_weights1': _L0_ffn_in['weights1'], 'L0_ffn_bias1': _L0_ffn_in['bias1'], 'L0_ffn_weights2': _L0_ffn_in['weights2'], 'L0_ffn_bias2': _L0_ffn_in['bias2'], 'L1_xattn_Wq': _L1_xattn_in['Wq'], 'L1_xattn_bq': _L1_xattn_in['bq'], 'L1_xattn_Wk': _L1_xattn_in['Wk'], 'L1_xattn_bk': _L1_xattn_in['bk'], 'L1_xattn_Wv': _L1_xattn_in['Wv'], 'L1_xattn_bv': _L1_xattn_in['bv'], 'L1_xattn_Wo': _L1_xattn_in['Wo'], 'L1_xattn_bo': _L1_xattn_in['bo'], 'L1_attn_Wq': _L1_attn_in['Wq'], 'L1_attn_bq': _L1_attn_in['bq'], 'L1_attn_Wk': _L1_attn_in['Wk'], 'L1_attn_bk': _L1_attn_in['bk'], 'L1_attn_Wv': _L1_attn_in['Wv'], 'L1_attn_bv': _L1_attn_in['bv'], 'L1_attn_Wo': _L1_attn_in['Wo'], 'L1_attn_bo': _L1_attn_in['bo'], 'L1_ffn_gate_w': _L1_ffn_in['gate_w'], 'L1_ffn_gate_up_w': _L1_ffn_in['gate_up_w'], 'L1_ffn_down_w': _L1_ffn_in['down_w']}

def reference(x, ctx_1024, L0_xattn_Wq, L0_xattn_bq, L0_xattn_Wk, L0_xattn_bk, L0_xattn_Wv, L0_xattn_bv, L0_xattn_Wo, L0_xattn_bo, L0_attn_Wq, L0_attn_bq, L0_attn_Wk, L0_attn_bk, L0_attn_Wv, L0_attn_bv, L0_attn_Wp, L0_attn_bp, L0_ffn_router_w, L0_ffn_router_b, L0_ffn_weights1, L0_ffn_bias1, L0_ffn_weights2, L0_ffn_bias2, L1_xattn_Wq, L1_xattn_bq, L1_xattn_Wk, L1_xattn_bk, L1_xattn_Wv, L1_xattn_bv, L1_xattn_Wo, L1_xattn_bo, L1_attn_Wq, L1_attn_bq, L1_attn_Wk, L1_attn_bk, L1_attn_Wv, L1_attn_bv, L1_attn_Wo, L1_attn_bo, L1_ffn_gate_w, L1_ffn_gate_up_w, L1_ffn_down_w):
    import jax
    import jax.numpy as jnp

    def _L0_xattn_ref(queries, keys, values, Wq, bq, Wk, bk, Wv, bv, Wo, bo):
        import jax, jax.numpy as jnp
        import numpy as np
        import math
        D_MODEL = 256
        N_HEADS = 16
        N, L, _ = queries.shape
        S = keys.shape[1]
        H = N_HEADS
        q = (queries @ Wq.T + bq).reshape(N, L, H, -1)
        k = (keys @ Wk.T + bk).reshape(N, S, H, -1)
        v = (values @ Wv.T + bv).reshape(N, S, H, -1)
        D = k.shape[-1]
        sm = jnp.einsum('nlhd,nshd->nlhs', q, k) / math.sqrt(D)
        causal_mask = jnp.triu(jnp.ones((L, S), dtype=bool), k=1)
        sm = jnp.where(causal_mask[None, :, None, :], -jnp.inf, sm)
        sm = jax.nn.softmax(sm, axis=-1)
        attn = jnp.einsum('nlhs,nshd->nlhd', sm, v)
        new_values = attn.reshape(N, L, H * D)
        return new_values @ Wo.T + bo

    def _L0_attn_ref(x, Wq, bq, Wk, bk, Wv, bv, Wp, bp):
        import jax, jax.numpy as jnp
        import numpy as np
        N_HEAD = 16
        ROPE_BASE = 10000.0

        def rotate_half(x):
            half = x.shape[-1] // 2
            return jnp.concatenate((-x[..., half:], x[..., :half]), axis=-1)

        def rope_freqs(T, head_dim, dtype):
            inv_freq = 1.0 / ROPE_BASE ** (jnp.arange(0, head_dim, 2, dtype=jnp.float32) / head_dim)
            t = jnp.arange(T, dtype=jnp.float32)
            freqs = t[:, None] * inv_freq[None, :]
            emb = jnp.concatenate((freqs, freqs), axis=-1)
            return emb.astype(dtype)
        B, T, C = x.shape
        H = N_HEAD
        D = C // H

        def heads(y):
            return y.reshape(B, T, H, D).transpose(0, 2, 1, 3)
        q = heads(x @ Wq.T + bq)
        k = heads(x @ Wk.T + bk)
        v = heads(x @ Wv.T + bv)
        emb = rope_freqs(T, D, x.dtype)
        cos, sin = (jnp.cos(emb), jnp.sin(emb))
        q = q * cos + rotate_half(q) * sin
        k = k * cos + rotate_half(k) * sin
        att = jnp.einsum('bhtd,bhsd->bhts', q, k) * (1.0 / jnp.sqrt(jnp.array(D, x.dtype)))
        causal = jnp.tril(jnp.ones((T, T), bool))
        att = jnp.where(causal[None, None], att, jnp.array(-jnp.inf, att.dtype))
        att = jax.nn.softmax(att, axis=-1)
        y = jnp.einsum('bhts,bhsd->bhtd', att, v)
        y = y.transpose(0, 2, 1, 3).reshape(B, T, C)
        return y @ Wp.T + bp

    def _L0_ffn_ref(x, router_w, router_b, weights1, bias1, weights2, bias2):
        import jax, jax.numpy as jnp
        import numpy as np
        B, K, D = (128, 32, 256)
        E = 32
        H = int(D * 0.25)

        def _rsqrt_uniform(key, shape, d):
            bound = d ** (-0.5)
            return jax.random.uniform(key, shape, jnp.float32, -bound, bound)
        b, k, d = x.shape
        x_flat = x.reshape(-1, d)
        n = x_flat.shape[0]
        logits = x_flat @ router_w.T + router_b
        routed_idx = jnp.argmax(logits, axis=-1)

        def expert_mlp(w1, b1, w2, b2):
            h = jax.nn.relu(x_flat @ w1 + b1)
            return jax.nn.relu(h @ w2 + b2)
        y_all = jax.vmap(expert_mlp)(weights1, bias1, weights2, bias2)
        out_flat = y_all[routed_idx, jnp.arange(n)]
        return out_flat.reshape(b, k, d)

    def _L1_xattn_ref(Q, K, V, Wq, bq, Wk, bk, Wv, bv, Wo, bo):
        import jax, jax.numpy as jnp
        import numpy as np
        N, L, E, H, D = (4, 512, 256, 16, 64)
        n, lq, e = Q.shape
        lk = K.shape[1]
        q = (Q @ Wq.T + bq).reshape(n, lq, H, D)
        k = (K @ Wk.T + bk).reshape(n, lk, H, D)
        v = (V @ Wv.T + bv).reshape(n, lk, H, D)
        scores = jnp.einsum('nqhd,nkhd->nqkh', q, k) / jnp.sqrt(jnp.float32(D))
        attn = jax.nn.softmax(scores, axis=2)
        out = jnp.einsum('nqkh,nkhd->nqhd', attn, v)
        out = out.reshape(n, lq, H * D)
        return (out @ Wo.T + bo).reshape(n, lq, E)

    def _L1_attn_ref(x, Wq, bq, Wk, bk, Wv, bv, Wo, bo):
        import jax, jax.numpy as jnp
        import numpy as np
        N_HEADS = 16
        B, S, E = x.shape
        H = N_HEADS
        D = E // H
        q = (x @ Wq.T + bq).reshape(B, S, H, D)
        k = (x @ Wk.T + bk).reshape(B, S, H, D)
        v = (x @ Wv.T + bv).reshape(B, S, H, D)
        scores = jnp.einsum('bqnd,bknd->bnqk', q, k) / jnp.sqrt(jnp.float32(D))
        attn = jax.nn.softmax(scores, axis=1)
        out = jnp.einsum('bnqk,bknd->bnqd', attn, v)
        out = out.transpose(0, 2, 1, 3).reshape(B, S, E)
        return out @ Wo.T + bo

    def _L1_ffn_ref(hidden_states, gate_w, gate_up_w, down_w):
        import jax, jax.numpy as jnp
        import numpy as np
        H = 256
        F = 1024
        E = 8
        TOP_K = 2
        B, S = (1, 512)
        b, s, h = hidden_states.shape
        x = hidden_states.reshape(-1, h)
        router_logits = x @ gate_w.T
        probs = jax.nn.softmax(router_logits.astype(jnp.float32), axis=-1)
        topw, sel = jax.lax.top_k(probs, TOP_K)
        topw = topw / jnp.sum(topw, axis=-1, keepdims=True)
        topw = topw.astype(x.dtype)
        combine = jnp.sum(jax.nn.one_hot(sel, E, dtype=x.dtype) * topw[..., None], axis=1)
        gu = jnp.einsum('th,efh->etf', x, gate_up_w)
        gate, up = (gu[..., :F], gu[..., F:])
        hact = up * jax.nn.gelu(gate, approximate=False)
        expert_out = jnp.einsum('etf,ehf->eth', hact, down_w)
        out = jnp.einsum('eth,te->th', expert_out, combine)
        return out.reshape(b, s, h)
    x = x + _L0_xattn_ref(_layernorm(x, axis=-1), ctx_1024, ctx_1024, L0_xattn_Wq, L0_xattn_bq, L0_xattn_Wk, L0_xattn_bk, L0_xattn_Wv, L0_xattn_bv, L0_xattn_Wo, L0_xattn_bo)
    x = x + _L0_attn_ref(_layernorm(x, axis=-1), L0_attn_Wq, L0_attn_bq, L0_attn_Wk, L0_attn_bk, L0_attn_Wv, L0_attn_bv, L0_attn_Wp, L0_attn_bp)
    x = x + _L0_ffn_ref(_layernorm(x, axis=-1), L0_ffn_router_w, L0_ffn_router_b, L0_ffn_weights1, L0_ffn_bias1, L0_ffn_weights2, L0_ffn_bias2)
    x = x + _L1_xattn_ref(_layernorm(x, axis=-1), ctx_1024, ctx_1024, L1_xattn_Wq, L1_xattn_bq, L1_xattn_Wk, L1_xattn_bk, L1_xattn_Wv, L1_xattn_bv, L1_xattn_Wo, L1_xattn_bo)
    x = x + _L1_attn_ref(_layernorm(x, axis=-1), L1_attn_Wq, L1_attn_bq, L1_attn_Wk, L1_attn_bk, L1_attn_Wv, L1_attn_bv, L1_attn_Wo, L1_attn_bo)
    x = x + _L1_ffn_ref(_layernorm(x, axis=-1), L1_ffn_gate_w, L1_ffn_gate_up_w, L1_ffn_down_w)
    return x

_drawn_inputs = setup_inputs


def setup_inputs(seed=0):
    import zlib

    import numpy as np

    out = dict(_drawn_inputs(seed))
    spreads = {'L0_attn_bq': (0.0, 0.405),
     'L0_attn_bk': (0.0, 0.633),
     'L0_attn_bv': (0.0, 0.1),
     'L0_attn_bp': (0.0, 0.1),
     'L1_xattn_bq': (0.0, 0.1),
     'L1_xattn_bk': (0.0, 0.8),
     'L1_xattn_bv': (0.0, 0.1),
     'L1_xattn_bo': (0.0, 0.1)}
    factors = {'L0_xattn_bq': 2.962,
     'L0_xattn_bk': 8.0,
     'L0_ffn_bias1': 8.0,
     'L0_ffn_bias2': 4.077,
     'L1_attn_bq': 8.0,
     'L1_attn_bk': 8.0,
     'L1_attn_bv': 5.732,
     'L1_attn_bo': 8.0,
     'L1_ffn_gate_w': 6.859,
     'L1_ffn_gate_up_w': 5.921,
     'L1_ffn_down_w': 5.912}
    for name, (base, spread) in spreads.items():
        noise = np.random.default_rng([zlib.crc32(name.encode()), seed]).standard_normal(out[name].shape)
        drawn = base * np.exp(spread * noise) if base else spread * noise
        out[name] = jnp.asarray(drawn.astype(out[name].dtype))
    for name, factor in factors.items():
        out[name] = (out[name] * factor).astype(out[name].dtype)
    return out
```

```python
from contextlib import ExitStack

import numpy as np

import concourse.bass as bass
from concourse import mybir

F32 = mybir.dt.float32
U32 = mybir.dt.uint32
BF16 = mybir.dt.bfloat16
ACT = mybir.ActivationFunctionType
ALU = mybir.AluOpType
AX = mybir.AxisListType

P = 128
D = 256
KT = D // P
B, L = 64, 32
TOK = B * L
TILES = TOK // P
BPT = P // L
CH = 512
PASSES = TOK // CH
TPC = CH // P
NH = 16
HD = D // NH
QUADS = 4
NEG = -1.0e30
EPS = 1e-5


class Scope:

    def __init__(self, nc, ctx, tag):
        self.nc, self.ctx, self.tag, self.sems = nc, ctx, tag, []
        ctx.callback(self.free_semaphores)

    def sb(self, name, shape, dt=F32):
        return self.ctx.enter_context(self.nc.sbuf_tensor(f"{self.tag}_{name}", shape, dt))

    def ps(self, name, shape, dt=F32):
        return self.ctx.enter_context(self.nc.psum_tensor(f"{self.tag}_{name}", shape, dt))

    def sem(self, name):
        self.sems.append(self.nc.alloc_semaphore(name=f"{self.tag}_{name}"))
        return self.sems[-1]

    def free_semaphores(self):
        if self.sems:
            self.nc.clear_and_free_semaphores(self.sems)
            self.nc.all_engine_barrier()


class Carve:

    def __init__(self, region):
        self.region, self.at = region, 0

    def sb(self, name, shape, dt=F32):
        n = int(np.prod(shape[1:]))
        assert self.at + n <= self.region.shape[1], name
        v = self.region[0:shape[0], self.at:self.at + n]
        self.at += n
        if dt is not F32:
            v = v.bitcast(dt)
        if len(shape) == 2:
            return v
        names = "abcd"[:len(shape) - 1]
        return v.rearrange(f"p ({' '.join(names)}) -> p {' '.join(names)}",
                           **{k: size for k, size in zip(names, shape[1:])})


def wait(eng, sem, value):
    if not isinstance(value, int) or value > 0:
        eng.wait_ge(sem, value)


def take_wait(nc, g):
    nc.vector.memset(g["spare"][:, :], 0.0)


def take_wait_pe(nc, g, psum):
    nc.tensor.matmul(psum, g["ident"][:, :], g["ident"][:, 0:2], start=True, stop=True)


def pipelined(nc, eng, steps):
    steps(0, None)
    steps(1, 0)
    with eng.Fori(2, PASSES) as c:
        steps(c, c - 1)
    steps(None, PASSES - 1)


def first_then_loop(eng, n, body):
    body(0)
    with eng.Fori(1, n) as c:
        body(c)


def half(t, i, by):
    if isinstance(t, int):
        return (t // 2 + 1) * by
    return (t - i) * (by // 2) + by


def rope_tables():
    half = HD // 2
    inv = (1.0 / np.float32(10000.0) ** (np.arange(0, HD, 2, dtype=np.float32) / np.float32(HD))).astype(np.float32)
    freqs = np.arange(L, dtype=np.float32)[:, None] * inv[None, :]
    emb = np.concatenate((freqs, freqs), axis=-1)
    sign = np.where(np.arange(HD) < half, -1.0, 1.0).astype(np.float32)
    cos = np.cos(emb).astype(np.float32).T
    sin = (np.sin(emb).astype(np.float32) * sign[None, :]).T
    return np.tile(cos, (P // HD, 1)).copy(), np.tile(sin, (P // HD, 1)).copy()


def layer_norm_dve(nc, dve, X, c, s, buf, n=TPC):
    for t in range(n):
        nc.vector.bn_stats(buf["st"][:, t, :], X[:, bass.ds(c * n + t, 1), :]).then_inc(s["st"], 1)
    dve.wait_ge(s["st"], c * n + n)
    take_wait(nc, s["g"])
    for t in range(n):
        nc.vector.bn_aggr(buf["mv"][:, t, :], buf["st"][:, t, :]).then_inc(s["mv"], 1)
    dve.wait_ge(s["rs"], c + 1)
    nc.vector.scalar_tensor_tensor(out=buf["nb"][:, 0:n], in0=buf["mv"][:, 0:n, 0], scalar=-1.0,
                                   in1=buf["rs"][:, 0:n], op0=ALU.mult, op1=ALU.mult).then_inc(s["nb"], 1)


def layer_norm_pool(nc, pool, c, s, buf, n=TPC):
    pool.wait_ge(s["mv"], c * n + n)
    nc.gpsimd.tensor_tensor(buf["ve"][:, 0:n], buf["mv"][:, 0:n, 1], s["g"]["eps"][:, 0:n], ALU.add).then_inc(s["ve"], 1)
    pool.wait_ge(s["ve"], c + 1)
    nc.gpsimd.tensor_tensor(buf["rs"][:, 0:n], buf["ve"][:, 0:n], buf["mhalf"][:, 0:n], ALU.pow).then_inc(s["rs"], 1)


def layer_norm_act(nc, act, X, XN, c, s, buf, xn_free, n=TPC):
    act.wait_ge(s["nb"], c + 1)
    wait(act, xn_free, c)
    for t in range(n):
        nc.scalar.activation(XN[:, t, :], X[:, bass.ds(c * n + t, 1), :], ACT.Identity,
                             bias=buf["nb"][:, t:t + 1], scale=buf["rs"][:, t:t + 1]).then_inc(s["xn"], 1)


def layer_norm_buffers(a):
    return {"st": a.sb("ln_stats", [P, TPC, 6]), "mv": a.sb("ln_mean_var", [P, TPC, 2]),
            "ve": a.sb("ln_var_eps", [P, TPC]), "rs": a.sb("ln_rstd", [P, TPC]),
            "nb": a.sb("ln_shift", [P, TPC]), "mhalf": None}


def layer_norm_semaphores(a, g):
    return {"g": g, **{k: a.sem("ln_" + k) for k in ("st", "mv", "ve", "rs", "nb", "xn")}}


def small_attention(nc, tag, X, g, dram, causal, rope, over_heads, ctx_dram):
    NJ = 4
    with ExitStack() as ctx:
        a = Scope(nc, ctx, tag)
        sb, ps, sem = a.sb, a.ps, a.sem
        w, loads = {}, []
        for kind in ["q", "k", "v", "o"] + (["qr", "kr"] if rope else []):
            w[kind] = sb(f"w{kind}", [P, KT, D])
            loads.append((w[kind][:, :, :], dram[f"{tag}_{kind}T"].rearrange("(k p) n -> p k n", p=P)))
            if kind in ("v", "o"):
                w["b" + kind] = sb(f"b{kind}", [P, D])
                loads.append((w["b" + kind][:, :], dram[f"{tag}_b{kind}"].partition_broadcast(P)))
            else:
                w["b" + kind] = sb(f"b{kind}", [P, KT])
                loads.append((w["b" + kind][:, :], dram[f"{tag}_b{kind}"].rearrange("(k p) -> p k", p=P)))
        w["bkm"] = sb("bk_masked", [P, 2, KT])
        s_w, s_bkm = sem("weights_loaded"), sem("masked_bias")
        NLD = 16 * len(loads)
        XN = sb("xn", [P, TPC, D])
        XT = sb("xt", [P, KT, CH])
        CT = sb("ct", [P, KT, CH]) if ctx_dram is not None else None
        QT = sb("qt", [P, KT, CH])
        KTm = sb("ktm", [P, KT, 2, CH])
        KR = sb("kr", [P, KT, CH]) if rope else None
        RT = sb("rt", [P, 2, NJ, CH]) if rope else None
        V = sb("v", [P, TPC, D])
        S = sb("s", [P, TPC, NH, L])
        PT = sb("pt", [P, TPC, NH, L])
        NX = L if over_heads else NH
        MX = sb("mx", [P, TPC, NX])
        SM = sb("sm", [P, TPC, NX])
        RC = sb("rc", [P, TPC, NX])
        O1 = sb("o1", [P, BPT, TPC * KT, L])
        OT = sb("ot", [P, TPC, KT, P])
        ln = layer_norm_buffers(a)
        ln["mhalf"] = g["mhalf"]
        s = layer_norm_semaphores(a, g)
        s_ct = sem("ctx_loaded")
        s_xt, s_xte = sem("x_transposed"), sem("xt_ready")
        s_qp, s_qk = sem("qk_projected"), sem("qk_ready")
        s_r1, s_r2 = sem("rope_products"), sem("rope_summed")
        s_vp, s_v = sem("v_projected"), sem("v_ready")
        s_s, s_m, s_mx, s_sub = sem("scores"), sem("scores_out"), sem("row_max"), sem("shifted")
        s_e, s_sum, s_rc, s_p, s_pt = sem("exps"), sem("sums"), sem("recips"), sem("probs"), sem("probs_t")
        s_o, s_o1, s_ot = sem("pv"), sem("pv_odd"), sem("pv_ready")
        s_y, s_xb, s_x = sem("out_projected"), sem("bias_added"), sem("x_updated")
        pS = [ps(f"psS{j}", [P, 512]) for j in range(4)]
        pO = [ps(f"psO{j}", [P, 512]) for j in range(4)]

        def heads_view(t):
            return S[:, t, :, :].rearrange("p h s -> p s h") if over_heads else S[:, t, :, :]

        def along(T, t):
            v = T[:, t, :]
            return (v.unsqueeze(1) if over_heads else v.unsqueeze(2)).to_broadcast([P, NH, L])

        if rope:
            jobs = [("q", 0), ("qr", 0), ("q", 1), ("qr", 1), ("k", 0), ("kr", 0), ("k", 1), ("kr", 1)]
        else:
            jobs = [("q", 0), ("q", 1), ("k", 0), ("k", 1)]
        NJOB = len(jobs)
        bank = [2, 3, 0, 1, 2, 3, 0, 1]
        NQK = 4 if rope else 6
        FOLDS = BPT * KT

        with nc.Block() as block:
            @block.sync
            def _(sp):
                with nc.allow_non_contiguous_dma(reason="biases onto partitions"):
                    for dst, w_src in loads:
                        sp.dma_start(dst, w_src).then_inc(s_w, 16)
                if ctx_dram is not None:
                    src = ctx_dram.rearrange("(k p) t -> p k t", p=P)
                    sp.dma_start(CT[:, :, :], src[:, :, 0:CH]).then_inc(s_ct, 16)
                    with sp.Fori(1, PASSES) as c:
                        sp.wait_ge(s_vp, c * TPC)
                        sp.dma_start(CT[:, :, :], src[:, :, bass.ds(c * CH, CH)]).then_inc(s_ct, 16)

            @block.tensor
            def _(pe):
                def turn(c):
                    wait(pe, s_qk, c * NQK)
                    wait(pe, s_ot, (c - 1) * FOLDS)
                    if rope:
                        wait(pe, s_r1, c * NJOB)
                    for t in range(TPC):
                        pe.wait_ge(s["xn"], c * TPC + t + 1)
                        for k in range(KT):
                            mm = nc.tensor.transpose(pO[k][:, t * P:(t + 1) * P], XN[:, t, k * P:(k + 1) * P],
                                                     g["ident"][:, :])
                    mm.then_inc(s_xt, 1)

                def source(kind, k):
                    return CT[:, k, :] if kind[0] in "kv" and ctx_dram is not None else XT[:, k, :]

                def project_qk(c):
                    pe.wait_ge(s_xte, c * KT + KT)
                    for n, (kind, f) in enumerate(jobs):
                        if kind == "k" and f == 0 and ctx_dram is not None:
                            pe.wait_ge(s_ct, 16 * (c + 1))
                        if n >= 4:
                            pe.wait_ge(s_r1, c * NJOB + n - 3)
                        for k in range(KT):
                            mm = nc.tensor.matmul(pO[bank[n]][:, :], w[kind][:, k, f * P:(f + 1) * P],
                                                  source(kind, k), start=(k == 0), stop=(k == KT - 1))
                        mm.then_inc(s_qp, 1)

                def project_v(c):
                    wait(pe, s_m, c * QUADS)
                    if ctx_dram is not None:
                        pe.wait_ge(s_ct, 16 * (c + 1))
                    for t in range(TPC):
                        for k in range(KT):
                            mm = nc.tensor.matmul(pS[2 + t // 2][:, (t % 2) * D:(t % 2) * D + D],
                                                  source("v", k)[:, t * P:(t + 1) * P], w["v"][:, k, :],
                                                  start=(k == 0), stop=(k == KT - 1))
                        mm.then_inc(s_vp, 1)

                def scores(c):
                    pe.wait_ge(s_qk, c * NQK + NQK)
                    if rope:
                        pe.wait_ge(s_r2, c * 4 + 4)
                    pe.wait_ge(s_v, c * TPC + TPC)
                    wait(pe, s_x, c * TPC)
                    take_wait_pe(nc, g, pS[0][:, 0:2])
                    for t in range(TPC):
                        for hf in range(KT):
                            for b in range(BPT):
                                for j in range(QUADS):
                                    r = slice(32 * j, 32 * j + 32)
                                    tok = slice(t * P + b * L, t * P + b * L + L)
                                    col = (t * KT + hf) * 2 * L
                                    mm = nc.tensor.matmul(pS[j][b * L:(b + 1) * L, col:col + 2 * L],
                                                          QT[r, hf, tok], KTm[r, hf, :, tok],
                                                          start=True, stop=True)
                    mm.then_inc(s_s, 1)

                def weigh_values(b):
                    pe.wait_ge(s_v, b * TPC + TPC)
                    if rope:
                        pe.wait_ge(s_r1, (b + 1) * NJOB if isinstance(b, int) and b == PASSES - 1
                                   else (b + 2) * NJOB)
                    else:
                        pe.wait_ge(s_qk, (b + 1) * NQK if isinstance(b, int) and b == PASSES - 1
                                   else (b + 2) * NQK)
                    for t in range(TPC):
                        pe.wait_ge(s_pt, b * TPC + t + 1)
                        take_wait_pe(nc, g, pO[0][:, t * P:t * P + 2])
                        for hf in range(KT):
                            for j in range(QUADS):
                                for bb in range(BPT):
                                    r = slice(32 * bb, 32 * bb + 32)
                                    f = hf * P + 32 * j
                                    h = hf * 8 + 2 * j
                                    col = (t * KT + hf) * 2 * L
                                    mm = nc.tensor.matmul(pO[bb][32 * j:32 * j + 32, col:col + 2 * L],
                                                          V[r, t, f:f + 32], PT[r, t, h:h + 2, :],
                                                          start=True, stop=True)
                    mm.then_inc(s_o, 1)

                def project_out(b):
                    pe.wait_ge(s_ot, b * FOLDS + FOLDS)
                    pe.wait_ge(s_m, b * QUADS + QUADS)
                    for t in range(TPC):
                        for k in range(KT):
                            mm = nc.tensor.matmul(pS[t // 2][:, (t % 2) * D:(t % 2) * D + D], OT[:, t, k, :],
                                                  w["o"][:, k, :], start=(k == 0), stop=(k == KT - 1))
                        mm.then_inc(s_y, 1)

                def steps(c, b):
                    if c is not None:
                        turn(c)
                        project_qk(c)
                    if b is not None:
                        weigh_values(b)
                    if c is not None:
                        project_v(c)
                    if b is not None:
                        project_out(b)
                    if c is not None:
                        scores(c)

                pe.wait_ge(s_w, NLD)
                pipelined(nc, pe, steps)

            @block.vector
            def _(dve):
                def transposed(c):
                    dve.wait_ge(s_xt, c + 1)
                    wait(dve, s_vp, c * TPC)
                    for k in range(KT):
                        nc.vector.tensor_copy(XT[:, k, :], pO[k][:, :]).then_inc(s_xte, 1)

                def rope_products(c):
                    wait(dve, s_r2, c * 4)
                    for n, (kind, f) in enumerate(jobs):
                        dve.wait_ge(s_qp, c * NJOB + n + 1)
                        nc.vector.scalar_tensor_tensor(
                            out=RT[:, n % 2, n // 2, :].rearrange("p (b l) -> p b l", l=L),
                            in0=pO[bank[n]][:, :].rearrange("p (b l) -> p b l", l=L),
                            scalar=w["b" + kind][:, f:f + 1],
                            in1=g["sin" if n % 2 else "cos"][:, :].unsqueeze(1).to_broadcast([P, CH // L, L]),
                            op0=ALU.add, op1=ALU.mult).then_inc(s_r1, 1)

                def values(c):
                    wait(dve, s_o, c)
                    for t in range(TPC):
                        if t % 2 == 0:
                            dve.wait_ge(s_vp, c * TPC + t + 2)
                        nc.vector.tensor_tensor(V[:, t, :], pS[2 + t // 2][:, (t % 2) * D:(t % 2) * D + D],
                                                w["bv"][:, :], ALU.add).then_inc(s_v, 1)

                def scores_out(c):
                    dve.wait_ge(s_s, c + 1)
                    wait(dve, s_pt, c * TPC)
                    for j in range(QUADS):
                        i0 = pS[j][:, :].rearrange("p (x e) -> p x e", e=2 * L)
                        o = S[:, :, :, :].rearrange("p t (f j e) s -> p j (t f) (e s)", f=KT, j=QUADS)[:, j]
                        if causal:
                            i0 = i0.rearrange("p x (e s) -> p x e s", e=2)
                            o = o.rearrange("p x (e s) -> p x e s", e=2)
                            msk = g["causal"][:, :].unsqueeze(1).unsqueeze(1).to_broadcast([P, 8, 2, L])
                            nc.vector.tensor_tensor(o, i0, msk, ALU.add).then_inc(s_m, 1)
                        else:
                            nc.vector.tensor_copy(o, i0).then_inc(s_m, 1)
                    dve.wait_ge(s_m, c * QUADS + QUADS)
                    wait(dve, s_sub, c * TPC)
                    for t in range(TPC):
                        nc.vector.tensor_reduce(MX[:, t, :], heads_view(t), AX.X, ALU.max).then_inc(s_mx, 1)

                def softmax_sums(b):
                    wait(dve, s_p, b * TPC)
                    for t in range(TPC):
                        dve.wait_ge(s_e, b * TPC + t + 1)
                        nc.vector.tensor_reduce(SM[:, t, :], heads_view(t), AX.X, ALU.add).then_inc(s_sum, 1)
                        dve.wait_ge(s_sum, b * TPC + t + 1)
                        nc.vector.reciprocal(RC[:, t, :], SM[:, t, :]).then_inc(s_rc, 1)
                    wait(dve, s_o, b)
                    for t in range(TPC):
                        dve.wait_ge(s_p, b * TPC + t + 1)
                        nc.vector.transpose(PT[:, t, :, :], S[:, t, :, :]).then_inc(s_pt, 1)

                def fold_values(b):
                    wait(dve, s_y, b * TPC)
                    for bb in range(BPT):
                        dve.wait_ge(s_o1, b * BPT + bb + 1)
                        for hf in range(KT):
                            src = pO[bb][:, :].rearrange("p (t f e q) -> p f e t q", f=KT, e=2, q=L)[:, hf, 0]
                            odd = O1[:, bb, :, :].rearrange("p (t f) q -> p f t q", f=KT)[:, hf]
                            nc.vector.scalar_tensor_tensor(
                                out=OT[:, :, hf, bb * L:(bb + 1) * L], in0=src, scalar=g["halves"][:, 0:1],
                                in1=odd, op0=ALU.mult, op1=ALU.add).then_inc(s_ot, 1)

                def update(b):
                    for t in range(TPC):
                        dve.wait_ge(s_y, b * TPC + (t // 2) * 2 + 2)
                        dve.wait_ge(s_xb, b * TPC + t + 1)
                        xt = X[:, bass.ds(b * TPC + t, 1), :].rearrange("p a d -> p (a d)")
                        nc.vector.tensor_tensor(xt, pS[t // 2][:, (t % 2) * D:(t % 2) * D + D], xt,
                                                ALU.add).then_inc(s_x, 1)

                def steps(c, b):
                    if c is not None:
                        layer_norm_dve(nc, dve, X, c, s, ln)
                        transposed(c)
                        if rope:
                            rope_products(c)
                    if b is not None:
                        softmax_sums(b)
                        fold_values(b)
                    if c is not None:
                        values(c)
                    if b is not None:
                        update(b)
                    if c is not None:
                        scores_out(c)

                dve.wait_ge(s_w, NLD)
                for e in range(2):
                    nc.vector.tensor_scalar(w["bkm"][:, e, :], w["bk"][:, :], g["halves"][:, e:e + 1], None,
                                            ALU.mult).then_inc(s_bkm, 1)
                pipelined(nc, dve, steps)

            @block.scalar
            def _(act):
                def queries_keys(c):
                    wait(act, s_s, c)
                    if rope:
                        for f in range(KT):
                            act.wait_ge(s_r2, c * 4 + f + 3)
                            for e in range(2):
                                nc.scalar.activation(KTm[:, f, e, :], KR[:, f, :], ACT.Copy,
                                                     scale=g["halves"][:, e:e + 1]).then_inc(s_qk, 1)
                        return
                    for n, (kind, f) in enumerate(jobs):
                        act.wait_ge(s_qp, c * NJOB + n + 1)
                        src = pO[bank[n]][:, :]
                        if kind == "q":
                            nc.scalar.activation(QT[:, f, :], src, ACT.Identity,
                                                 bias=w["bq"][:, f:f + 1]).then_inc(s_qk, 1)
                        else:
                            for e in range(2):
                                nc.scalar.activation(KTm[:, f, e, :], src, ACT.Identity,
                                                     bias=w["bkm"][:, e, f:f + 1],
                                                     scale=g["halves"][:, e:e + 1]).then_inc(s_qk, 1)

                def exps(b):
                    for t in range(TPC):
                        act.wait_ge(s_sub, b * TPC + t + 1)
                        nc.scalar.activation(S[:, t, :, :], S[:, t, :, :], ACT.Exp,
                                             scale=HD ** -0.5).then_inc(s_e, 1)

                def odd_heads(b):
                    act.wait_ge(s_o, b + 1)
                    wait(act, s_ot, b * FOLDS)
                    for bb in range(BPT):
                        src = pO[bb][:, :].rearrange("p (x e q) -> p e x q", e=2, q=L)[:, 1]
                        nc.scalar.activation(O1[:, bb, :, :], src, ACT.Copy,
                                             scale=g["halves"][:, 1:2]).then_inc(s_o1, 1)

                def steps(c, b):
                    if c is not None:
                        layer_norm_act(nc, act, X, XN, c, s, ln, s_xt)
                    if b is not None:
                        exps(b)
                    if c is not None:
                        queries_keys(c)
                    if b is not None:
                        odd_heads(b)

                act.wait_ge(s_w, NLD)
                act.wait_ge(s_bkm, 2)
                pipelined(nc, act, steps)

            @block.gpsimd
            def _(pool):
                def shift(b):
                    for t in range(TPC):
                        pool.wait_ge(s_mx, b * TPC + t + 1)
                        nc.gpsimd.tensor_tensor(S[:, t, :, :], S[:, t, :, :], along(MX, t),
                                                ALU.subtract).then_inc(s_sub, 1)

                def add_bias(c):
                    for t in range(TPC):
                        pool.wait_ge(s["xn"], c * TPC + t + 1)
                        xt = X[:, bass.ds(c * TPC + t, 1), :].rearrange("p a d -> p (a d)")
                        nc.gpsimd.tensor_tensor(xt, xt, w["bo"][:, :], ALU.add).then_inc(s_xb, 1)

                def rope_sums(c):
                    wait(pool, s_s, c)
                    wait(pool, s_qk, c * NQK)
                    for i in range(4):
                        pool.wait_ge(s_r1, c * NJOB + 2 * i + 2)
                        dst = QT[:, i, :] if i < 2 else KR[:, i - 2, :]
                        nc.gpsimd.tensor_tensor(dst, RT[:, 0, i, :], RT[:, 1, i, :], ALU.add).then_inc(s_r2, 1)

                def normalise(b):
                    for t in range(TPC):
                        pool.wait_ge(s_rc, b * TPC + t + 1)
                        nc.gpsimd.tensor_tensor(S[:, t, :, :], S[:, t, :, :], along(RC, t),
                                                ALU.mult).then_inc(s_p, 1)

                def steps(c, b):
                    if c is not None:
                        layer_norm_pool(nc, pool, c, s, ln)
                    if b is not None:
                        shift(b)
                    if c is not None and rope:
                        rope_sums(c)
                    if b is not None:
                        normalise(b)
                    if c is not None:
                        add_bias(c)

                pool.wait_ge(s_w, NLD)
                pipelined(nc, pool, steps)


NE0 = 32
H0 = D // 4
PAIRS = NE0 // 2


def routed_ffn0(nc, tag, X, g, dram):
    with ExitStack() as ctx:
        a = Scope(nc, ctx, tag)
        sb, ps, sem = a.sb, a.ps, a.sem
        W1 = sb("w1", [P, KT, NE0 * H0])
        W2 = sb("w2", [P, PAIRS, D])
        RW = sb("router_w", [P, KT, NE0])
        RB = sb("router_b", [P, NE0])
        B1 = sb("b1", [P, PAIRS])
        B2 = sb("b2", [NE0, D])
        SEL = sb("pair_select", [NE0, PAIRS * P])
        SELh = sb("pair_select_bf", [NE0, PAIRS * P], BF16)
        IOTA = sb("iota", [P, NE0])
        XTall = sb("xt_all", [P, KT, TOK])
        OHall = sb("onehot_t", [NE0, TOK], BF16)
        B2S = sb("b2_selected", [P, TILES, D])
        s_w, s_wb = sem("weights_loaded"), sem("select_ready")
        loads = [(RW[:, :, :], dram["ffn0_rT"].rearrange("(k p) n -> p k n", p=P)),
                 (RB[:, :], dram["ffn0_rb"].partition_broadcast(P)),
                 (IOTA[:, :], dram["iota32"]), (SEL[:, :], dram["pair_select"]), (B2[:, :], dram["ffn0_b2"]),
                 (B1[:, :], dram["ffn0_b1"].rearrange("(j p) -> p j", p=P)),
                 (W1[:, :, :], dram["ffn0_w1"].rearrange("(k p) n -> p k n", p=P)),
                 (W2[:, :, :], dram["ffn0_w2"].rearrange("(j p) n -> p j n", p=P))]
        NLD = 16 * len(loads)

        with ExitStack() as ctx2:
            a2 = Scope(nc, ctx2, tag + "r")
            XN = a2.sb("xn", [P, TPC, D])
            XT = a2.sb("xt", [P, KT, CH])
            LG = a2.sb("logits", [P, TPC, NE0])
            M8 = a2.sb("max8", [P, TPC, 8])
            I8 = a2.sb("idx8", [P, TPC, 8], U32)
            IF = a2.sb("idx", [P, TPC])
            OH = a2.sb("onehot", [P, TPC, NE0])
            OHT = a2.sb("onehot_t", [NE0, CH])
            ln = layer_norm_buffers(a2)
            ln["mhalf"] = g["mhalf"]
            s = layer_norm_semaphores(a2, g)
            s_xt, s_xte, s_xc = a2.sem("x_transposed"), a2.sem("xt_ready"), a2.sem("xt_kept")
            s_lg, s_l, s_m8, s_i8 = a2.sem("logits"), a2.sem("logits_out"), a2.sem("max8"), a2.sem("idx8")
            s_if, s_oh, s_oht, s_ohe = a2.sem("idx"), a2.sem("onehot"), a2.sem("onehot_t"), a2.sem("onehot_out")
            s_ohk = a2.sem("onehot_kept")
            s_b2, s_b2e = a2.sem("b2"), a2.sem("b2_out")
            pT = [a2.ps(f"pT{j}", [P, 512]) for j in range(KT)]
            pL = a2.ps("pL", [P, TPC, NE0])
            pH = a2.ps("pH", [NE0, 512])
            pB = [a2.ps(f"pB{j}", [P, 512]) for j in range(2)]
            with nc.Block() as block:
                @block.sync
                def _(sp):
                    with nc.allow_non_contiguous_dma(reason="biases onto partitions"):
                        for dst, src in loads:
                            sp.dma_start(dst, src).then_inc(s_w, 16)

                @block.tensor
                def _(pe):
                    def select_biases(b):
                        pe.wait_ge(s_oh, b * TPC + TPC)
                        wait(pe, s_ohe, b)
                        wait(pe, s_ohk, b)
                        for t in range(TPC):
                            mm = nc.tensor.transpose(pH[:, t * P:(t + 1) * P], OH[:, t, :], g["ident"][:, :])
                        mm.then_inc(s_oht, 1)
                        pe.wait_ge(s_ohe, b + 1)
                        wait(pe, s_b2e, b * TPC)
                        for t in range(TPC):
                            nc.tensor.matmul(pB[t // 2][:, (t % 2) * D:(t % 2) * D + D], OHT[:, t * P:(t + 1) * P],
                                             B2[:, :], start=True, stop=True).then_inc(s_b2, 1)

                    def logits(c):
                        wait(pe, s_xte, c * KT)
                        wait(pe, s_xc, c * KT)
                        for t in range(TPC):
                            pe.wait_ge(s["xn"], c * TPC + t + 1)
                            for k in range(KT):
                                mm = nc.tensor.transpose(pT[k][:, t * P:(t + 1) * P], XN[:, t, k * P:(k + 1) * P],
                                                         g["ident"][:, :])
                        mm.then_inc(s_xt, 1)
                        pe.wait_ge(s_xte, c * KT + KT)
                        wait(pe, s_l, c)
                        for t in range(TPC):
                            for k in range(KT):
                                mm = nc.tensor.matmul(pL[:, t, :], XT[:, k, t * P:(t + 1) * P], RW[:, k, :],
                                                      start=(k == 0), stop=(k == KT - 1))
                        mm.then_inc(s_lg, 1)

                    def steps(c, b):
                        if b is not None:
                            select_biases(b)
                        if c is not None:
                            logits(c)

                    pe.wait_ge(s_w, NLD)
                    pipelined(nc, pe, steps)

                @block.vector
                def _(dve):
                    def route(b):
                        dve.wait_ge(s_lg, b + 1)
                        nc.vector.tensor_tensor(LG[:, :, :], pL[:, :, :],
                                                RB[:, :].unsqueeze(1).to_broadcast([P, TPC, NE0]),
                                                ALU.add).then_inc(s_l, 1)
                        dve.wait_ge(s_l, b + 1)
                        take_wait(nc, g)
                        for t in range(TPC):
                            nc.vector.max(M8[:, t, :], LG[:, t, :]).then_inc(s_m8, 1)
                        dve.wait_ge(s_m8, b * TPC + TPC)
                        take_wait(nc, g)
                        for t in range(TPC):
                            nc.vector.max_index(I8[:, t, :], M8[:, t, :], LG[:, t, :]).then_inc(s_i8, 1)
                        dve.wait_ge(s_i8, b * TPC + TPC)
                        nc.vector.tensor_copy(IF[:, :], I8[:, :, 0]).then_inc(s_if, 1)
                        wait(dve, s_oht, b)
                        dve.wait_ge(s_if, b + 1)
                        for t in range(TPC):
                            nc.vector.tensor_scalar(OH[:, t, :], IOTA[:, :], IF[:, t:t + 1], None,
                                                    ALU.is_equal).then_inc(s_oh, 1)
                        dve.wait_ge(s_oht, b + 1)
                        wait(dve, s_b2, b * TPC)
                        nc.vector.tensor_copy(OHT[:, :], pH[:, :]).then_inc(s_ohe, 1)
                        for t in range(TPC):
                            if t % 2 == 0:
                                dve.wait_ge(s_b2, b * TPC + t + 2)
                            dst = B2S[:, bass.ds(b * TPC + t, 1), :].rearrange("p a d -> p (a d)")
                            nc.vector.tensor_copy(dst, pB[t // 2][:, (t % 2) * D:(t % 2) * D + D]).then_inc(s_b2e, 1)

                    def transposed(c):
                        dve.wait_ge(s_xt, c + 1)
                        wait(dve, s_lg, c)
                        for k in range(KT):
                            nc.vector.tensor_copy(XT[:, k, :], pT[k][:, :]).then_inc(s_xte, 1)

                    def steps(c, b):
                        if c is not None:
                            layer_norm_dve(nc, dve, X, c, s, ln)
                        if b is not None:
                            route(b)
                        if c is not None:
                            transposed(c)

                    dve.wait_ge(s_w, NLD)
                    nc.vector.tensor_copy(SELh[:, :], SEL[:, :]).then_inc(s_wb, 1)
                    pipelined(nc, dve, steps)

                @block.scalar
                def _(act):
                    def steps(c, b):
                        if b is not None:
                            act.wait_ge(s_ohe, b + 1)
                            nc.scalar.copy(OHall[:, bass.ds(b * CH, CH)], OHT[:, :]).then_inc(s_ohk, 1)
                        if c is not None:
                            layer_norm_act(nc, act, X, XN, c, s, ln, s_xt)
                            act.wait_ge(s_xte, c * KT + KT)
                            for k in range(KT):
                                nc.scalar.copy(XTall[:, k, bass.ds(c * CH, CH)], pT[k][:, :]).then_inc(s_xc, 1)

                    pipelined(nc, act, steps)

                @block.gpsimd
                def _(pool):
                    layer_norm_pool(nc, pool, 0, s, ln)
                    with pool.Fori(1, PASSES) as c:
                        layer_norm_pool(nc, pool, c, s, ln)

        with ExitStack() as ctx3:
            a3 = Scope(nc, ctx3, tag + "e")
            HR = a3.sb("hidden", [P, 2, CH])
            HM = a3.sb("hidden_masked", [P, 2, CH])
            Y = a3.sb("y", [P, TPC, D])
            s_h, s_hr, s_mk, s_hm = a3.sem("hidden"), a3.sem("hidden_out"), a3.sem("mask"), a3.sem("masked")
            s_y2, s_yp, s_y, s_x = a3.sem("pair_summed"), a3.sem("y"), a3.sem("y_out"), a3.sem("x_updated")
            pH = [a3.ps(f"pH{j}", [P, 512]) for j in range(3)]
            pM = [a3.ps(f"pM{j}", [P, 512]) for j in range(3)]
            pY = [a3.ps(f"pY{j}", [P, 512]) for j in range(2)]
            PP = PAIRS

            def passes(eng, body):
                body(0)
                with eng.Fori(1, PASSES) as c:
                    body(c)

            with nc.Block() as block:
                @block.tensor
                def _(pe):
                    def hidden(c, p):
                        wait(pe, s_hr, c * PP + p - 2)
                        wait(pe, s_hm, c * PP + p - 2)
                        for k in range(KT):
                            mm = nc.tensor.matmul(pH[p % 3][:, :], W1[:, k, p * P:(p + 1) * P],
                                                  XTall[:, k, bass.ds(c * CH, CH)],
                                                  start=(k == 0), stop=(k == KT - 1))
                        mm.then_inc(s_h, 1)
                        nc.tensor.matmul(pM[p % 3][:, :], SELh[:, p * P:(p + 1) * P], OHall[:, bass.ds(c * CH, CH)],
                                         start=True, stop=True).then_inc(s_mk, 1)

                    def out(c, p):
                        pe.wait_ge(s_hm, c * PP + p + 1)
                        if p == 0:
                            wait(pe, s_y, c * TPC)
                        for t in range(TPC):
                            mm = nc.tensor.matmul(pY[t // 2][:, (t % 2) * D:(t % 2) * D + D],
                                                  HM[:, p % 2, t * P:(t + 1) * P], W2[:, p, :],
                                                  start=(p == 0 and t % 2 == 0), stop=(p == PP - 1),
                                                  skip_group_check=True)
                        mm.then_inc(s_y2, 1)

                    def body(c):
                        for p in range(PP):
                            hidden(c, p)
                            if p > 0:
                                out(c, p - 1)
                        out(c, PP - 1)

                    passes(pe, body)

                @block.scalar
                def _(act):
                    def body(c):
                        for p in range(PP):
                            act.wait_ge(s_h, c * PP + p + 1)
                            wait(act, s_hm, c * PP + p - 1)
                            nc.scalar.activation(HR[:, p % 2, :], pH[p % 3][:, :], ACT.Relu,
                                                 bias=B1[:, p:p + 1]).then_inc(s_hr, 1)

                    passes(act, body)

                @block.vector
                def _(dve):
                    def body(c):
                        for p in range(PP):
                            dve.wait_ge(s_hr, c * PP + p + 1)
                            dve.wait_ge(s_mk, c * PP + p + 1)
                            wait(dve, s_y2, c * PP + p - 1)
                            nc.vector.tensor_tensor(HM[:, p % 2, :], pM[p % 3][:, :], HR[:, p % 2, :],
                                                    ALU.mult).then_inc(s_hm, 1)
                        dve.wait_ge(s_y2, c * PP + PP)
                        wait(dve, s_x, c * TPC)
                        for t in range(TPC):
                            bs = B2S[:, bass.ds(c * TPC + t, 1), :].rearrange("p a d -> p (a d)")
                            nc.vector.tensor_tensor(Y[:, t, :], pY[t // 2][:, (t % 2) * D:(t % 2) * D + D], bs,
                                                    ALU.add).then_inc(s_y, 1)
                        for t in range(TPC):
                            dve.wait_ge(s_y, c * TPC + t + 1)
                            xt = X[:, bass.ds(c * TPC + t, 1), :].rearrange("p a d -> p (a d)")
                            nc.vector.scalar_tensor_tensor(out=xt, in0=Y[:, t, :], scalar=0.0, in1=xt,
                                                           op0=ALU.max, op1=ALU.add).then_inc(s_x, 1)

                    passes(dve, body)


XW = 1024
XD = XW // NH
SK = 257
XCH = 256
XTP = XCH // P
XPASSES = TOK // XCH
XB = XCH // L
ROWS = NH * L
RT4 = ROWS // P


def cross_attention(nc, tag, X, g, dram):
    with ExitStack() as ctx:
        a = Scope(nc, ctx, tag)
        sb, ps, sem = a.sb, a.ps, a.sem
        WQ = sb("wq", [P, KT, XW])
        WK = sb("wk", [P, XW // P, D])
        WV = sb("wv", [P, KT, XW])
        WO = sb("wo", [P, XW // P, D])
        BQ = sb("bq", [P, XW // P])
        BV = sb("bv", [P, XW // P])
        BO = sb("bo", [P, D])
        XN = sb("xn", [P, XTP, D])
        XT = sb("xt", [P, KT, XCH])
        QT = sb("qt", [P, XW // P, XCH])
        G = sb("queries_to_context", [P, KT, XB, ROWS])
        CT = sb("ctx_t", [P, 2, KT, SK])
        CX = sb("ctx", [P, 2, KT, D])
        CL = sb("ctx_last", [1, 2, D])
        PR = sb("probs", [P, 2, RT4, SK])
        NM = sb("neg_max", [P, 2, RT4])
        NB = sb("exp_bias", [P, 2, RT4])
        SM = sb("sums", [P, 2, RT4])
        RC = sb("recips", [P, 2, RT4])
        PT = sb("probs_t", [P, 2, KT, ROWS])
        PL = sb("probs_last", [1, 2, ROWS])
        MX = sb("mixed_context", [P, KT, NH, XCH])
        OT = sb("heads_out", [P, XW // P, XCH])
        ln = layer_norm_buffers(a)
        ln["mhalf"] = g["mhalf"]
        s = layer_norm_semaphores(a, g)
        s_w = sem("weights_loaded")
        s_ct, s_cx = [sem(f"ctx_t_loaded{i}") for i in range(2)], [sem(f"ctx_loaded{i}") for i in range(2)]
        s_xt, s_xte = sem("x_transposed"), sem("xt_ready")
        s_qp, s_q = sem("q_projected"), sem("q_ready")
        s_gp, s_ga, s_gd = sem("g_projected"), sem("g_even_ready"), sem("g_odd_ready")
        s_s, s_nm, s_nb, s_e = sem("scores"), sem("row_max"), sem("exp_bias"), sem("exps")
        s_rc, s_p, s_t = sem("recips"), sem("probs"), sem("probs_transposed")
        s_tl, s_pa, s_pd, s_pl = sem("last_transposed"), sem("pt0_ready"), sem("pt1_ready"), sem("pt_last_ready")
        s_m, s_ma, s_md = sem("mixed"), sem("mix0_ready"), sem("mix1_ready")
        s_o, s_oe = sem("heads_projected"), sem("heads_ready")
        s_y, s_xb, s_x = sem("out_projected"), sem("bias_added"), sem("x_updated")
        pS = [ps(f"pS{j}", [P, 512]) for j in range(RT4)]
        pA = [ps(f"pA{j}", [P, 512]) for j in range(2)]
        pM = [ps(f"pM{j}", [P, 512]) for j in range(2)]
        FT = XW // P
        loads = [(WQ[:, :, :], dram["L1x_qT"].rearrange("(k p) n -> p k n", p=P)),
                 (BQ[:, :], dram["L1x_bq"].rearrange("(k p) -> p k", p=P)),
                 (WK[:, :, :], dram["L1x_k"].rearrange("(k p) n -> p k n", p=P)),
                 (WV[:, :, :], dram["L1x_vT"].rearrange("(k p) n -> p k n", p=P)),
                 (WO[:, :, :], dram["L1x_oT"].rearrange("(k p) n -> p k n", p=P)),
                 (BV[:, :], dram["L1x_bv"].rearrange("(k p) -> p k", p=P)),
                 (BO[:, :], dram["L1x_bo"].partition_broadcast(P))]
        NLD = 16 * len(loads)

        def passes(eng, body):
            body(0)
            with eng.Fori(1, XPASSES) as c:
                body(c)

        with nc.Block() as block:
            @block.sync
            def _(sp):
                def body(c):
                    for b in range(XB):
                        gb, i = c * XB + b, b % 2
                        wait(sp, s_s, gb - 1)
                        sp.dma_start(CT[:, i, :, :], dram["ctxT"].rearrange("b (k p) s -> b p k s", p=P)
                                     [bass.ds(gb, 1)].rearrange("a p k s -> p (a k) s")).then_inc(s_ct[i], 16)
                        wait(sp, s_m, gb - 1)
                        rows = dram["ctx"][bass.ds(gb, 1)]
                        sp.dma_start(CX[:, i, :, :], rows[:, 0:KT * P, :].rearrange("a (k p) d -> p (a k) d", p=P)
                                     ).then_inc(s_cx[i], 16)
                        sp.dma_start(CL[:, i, :], rows[:, KT * P, :]).then_inc(s_cx[i], 16)

                with nc.allow_non_contiguous_dma(reason="biases onto partitions"):
                    for dst, src in loads:
                        sp.dma_start(dst, src).then_inc(s_w, 16)
                passes(sp, body)

            @block.tensor
            def _(pe):
                def queries(c):
                    wait(pe, s_pa, c * XB)
                    wait(pe, s_pd, c * XB)
                    wait(pe, s_oe, c * FT)
                    for t in range(XTP):
                        pe.wait_ge(s["xn"], c * XTP + t + 1)
                        for k in range(KT):
                            mm = nc.tensor.transpose(pA[k][:, t * P:(t + 1) * P], XN[:, t, k * P:(k + 1) * P],
                                                     g["ident"][:, :])
                    mm.then_inc(s_xt, 1)
                    pe.wait_ge(s_xte, c * KT + KT)
                    for f in range(FT):
                        if f >= 2:
                            pe.wait_ge(s_q, c * FT + f - 1)
                        for k in range(KT):
                            mm = nc.tensor.matmul(pA[f % 2][:, 0:XCH], WQ[:, k, f * P:(f + 1) * P], XT[:, k, :],
                                                  start=(k == 0), stop=(k == KT - 1))
                        mm.then_inc(s_qp, 1)
                    for h in range(NH):
                        r = slice(64 * (h % 2), 64 * (h % 2) + 64)
                        if h < 2:
                            pe.wait_ge(s_q, c * FT + FT)
                        else:
                            done = s_ga if h % 2 == 0 else s_gd
                            pe.wait_ge(done, c * (NH // 2) + h // 2)
                        for m in range(KT):
                            mm = nc.tensor.matmul(pA[h % 2][:, m * XCH:(m + 1) * XCH],
                                                  WK[r, h // 2, m * P:(m + 1) * P], QT[r, h // 2, :],
                                                  start=True, stop=True)
                        mm.then_inc(s_gp, 1)

                def scores(c, b):
                    gb = c * XB + b
                    pe.wait_ge(s_ct[b % 2], (c * (XB // 2) + b // 2 + 1) * 16)
                    if b == 0:
                        pe.wait_ge(s_ga, (c + 1) * (NH // 2))
                        pe.wait_ge(s_gd, (c + 1) * (NH // 2))
                    for t in range(RT4):
                        wait(pe, s_e, (gb - 1) * RT4 + t + 1)
                        if t == RT4 - 1:
                            wait(pe, s_pl, gb)
                        for k in range(KT):
                            mm = nc.tensor.matmul(pS[t][:, 0:SK], G[:, k, b, t * P:(t + 1) * P], CT[:, b % 2, k, :],
                                                  start=(k == 0), stop=(k == KT - 1))
                    mm.then_inc(s_s, 1)

                def turn(c, b):
                    gb, i = c * XB + b, b % 2
                    pe.wait_ge(s_p, gb * RT4 + RT4)
                    wait(pe, s_pa, gb)
                    wait(pe, s_pd, gb)
                    for t in range(RT4):
                        mm = nc.tensor.transpose(pS[RT4 - 1][0:1, t * P:(t + 1) * P], PR[:, i, t, KT * P:SK],
                                                 g["ident"][:, :])
                    mm.then_inc(s_tl, 1)
                    for k in range(KT):
                        for t in range(RT4):
                            mm = nc.tensor.transpose(pA[k][:, t * P:(t + 1) * P], PR[:, i, t, k * P:(k + 1) * P],
                                                     g["ident"][:, :])
                        mm.then_inc(s_t, 1)

                def mix(c, b):
                    gb, i = c * XB + b, b % 2
                    pe.wait_ge(s_cx[i], (c * (XB // 2) + b // 2 + 1) * 32)
                    pe.wait_ge(s_pa, gb + 1)
                    pe.wait_ge(s_pd, gb + 1)
                    pe.wait_ge(s_pl, gb + 1)
                    wait(pe, s_ma, gb)
                    wait(pe, s_md, gb)
                    if b == 0:
                        wait(pe, s_x, c * XTP)
                    for m in range(KT):
                        for k in range(KT):
                            nc.tensor.matmul(pM[m][:, :], CX[:, i, k, m * P:(m + 1) * P], PT[:, i, k, :],
                                             start=(k == 0), stop=False)
                        mm = nc.tensor.matmul(pM[m][:, :], CL[0:1, i, m * P:(m + 1) * P], PL[0:1, i, :],
                                              start=False, stop=True)
                    mm.then_inc(s_m, 1)

                def outputs(c):
                    pe.wait_ge(s_ma, (c + 1) * XB)
                    pe.wait_ge(s_md, (c + 1) * XB)
                    for f in range(FT):
                        if f >= 2:
                            pe.wait_ge(s_oe, c * FT + f - 1)
                        for e in range(2):
                            h = 2 * f + e
                            for k in range(KT):
                                mm = nc.tensor.matmul(pA[f % 2][64 * e:64 * e + 64, 0:XCH],
                                                      WV[:, k, h * XD:(h + 1) * XD], MX[:, k, h, :],
                                                      start=(k == 0), stop=(k == KT - 1))
                        mm.then_inc(s_o, 1)
                    pe.wait_ge(s_oe, c * FT + FT)
                    for t in range(XTP):
                        for f in range(FT):
                            mm = nc.tensor.matmul(pM[t][:, 0:D], OT[:, f, t * P:(t + 1) * P], WO[:, f, :],
                                                  start=(f == 0), stop=(f == FT - 1))
                        mm.then_inc(s_y, 1)

                def body(c):
                    queries(c)
                    scores(c, 0)
                    for b in range(XB):
                        turn(c, b)
                        if b + 1 < XB:
                            scores(c, b + 1)
                        mix(c, b)
                    outputs(c)

                pe.wait_ge(s_w, NLD)
                passes(pe, body)

            @block.vector
            def _(dve):
                def body(c):
                    layer_norm_dve(nc, dve, X, c, s, ln, XTP)
                    dve.wait_ge(s_xt, c + 1)
                    wait(dve, s_qp, c * FT)
                    for k in range(KT):
                        nc.vector.tensor_copy(XT[:, k, :], pA[k][:, 0:XCH]).then_inc(s_xte, 1)
                    for h in range(1, NH, 2):
                        dve.wait_ge(s_gp, c * NH + h + 1)
                        if h == 1:
                            wait(dve, s_s, c * XB)
                        o = G[:, :, :, h * L:(h + 1) * L]
                        nc.vector.tensor_copy(o, pA[1][:, :].rearrange("p (m b q) -> p m b q", m=KT, q=L)
                                              ).then_inc(s_gd, 1)
                    row_maxima(c, 0)
                    for b in range(XB):
                        probabilities(c, b)
                        if b + 1 < XB:
                            row_maxima(c, b + 1)
                        gb = c * XB + b
                        dve.wait_ge(s_m, gb + 1)
                        if b == 0:
                            wait(dve, s_o, c * FT)
                        nc.vector.tensor_copy(MX[:, 1, :, b * L:(b + 1) * L],
                                              pM[1][:, :].rearrange("p (h q) -> p h q", q=L)).then_inc(s_md, 1)
                    for t in range(XTP):
                        dve.wait_ge(s_y, c * XTP + t + 1)
                        dve.wait_ge(s_xb, c * XTP + t + 1)
                        xt = X[:, bass.ds(c * XTP + t, 1), :].rearrange("p a d -> p (a d)")
                        nc.vector.tensor_tensor(xt, pM[t][:, 0:D], xt, ALU.add).then_inc(s_x, 1)

                def row_maxima(c, b):
                    gb, i = c * XB + b, b % 2
                    dve.wait_ge(s_s, gb + 1)
                    for t in range(RT4):
                        nc.vector.tensor_reduce(NM[:, i, t:t + 1], pS[t][:, 0:SK], AX.X, ALU.max,
                                                negate=True).then_inc(s_nm, 1)
                    dve.wait_ge(s_nm, gb * RT4 + RT4)
                    nc.vector.tensor_scalar(NB[:, i, :], NM[:, i, :], XD ** -0.5, None,
                                            ALU.mult).then_inc(s_nb, 1)

                def probabilities(c, b):
                    gb, i = c * XB + b, b % 2
                    dve.wait_ge(s_e, gb * RT4 + RT4)
                    nc.vector.reciprocal(RC[:, i, :], SM[:, i, :]).then_inc(s_rc, 1)
                    dve.wait_ge(s_rc, gb + 1)
                    for t in range(RT4):
                        nc.vector.tensor_scalar(PR[:, i, t, :], PR[:, i, t, :], RC[:, i, t:t + 1], None,
                                                ALU.mult).then_inc(s_p, 1)
                    dve.wait_ge(s_tl, gb + 1)
                    wait(dve, s_m, gb - 1)
                    nc.vector.tensor_copy(PL[0:1, i, :], pS[RT4 - 1][0:1, :]).then_inc(s_pl, 1)
                    dve.wait_ge(s_t, gb * KT + KT)
                    nc.vector.tensor_copy(PT[:, i, 1, :], pA[1][:, :]).then_inc(s_pd, 1)

                passes(dve, body)

            @block.scalar
            def _(act):
                def body(c):
                    layer_norm_act(nc, act, X, XN, c, s, ln, s_xt, XTP)
                    if isinstance(c, int):
                        act.wait_ge(s_w, NLD)
                    for f in range(FT):
                        act.wait_ge(s_qp, c * FT + f + 1)
                        wait(act, s_gp, c * NH)
                        nc.scalar.activation(QT[:, f, :], pA[f % 2][:, 0:XCH], ACT.Identity,
                                             bias=BQ[:, f:f + 1]).then_inc(s_q, 1)
                    for h in range(0, NH, 2):
                        act.wait_ge(s_gp, c * NH + h + 1)
                        if h == 0:
                            wait(act, s_s, c * XB)
                        nc.scalar.copy(G[:, :, :, h * L:(h + 1) * L],
                                       pA[0][:, :].rearrange("p (m b q) -> p m b q", m=KT, q=L)).then_inc(s_ga, 1)
                    exps(c, 0)
                    for b in range(XB):
                        gb, i = c * XB + b, b % 2
                        act.wait_ge(s_t, gb * KT + 1)
                        wait(act, s_m, gb - 1)
                        nc.scalar.copy(PT[:, i, 0, :], pA[0][:, :]).then_inc(s_pa, 1)
                        if b + 1 < XB:
                            exps(c, b + 1)
                        act.wait_ge(s_m, gb + 1)
                        if b == 0:
                            wait(act, s_o, c * FT)
                        nc.scalar.copy(MX[:, 0, :, b * L:(b + 1) * L],
                                       pM[0][:, :].rearrange("p (h q) -> p h q", q=L)).then_inc(s_ma, 1)
                    for f in range(FT):
                        act.wait_ge(s_o, c * FT + f + 1)
                        if f == 0:
                            wait(act, s_y, c * XTP)
                        nc.scalar.activation(OT[:, f, :], pA[f % 2][:, 0:XCH], ACT.Identity,
                                             bias=BV[:, f:f + 1]).then_inc(s_oe, 1)

                def exps(c, b):
                    gb, i = c * XB + b, b % 2
                    act.wait_ge(s_nb, gb + 1)
                    wait(act, s_t, (gb - 1) * KT)
                    wait(act, s_rc, gb - 1)
                    for t in range(RT4):
                        nc.scalar.activation(PR[:, i, t, :], pS[t][:, 0:SK], ACT.Exp, bias=NB[:, i, t:t + 1],
                                             scale=XD ** -0.5, accum_out=SM[:, i, t:t + 1]).then_inc(s_e, 1)

                passes(act, body)

            @block.gpsimd
            def _(pool):
                def body(c):
                    layer_norm_pool(nc, pool, c, s, ln, XTP)
                    if isinstance(c, int):
                        pool.wait_ge(s_w, NLD)
                    for t in range(XTP):
                        pool.wait_ge(s["xn"], c * XTP + t + 1)
                        xt = X[:, bass.ds(c * XTP + t, 1), :].rearrange("p a d -> p (a d)")
                        nc.gpsimd.tensor_tensor(xt, xt, BO[:, :], ALU.add).then_inc(s_xb, 1)

                passes(pool, body)


NE1 = 8
F1 = 1024
FT1 = F1 // P
TOP = 2
SLOT_TILES = (TOP * TOK + NE1 * (P - 1)) // P
SLOTS = SLOT_TILES * P


def routed_ffn1(nc, tag, X, g, dram, out):
    with ExitStack() as ctx:
        a = Scope(nc, ctx, tag)
        sb, ps, sem = a.sb, a.ps, a.sem
        GU, WE = KT * 2 * F1, KT * 2 * F1 + FT1 * D
        W = sb("w_experts", [P, NE1 * WE])
        carve = Carve(W[:, (NE1 - 1) * WE:NE1 * WE])
        POS = sb("slots", [P, TOP, TILES], U32)
        WT = sb("weights", [P, TOP, TILES])
        E32 = sb("tile_expert", [1, SLOT_TILES], U32)
        x_mid = nc.dram_tensor("x_mid", (TOK, D), F32, kind="Internal").ap()
        xs = nc.dram_tensor("x_slots", (SLOTS, D), F32, kind="Internal").ap()
        ys = nc.dram_tensor("y_slots", (SLOTS, D), F32, kind="Internal").ap()
        s_we = sem("experts_loaded")
        NWE = 16 * 2 * NE1
        s_sc = sem("rows_scattered")

        def load_expert(sp, e):
            gu = W[:, e * WE:e * WE + GU].rearrange("p (k n) -> p k n", k=KT)
            dn = W[:, e * WE + GU:(e + 1) * WE].rearrange("p (f n) -> p f n", f=FT1)
            sp.dma_start(gu, dram["ffn1_gu"][e].rearrange("(k p) n -> p k n", p=P)).then_inc(s_we, 16)
            sp.dma_start(dn, dram["ffn1_d"][e].rearrange("(f p) n -> p f n", p=P)).then_inc(s_we, 16)

        with ExitStack() as ctx2:
            a2 = Scope(nc, ctx2, tag + "r")
            RW = carve.sb("router_w", [P, KT, NE1])
            TRI = carve.sb("before", [P, P])
            IOTA = carve.sb("iota", [P, NE1])
            LG = carve.sb("logits", [P, TILES, NE1])
            s_w, s_mid, s_zf = a2.sem("weights_loaded"), a2.sem("x_stored"), a2.sem("slots_zeroed")
            with ExitStack() as ctx3:
                a3 = Scope(nc, ctx3, tag + "l")
                XN = carve.sb("xn", [P, TPC, D])
                XT = carve.sb("xt", [P, KT, CH])
                ln = layer_norm_buffers(carve)
                ln["mhalf"] = g["mhalf"]
                s = layer_norm_semaphores(a3, g)
                s_z = a3.sem("zeros")
                s_xt, s_xte, s_xk = a3.sem("x_transposed"), a3.sem("xt_ready"), a3.sem("xn_kept")
                s_lg, s_l = a3.sem("logits"), a3.sem("logits_out")
                ZR = carve.sb("zeros", [P, D])
                pT = [a3.ps(f"pT{j}", [P, 512]) for j in range(KT)]
                pL = a3.ps("pL", [P, TPC, NE1])
                with nc.Block() as block:
                    @block.sync
                    def _(sp):
                        sp.dma_start(RW[:, :, :], dram["ffn1_rT"].rearrange("(k p) n -> p k n", p=P)).then_inc(s_w, 16)
                        sp.dma_start(TRI[:, :], dram["before"]).then_inc(s_w, 16)
                        sp.dma_start(IOTA[:, :], dram["iota32"][:, 0:NE1]).then_inc(s_w, 16)
                        sp.dma_start(x_mid.rearrange("(t p) d -> p t d", p=P), X[:, :, :]).then_inc(s_mid, 16)
                        sp.wait_ge(s_z, 1)
                        sp.dma_start(xs.rearrange("(t p) d -> p t d", p=P),
                                     ZR[:, :].unsqueeze(1).to_broadcast([P, SLOT_TILES, D])).then_inc(s_zf, 16)
                        for e in range(NE1 - 1):
                            load_expert(sp, e)
                        sp.wait_ge(s_zf, 16)
                        sp.wait_ge(s_mid, 16)

                    @block.tensor
                    def _(pe):
                        def body(c):
                            wait(pe, s_xte, c * KT)
                            for t in range(TPC):
                                pe.wait_ge(s["xn"], c * TPC + t + 1)
                                for k in range(KT):
                                    mm = nc.tensor.transpose(pT[k][:, t * P:(t + 1) * P],
                                                             XN[:, t, k * P:(k + 1) * P], g["ident"][:, :])
                            mm.then_inc(s_xt, 1)
                            pe.wait_ge(s_xte, c * KT + KT)
                            wait(pe, s_l, c)
                            for t in range(TPC):
                                for k in range(KT):
                                    mm = nc.tensor.matmul(pL[:, t, :], XT[:, k, t * P:(t + 1) * P], RW[:, k, :],
                                                          start=(k == 0), stop=(k == KT - 1))
                            mm.then_inc(s_lg, 1)

                        pe.wait_ge(s_w, 48)
                        first_then_loop(pe, PASSES, body)

                    @block.vector
                    def _(dve):
                        def body(c):
                            layer_norm_dve(nc, dve, X, c, s, ln)
                            if not isinstance(c, int):
                                logits_out(c - 1)
                            dve.wait_ge(s_xt, c + 1)
                            wait(dve, s_lg, c)
                            for k in range(KT):
                                nc.vector.tensor_copy(XT[:, k, :], pT[k][:, :]).then_inc(s_xte, 1)

                        def logits_out(c):
                            dve.wait_ge(s_lg, c + 1)
                            nc.vector.tensor_copy(LG[:, bass.ds(c * TPC, TPC), :], pL[:, :, :]).then_inc(s_l, 1)

                        nc.vector.memset(ZR[:, :], 0.0).then_inc(s_z, 1)
                        first_then_loop(dve, PASSES, body)
                        logits_out(PASSES - 1)

                    @block.scalar
                    def _(act):
                        def body(c):
                            wait(act, s_xk, c * TPC)
                            layer_norm_act(nc, act, X, XN, c, s, ln, s_xt)

                        first_then_loop(act, PASSES, body)

                    @block.gpsimd
                    def _(pool):
                        def body(c):
                            layer_norm_pool(nc, pool, c, s, ln)
                            for t in range(TPC):
                                pool.wait_ge(s["xn"], c * TPC + t + 1)
                                xt = X[:, bass.ds(c * TPC + t, 1), :].rearrange("p a d -> p (a d)")
                                nc.gpsimd.tensor_copy(xt, XN[:, t, :]).then_inc(s_xk, 1)

                        pool.wait_ge(s_mid, 16)
                        first_then_loop(pool, PASSES, body)

            M8 = carve.sb("max8", [P, TILES, 8])
            I8 = carve.sb("idx8", [P, TILES, 8], U32)
            IX = carve.sb("idx", [P, TILES, TOP])
            OH = carve.sb("onehots", [P, TOP, TILES, NE1])
            CN = carve.sb("chosen", [P, TILES, NE1])
            CP = carve.sb("counted", [P, TILES + 1, NE1])
            NG = carve.sb("more_than", [P, NE1, TILES])
            TH = carve.sb("thresholds", [P, TILES])
            NT = carve.sb("tiles_of", [P, NE1])
            TB = carve.sb("first_tile", [P, NE1 + 1])
            BS = carve.sb("first_slot", [P, TILES, NE1])
            SL = carve.sb("slot_of", [P, TILES, NE1])
            SX = carve.sb("slot_masked", [P, TOP, TILES, NE1])
            PF = carve.sb("slot_f", [P, TOP, TILES])
            EX = carve.sb("exp2", [P, TILES])
            E1 = carve.sb("exp_sum", [P, TILES])
            DF = carve.sb("diff", [P, TILES])
            GE = carve.sb("tile_past", [1, NE1 - 1, SLOT_TILES])
            EF = carve.sb("tile_expert_f", [1, SLOT_TILES])
            ONE = carve.sb("ones", [P, P])
            s_m8, s_i8, s_oh, s_cn = a2.sem("max8"), a2.sem("idx8"), a2.sem("onehots"), a2.sem("chosen")
            s_rk, s_st, s_df, s_ex = a2.sem("ranks"), a2.sem("step"), a2.sem("diff"), a2.sem("exp2")
            s_pos, s_e = a2.sem("slots_known"), a2.sem("experts_known")
            pR = a2.ps("pR", [P, TILES, NE1])
            pC = a2.ps("pC", [P, TILES, NE1])
            with nc.Block() as block:
                @block.vector
                def _(dve):
                    count = [0]

                    def step(ins):
                        count[0] += 1
                        ins.then_inc(s_st, 1)
                        dve.wait_ge(s_st, count[0])

                    nc.vector.memset(ONE[:, :], 1.0)
                    for t in range(TILES):
                        ins = nc.vector.max(M8[:, t, :], LG[:, t, :])
                    step(ins)
                    for t in range(TILES):
                        ins = nc.vector.max_index(I8[:, t, :], M8[:, t, :], LG[:, t, :])
                    step(ins)
                    nc.vector.tensor_tensor(DF[:, :], M8[:, :, 1], M8[:, :, 0], ALU.subtract).then_inc(s_df, 1)
                    step(nc.vector.tensor_copy(IX[:, :, :], I8[:, :, 0:TOP]))
                    for i in range(TOP):
                        ins = nc.vector.tensor_tensor(OH[:, i, :, :],
                                                      IOTA[:, :].unsqueeze(1).to_broadcast([P, TILES, NE1]),
                                                      IX[:, :, i].unsqueeze(2).to_broadcast([P, TILES, NE1]),
                                                      ALU.is_equal)
                    step(ins)
                    nc.vector.tensor_tensor(CN[:, :, :], OH[:, 0], OH[:, 1], ALU.add).then_inc(s_cn, 1)
                    nc.vector.memset(CP[:, 0, :], 0.0)
                    step(nc.vector.memset(TB[:, 0:1], 0.0))
                    for t in range(1, TILES):
                        ins = nc.vector.memset(TH[:, t:t + 1], float(t * P))
                    dve.wait_ge(s_rk, 1)
                    for t in range(TILES):
                        step(nc.vector.tensor_tensor(CP[:, t + 1, :], CP[:, t, :], pC[:, t, :], ALU.add))
                    step(nc.vector.tensor_tensor(
                        NG[:, :, 1:TILES], CP[:, TILES, :].unsqueeze(2).to_broadcast([P, NE1, TILES - 1]),
                        TH[:, 1:TILES].unsqueeze(1).to_broadcast([P, NE1, TILES - 1]), ALU.is_gt))
                    step(nc.vector.tensor_reduce(NT[:, :], NG[:, :, 1:TILES], AX.X, ALU.add))
                    step(nc.vector.tensor_scalar(NT[:, :], NT[:, :], 1.0, None, ALU.add))
                    for e in range(NE1):
                        step(nc.vector.tensor_tensor(TB[:, e + 1:e + 2], TB[:, e:e + 1], NT[:, e:e + 1], ALU.add))
                    step(nc.vector.scalar_tensor_tensor(
                        out=BS[:, :, :], in0=TB[:, 0:NE1].unsqueeze(1).to_broadcast([P, TILES, NE1]), scalar=float(P),
                        in1=CP[:, 0:TILES, :], op0=ALU.mult, op1=ALU.add))
                    step(nc.vector.tensor_tensor(SL[:, :, :], pR[:, :, :], BS[:, :, :], ALU.add))
                    for i in range(TOP):
                        ins = nc.vector.tensor_tensor(SX[:, i], SL[:, :, :], OH[:, i], ALU.mult)
                    step(ins)
                    for i in range(TOP):
                        ins = nc.vector.tensor_reduce(PF[:, i, :], SX[:, i], AX.X, ALU.add)
                    step(ins)
                    nc.vector.tensor_copy(POS[:, :, :], PF[:, :, :]).then_inc(s_pos, 1)
                    for e in range(1, NE1):
                        ins = nc.vector.tensor_scalar(GE[0:1, e - 1, :], g["tile_no"][0:1, :], TB[0:1, e:e + 1], None,
                                                      ALU.is_ge)
                    step(ins)
                    step(nc.vector.tensor_reduce(EF[:, :], GE[:, :, :].rearrange("p e t -> p t e"), AX.X, ALU.add))
                    nc.vector.tensor_copy(E32[:, :], EF[:, :]).then_inc(s_e, 1)
                    dve.wait_ge(s_ex, 1)
                    step(nc.vector.tensor_scalar(E1[:, :], EX[:, :], 1.0, None, ALU.add))
                    step(nc.vector.reciprocal(WT[:, 0, :], E1[:, :]))
                    nc.vector.tensor_tensor(WT[:, 1, :], WT[:, 0, :], EX[:, :], ALU.mult)

                @block.scalar
                def _(act):
                    act.wait_ge(s_df, 1)
                    nc.scalar.activation(EX[:, :], DF[:, :], ACT.Exp).then_inc(s_ex, 1)

                @block.tensor
                def _(pe):
                    pe.wait_ge(s_cn, 1)
                    nc.tensor.matmul(pR[:, :, :], TRI[:, :], CN[:, :, :], start=True, stop=True)
                    nc.tensor.matmul(pC[:, :, :], ONE[:, :], CN[:, :, :], start=True, stop=True).then_inc(s_rk, 1)

                @block.gpsimd
                def _(pool):
                    pool.wait_ge(s_pos, 1)
                    for t in range(TILES):
                        for i in range(TOP):
                            pool.indirect_dma_start(xs, bass.IndirectOffsetOnAxis(ap=POS[:, i, t:t + 1], axis=0),
                                                    X[:, t, :], None).then_inc(s_sc, 16)
                    pool.wait_ge(s_sc, 16 * TILES * TOP)

        with ExitStack() as ctx2:
            a2 = Scope(nc, ctx2, tag + "e")
            XF = X[:, :, :].rearrange("p t d -> p (t d)")
            H = XF[:, 0:2 * F1].rearrange("p (i f) -> p i f", i=2)
            HT = XF[:, 2 * F1:3 * F1].rearrange("p (f t) -> p f t", f=FT1)
            XS = XF[:, 3 * F1:3 * F1 + 2 * D].rearrange("p (i d) -> p i d", i=2)
            XST = XF[:, 3 * F1 + 2 * D:4 * F1].rearrange("p (i k t) -> p i k t", i=2, k=KT)
            Y = a2.sb("y", [P, 2, D])
            s_xs = [a2.sem(f"slots_loaded{i}") for i in range(2)]
            s_ys = [a2.sem(f"y_stored{i}") for i in range(2)]
            s_t, s_te = a2.sem("x_transposed"), a2.sem("xt_ready")
            s_g, s_u, s_ge, s_h = a2.sem("gate"), a2.sem("up"), a2.sem("gelu"), a2.sem("hidden")
            s_ht, s_h0, s_h1 = a2.sem("hidden_transposed"), a2.sem("ht0_ready"), a2.sem("ht1_ready")
            s_y, s_ye = a2.sem("down"), a2.sem("y_ready")
            pX = a2.ps("pX", [P, KT, P])
            pG = [a2.ps(f"pG{j}", [P, 512]) for j in range(2)]
            pU = [a2.ps(f"pU{j}", [P, 512]) for j in range(2)]
            pH = [a2.ps(f"pH{j}", [P, 512]) for j in range(2)]
            pY = a2.ps("pY", [P, D])
            NT_ = SLOT_TILES

            def tiles(eng, step, drain):
                step(0, 0)
                step(1, 1)
                with eng.Fori(1, NT_ // 2) as j:
                    step(j * 2, 0)
                    step(j * 2 + 1, 1)
                if NT_ % 2:
                    step(NT_ - 1, 0)
                drain(NT_ - 1)

            with nc.Block() as block:
                @block.sync
                def _(sp):
                    load_expert(sp, NE1 - 1)

                    def step(t, i):
                        wait(sp, s_t, t - 1)
                        sp.dma_start(XS[:, i, :], xs.rearrange("(t p) d -> p t d", p=P)[:, bass.ds(t, 1), :]
                                     .rearrange("p a d -> p (a d)")).then_inc(s_xs[i], 16)

                    tiles(sp, step, lambda t: None)

                @block.tensor
                def _(pe):
                    def turn(t, i):
                        pe.wait_ge(s_xs[i], half(t, i, 16))
                        wait(pe, s_te, t)
                        for k in range(KT):
                            mm = nc.tensor.transpose(pX[:, k, :], XS[:, i, k * P:(k + 1) * P], g["ident"][:, :])
                        mm.then_inc(s_t, 1)

                    def gate_up(t, i):
                        e = pe.value_load(E32[0:1, bass.ds(t, 1)], min_val=0, max_val=NE1 - 1)
                        pe.wait_ge(s_te, t + 1)
                        for n in range(2):
                            for bank, off, done in ((pG, 0, s_g), (pU, F1, s_u)):
                                wait(pe, s_ge if bank is pG else s_h, 2 * t + n - 1)
                                for k in range(KT):
                                    mm = nc.tensor.matmul(bank[n][:, :], XST[:, i, k, :],
                                                          W[:, bass.ds(e * WE + (k * 2 * F1 + off + n * 512), 512)],
                                                          start=(k == 0), stop=(k == KT - 1))
                                mm.then_inc(done, 1)

                    def hidden_across(t, i):
                        pe.wait_ge(s_h, 2 * t + 2)
                        wait(pe, s_h0, t)
                        wait(pe, s_h1, t)
                        for f in range(FT1):
                            mm = nc.tensor.transpose(pH[f // 4][:, (f % 4) * P:(f % 4) * P + P],
                                                     H[:, i, f * P:(f + 1) * P], g["ident"][:, :])
                            if f % 4 == 3:
                                mm.then_inc(s_ht, 1)

                    def down(t):
                        e = pe.value_load(E32[0:1, bass.ds(t, 1)], min_val=0, max_val=NE1 - 1)
                        pe.wait_ge(s_h0, t + 1)
                        pe.wait_ge(s_h1, t + 1)
                        wait(pe, s_ye, t)
                        for f in range(FT1):
                            mm = nc.tensor.matmul(pY[:, :], HT[:, f, :], W[:, bass.ds(e * WE + (GU + f * D), D)],
                                                  start=(f == 0), stop=(f == FT1 - 1))
                        mm.then_inc(s_y, 1)

                    def step(t, i):
                        gate_up(t, i)
                        first = isinstance(t, int) and t == 0
                        if not first:
                            hidden_across(t - 1, 1 - i)
                        if not (isinstance(t, int) and t == NT_ - 1):
                            turn(t + 1, 1 - i)
                        if not first:
                            down(t - 1)

                    def drain(t):
                        hidden_across(t, t % 2)
                        down(t)

                    pe.wait_ge(s_we, NWE)
                    turn(0, 0)
                    tiles(pe, step, drain)

                @block.scalar
                def _(act):
                    def store(t, i):
                        act.wait_ge(s_ye, t + 1)
                        act.dma_start(ys.rearrange("(t p) d -> p t d", p=P)[:, bass.ds(t, 1), :]
                                      .rearrange("p a d -> p (a d)"), Y[:, i, :]).then_inc(s_ys[i], 16)

                    def step(t, i):
                        for n in range(2):
                            act.wait_ge(s_g, 2 * t + n + 1)
                            if n == 0:
                                wait(act, s_ht, 2 * t - 2)
                            nc.scalar.activation(H[:, i, n * 512:(n + 1) * 512], pG[n][:, :],
                                                 ACT.Gelu).then_inc(s_ge, 1)
                        if not (isinstance(t, int) and t == 0):
                            finish(t - 1, 1 - i)

                    def finish(t, i):
                        act.wait_ge(s_ht, 2 * t + 1)
                        wait(act, s_y, t)
                        nc.scalar.copy(HT[:, 0:4, :], pH[0][:, :].rearrange("p (f t) -> p f t", t=P)).then_inc(s_h0, 1)
                        store(t, i)

                    tiles(act, step, lambda t: finish(t, t % 2))
                    for i in range(2):
                        act.wait_ge(s_ys[i], half(NT_ - 1 if (NT_ - 1) % 2 == i else NT_ - 2, i, 16))

                @block.vector
                def _(dve):
                    def rows_across(t, i):
                        dve.wait_ge(s_t, t + 1)
                        wait(dve, s_u, 2 * t - 2)
                        nc.vector.tensor_copy(XST[:, i, :, :], pX[:, :, :]).then_inc(s_te, 1)

                    def step(t, i):
                        if not (isinstance(t, int) and t == 0):
                            across(t - 1)
                        if not (isinstance(t, int) and t == NT_ - 1):
                            rows_across(t + 1, 1 - i)
                        if not (isinstance(t, int) and t == 0):
                            out_rows(t - 1, 1 - i)
                        gated(t, i)

                    def gated(t, i):
                        for n in range(2):
                            dve.wait_ge(s_ge, 2 * t + n + 1)
                            dve.wait_ge(s_u, 2 * t + n + 1)
                            h = H[:, i, n * 512:(n + 1) * 512]
                            nc.vector.tensor_tensor(h, pU[n][:, :], h, ALU.mult).then_inc(s_h, 1)

                    def across(t):
                        dve.wait_ge(s_ht, 2 * t + 2)
                        wait(dve, s_y, t)
                        nc.vector.tensor_copy(HT[:, 4:8, :], pH[1][:, :].rearrange("p (f t) -> p f t", t=P)
                                              ).then_inc(s_h1, 1)

                    def out_rows(t, i):
                        dve.wait_ge(s_y, t + 1)
                        if not (isinstance(t, int) and t < 2):
                            dve.wait_ge(s_ys[i], half(t - 2, i, 16))
                        nc.vector.tensor_copy(Y[:, i, :], pY[:, :]).then_inc(s_ye, 1)

                    def drain(t):
                        across(t)
                        out_rows(t, t % 2)

                    rows_across(0, 0)
                    tiles(dve, step, drain)

        with ExitStack() as ctx2:
            a2 = Scope(nc, ctx2, tag + "c")
            XM = X
            YG = a2.sb("y_gathered", [P, 2, TOP, D])
            s_xm, s_yg = a2.sem("x_loaded"), [a2.sem(f"rows_gathered{i}") for i in range(2)]
            s_a, s_o, s_st = a2.sem("first_added"), a2.sem("out_ready"), a2.sem("out_stored")
            with nc.Block() as block:
                @block.sync
                def _(sp):
                    sp.dma_start(XM[:, :, :], x_mid.rearrange("(t p) d -> p t d", p=P)).then_inc(s_xm, 16)
                    for t in range(0, TILES, TPC):
                        sp.wait_ge(s_o, t + TPC)
                        sp.dma_start(out.rearrange("(t p) d -> p t d", p=P)[:, t:t + TPC, :],
                                     XM[:, t:t + TPC, :]).then_inc(s_st, 16)
                    sp.wait_ge(s_st, 16 * (TILES // TPC))

                @block.gpsimd
                def _(pool):
                    for t in range(TILES):
                        if t >= 2:
                            pool.wait_ge(s_o, t - 1)
                        for i in range(TOP):
                            pool.indirect_dma_start(YG[:, t % 2, i, :], None, ys,
                                                    bass.IndirectOffsetOnAxis(ap=POS[:, i, t:t + 1], axis=0)
                                                    ).then_inc(s_yg[t % 2], 16)

                @block.vector
                def _(dve):
                    dve.wait_ge(s_xm, 16)
                    for t in range(TILES):
                        dve.wait_ge(s_yg[t % 2], 32 * (t // 2 + 1))
                        nc.vector.scalar_tensor_tensor(out=XM[:, t, :], in0=YG[:, t % 2, 0, :],
                                                       scalar=WT[:, 0, t:t + 1], in1=XM[:, t, :],
                                                       op0=ALU.mult, op1=ALU.add).then_inc(s_a, 1)
                        dve.wait_ge(s_a, t + 1)
                        nc.vector.scalar_tensor_tensor(out=XM[:, t, :], in0=YG[:, t % 2, 1, :],
                                                       scalar=WT[:, 1, t:t + 1], in1=XM[:, t, :],
                                                       op0=ALU.mult, op1=ALU.add).then_inc(s_o, 1)


SMALL = {"L0x": ("L0_xattn_", "Wo", "bo"), "L0a": ("L0_attn_", "Wp", "bp"), "L1a": ("L1_attn_", "Wo", "bo")}


def load_phase(nc, dram, X, g):
    loads = [(X[:, :, :], dram["x"].rearrange("(t p) d -> p t d", p=P))]
    loads += [(g[k][:, :], dram[k]) for k in ("ident", "causal", "halves", "cos", "sin", "tile_no")]
    with nc.Block() as block:
        @block.sync
        def _(sp):
            for dst, src in loads:
                sp.dma_start(dst, src).then_inc(g["loaded"], 16)
            sp.wait_ge(g["loaded"], 16 * len(loads))

        @block.gpsimd
        def _(pool):
            nc.gpsimd.memset(g["mhalf"][:, :], -0.5).then_inc(g["made"], 1)
            nc.gpsimd.memset(g["eps"][:, :], EPS).then_inc(g["made"], 1)


def build_program(nc, dram, out, phases=(1, 2, 3, 4, 5, 6)):
    with ExitStack() as ctx:
        a = Scope(nc, ctx, "all")
        X = a.sb("x", [P, TILES, D])
        g = {"ident": a.sb("ident", [P, P]), "causal": a.sb("causal", [P, L]), "halves": a.sb("halves", [P, 2]),
             "cos": a.sb("cos", [P, L]), "sin": a.sb("sin", [P, L]), "mhalf": a.sb("mhalf", [P, TPC]), "eps": a.sb("eps", [P, TPC]), "tile_no": a.sb("tile_no", [1, SLOT_TILES]), "spare": a.sb("spare", [P, 1]),
             "loaded": a.sem("loaded"), "made": a.sem("made")}
        load_phase(nc, dram, X, g)
        if 1 in phases:
            small_attention(nc, "L0x", X, g, dram, True, False, False, dram["ctx_head"])
        if 2 in phases:
            small_attention(nc, "L0a", X, g, dram, True, True, False, None)
        if 3 in phases:
            routed_ffn0(nc, "L0f", X, g, dram)
        if 4 in phases:
            cross_attention(nc, "L1x", X, g, dram)
        if 5 in phases:
            small_attention(nc, "L1a", X, g, dram, False, False, True, None)
        if 6 in phases:
            routed_ffn1(nc, "L1f", X, g, dram, out)
            return
        s_out = a.sem("out_stored")
        with nc.Block() as block:
            @block.sync
            def _(sp):
                sp.dma_start(out.rearrange("(t p) d -> p t d", p=P), X[:, :, :]).then_inc(s_out, 16)
                sp.wait_ge(s_out, 16)


def lay_out(inputs):
    f = {k: np.asarray(v) for k, v in inputs.items()}
    arr = {"x": f["x"].reshape(TOK, D)}
    arr["ctx_head"] = f["ctx_1024"][:, :L, :].reshape(TOK, D).T
    perm = np.array([h * HD + (d + HD // 2) % HD for h in range(NH) for d in range(HD)])
    for tag, (pre, wo, bo) in SMALL.items():
        for kind in "qkv":
            arr[f"{tag}_{kind}T"] = f[f"{pre}W{kind}"].T
            arr[f"{tag}_b{kind}"] = f[f"{pre}b{kind}"]
        arr[f"{tag}_oT"] = f[pre + wo].T
        arr[f"{tag}_bo"] = f[pre + bo]
        if tag == "L0a":
            for kind in "qk":
                arr[f"{tag}_{kind}rT"] = f[f"{pre}W{kind}"].T[:, perm]
                arr[f"{tag}_b{kind}r"] = f[f"{pre}b{kind}"][perm]
    arr["ctx"], arr["ctxT"] = f["ctx_1024"], f["ctx_1024"].transpose(0, 2, 1)
    for kind in "qvo":
        arr[f"L1x_{kind}T"] = f[f"L1_xattn_W{kind}"].T
        arr[f"L1x_b{kind}"] = f[f"L1_xattn_b{kind}"]
    arr["L1x_k"] = f["L1_xattn_Wk"]
    arr["ffn1_rT"] = f["L1_ffn_gate_w"].T
    arr["ffn1_gu"] = f["L1_ffn_gate_up_w"].transpose(0, 2, 1)
    arr["ffn1_d"] = f["L1_ffn_down_w"].transpose(0, 2, 1)
    arr["tile_no"] = np.arange(SLOT_TILES, dtype=np.float32)[None, :]
    arr["before"] = np.triu(np.ones((P, P), np.float32), 1)
    arr["ffn0_rT"], arr["ffn0_rb"] = f["L0_ffn_router_w"].T, f["L0_ffn_router_b"]
    arr["ffn0_w1"] = f["L0_ffn_weights1"].transpose(1, 0, 2).reshape(D, NE0 * H0)
    arr["ffn0_b1"] = f["L0_ffn_bias1"].reshape(NE0 * H0)
    arr["ffn0_w2"] = f["L0_ffn_weights2"].reshape(NE0 * H0, D)
    arr["ffn0_b2"] = f["L0_ffn_bias2"]
    arr["iota32"] = np.tile(np.arange(NE0, dtype=np.float32), (P, 1))
    arr["pair_select"] = (np.arange(NE0)[:, None] == np.arange(NE0 * H0)[None, :] // H0).astype(np.float32)
    cos, sin = rope_tables()
    q = np.arange(P) % L
    arr.update(ident=np.eye(P, dtype=np.float32), cos=cos, sin=sin,
               causal=np.where(np.arange(L)[None, :] > q[:, None], NEG, 0.0).astype(np.float32),
               halves=np.stack([(np.arange(P) // HD) % 2 == e for e in range(2)], 1).astype(np.float32))
    return {k: np.ascontiguousarray(v) for k, v in arr.items()}


def kernel(**inputs):
    import concourse.bacc as bacc
    from concourse.bass_utils import run_bass_kernel_spmd

    arr = lay_out(inputs)
    nc = bacc.Bacc("TRN2", target_bir_lowering=False, num_devices=1, dynamic_dma_scratch_size=8192)
    dram = {k: nc.dram_tensor(f"in_{k}", v.shape, mybir.dt.from_np(v.dtype), kind="ExternalInput").ap()
            for k, v in arr.items()}
    out = nc.dram_tensor("out", (TOK, D), F32, kind="ExternalOutput").ap()
    build_program(nc, dram, out)
    r = run_bass_kernel_spmd(nc, [{f"in_{k}": v for k, v in arr.items()}], core_ids=[0])
    return r.results[0]["out"].reshape(B, L, D)
```

```python
from contextlib import ExitStack

import numpy as np

import concourse.bass as bass
from concourse import mybir

F32 = mybir.dt.float32
U32 = mybir.dt.uint32
BF16 = mybir.dt.bfloat16
F32R = mybir.dt.float32r
ACT = mybir.ActivationFunctionType
ALU = mybir.AluOpType
AX = mybir.AxisListType

P = 128
D = 256
KT = D // P
B, L = 64, 32
TOK = B * L
TILES = TOK // P
BPT = P // L
CH = 512
PASSES = TOK // CH
TPC = CH // P
NH = 16
HD = D // NH
QUADS = 4
NEG = -1.0e30
EPS = 1e-5


class Scope:

    def __init__(self, nc, ctx, tag):
        self.nc, self.ctx, self.tag, self.sems = nc, ctx, tag, []
        ctx.callback(self.free_semaphores)

    def sb(self, name, shape, dt=F32):
        return self.ctx.enter_context(self.nc.sbuf_tensor(f"{self.tag}_{name}", shape, dt))

    def ps(self, name, shape, dt=F32):
        return self.ctx.enter_context(self.nc.psum_tensor(f"{self.tag}_{name}", shape, dt))

    def sem(self, name):
        self.sems.append(self.nc.alloc_semaphore(name=f"{self.tag}_{name}"))
        return self.sems[-1]

    def free_semaphores(self):
        if self.sems:
            self.nc.clear_and_free_semaphores(self.sems)
            self.nc.all_engine_barrier()


class Carve:

    def __init__(self, region):
        self.region, self.at = region, 0

    def sb(self, name, shape, dt=F32):
        n = int(np.prod(shape[1:]))
        assert self.at + n <= self.region.shape[1], name
        v = self.region[0:shape[0], self.at:self.at + n]
        self.at += n
        if dt is not F32:
            v = v.bitcast(dt)
        if len(shape) == 2:
            return v
        names = "abcd"[:len(shape) - 1]
        return v.rearrange(f"p ({' '.join(names)}) -> p {' '.join(names)}",
                           **{k: size for k, size in zip(names, shape[1:])})


def wait(eng, sem, value):
    if not isinstance(value, int) or value > 0:
        eng.wait_ge(sem, value)


def take_wait(nc, g):
    nc.vector.memset(g["spare"][:, :], 0.0)


def take_wait_pe(nc, g, psum):
    nc.tensor.matmul(psum, g["ident"][:, :], g["ident"][:, 0:2], start=True, stop=True)


def pipelined(nc, eng, steps):
    steps(0, None)
    steps(1, 0)
    with eng.Fori(2, PASSES) as c:
        steps(c, c - 1)
    steps(None, PASSES - 1)


def first_then_loop(eng, n, body):
    body(0)
    with eng.Fori(1, n) as c:
        body(c)


def half(t, i, by):
    if isinstance(t, int):
        return (t // 2 + 1) * by
    return (t - i) * (by // 2) + by


def rope_tables():
    half = HD // 2
    inv = (1.0 / np.float32(10000.0) ** (np.arange(0, HD, 2, dtype=np.float32) / np.float32(HD))).astype(np.float32)
    freqs = np.arange(L, dtype=np.float32)[:, None] * inv[None, :]
    emb = np.concatenate((freqs, freqs), axis=-1)
    sign = np.where(np.arange(HD) < half, -1.0, 1.0).astype(np.float32)
    cos = np.cos(emb).astype(np.float32).T
    sin = (np.sin(emb).astype(np.float32) * sign[None, :]).T
    return np.tile(cos, (P // HD, 1)).copy(), np.tile(sin, (P // HD, 1)).copy()


def layer_norm_moments(nc, dve, X, c, s, buf, n=TPC):
    for t in range(n):
        nc.vector.bn_stats(buf["st"][:, t, :], X[:, bass.ds(c * n + t, 1), :]).then_inc(s["st"], 1)
    dve.wait_ge(s["st"], c * n + n)
    take_wait(nc, s["g"])
    for t in range(n):
        nc.vector.bn_aggr(buf["mv"][:, t, :], buf["st"][:, t, :]).then_inc(s["mv"], 1)


def layer_norm_shift(nc, dve, c, s, buf, n=TPC):
    dve.wait_ge(s["rs"], c + 1)
    nc.vector.scalar_tensor_tensor(out=buf["nb"][:, 0:n], in0=buf["mv"][:, 0:n, 0], scalar=-1.0,
                                   in1=buf["rs"][:, 0:n], op0=ALU.mult, op1=ALU.mult).then_inc(s["nb"], 1)


def layer_norm_dve(nc, dve, X, c, s, buf, n=TPC):
    layer_norm_moments(nc, dve, X, c, s, buf, n)
    layer_norm_shift(nc, dve, c, s, buf, n)


def layer_norm_pool(nc, pool, c, s, buf, n=TPC):
    pool.wait_ge(s["mv"], c * n + n)
    nc.gpsimd.tensor_tensor(buf["ve"][:, 0:n], buf["mv"][:, 0:n, 1], s["g"]["eps"][:, 0:n], ALU.add).then_inc(s["ve"], 1)
    pool.wait_ge(s["ve"], c + 1)
    nc.gpsimd.tensor_tensor(buf["rs"][:, 0:n], buf["ve"][:, 0:n], buf["mhalf"][:, 0:n], ALU.pow).then_inc(s["rs"], 1)


def layer_norm_act(nc, act, X, XN, c, s, buf, xn_free, n=TPC):
    act.wait_ge(s["nb"], c + 1)
    wait(act, xn_free, c)
    for t in range(n):
        nc.scalar.activation(XN[:, t, :], X[:, bass.ds(c * n + t, 1), :], ACT.Identity,
                             bias=buf["nb"][:, t:t + 1], scale=buf["rs"][:, t:t + 1]).then_inc(s["xn"], 1)


def layer_norm_buffers(a):
    return {"st": a.sb("ln_stats", [P, TPC, 6]), "mv": a.sb("ln_mean_var", [P, TPC, 2]),
            "ve": a.sb("ln_var_eps", [P, TPC]), "rs": a.sb("ln_rstd", [P, TPC]),
            "nb": a.sb("ln_shift", [P, TPC]), "mhalf": None}


def layer_norm_semaphores(a, g):
    return {"g": g, **{k: a.sem("ln_" + k) for k in ("st", "mv", "ve", "rs", "nb", "xn")}}


def small_attention(nc, tag, X, g, dram, causal, rope, over_heads, ctx_dram):
    NJ = 4
    with ExitStack() as ctx:
        a = Scope(nc, ctx, tag)
        sb, ps, sem = a.sb, a.ps, a.sem
        w, loads = {}, []
        for kind in ["q", "k", "v", "o"] + (["qr", "kr"] if rope else []):
            w[kind] = sb(f"w{kind}", [P, KT, D])
            loads.append((w[kind][:, :, :], dram[f"{tag}_{kind}T"].rearrange("(k p) n -> p k n", p=P)))
            if kind in ("v", "o"):
                w["b" + kind] = sb(f"b{kind}", [P, D])
                loads.append((w["b" + kind][:, :], dram[f"{tag}_b{kind}"].partition_broadcast(P)))
            else:
                w["b" + kind] = sb(f"b{kind}", [P, KT])
                loads.append((w["b" + kind][:, :], dram[f"{tag}_b{kind}"].rearrange("(k p) -> p k", p=P)))
        w["bkm"] = sb("bk_masked", [P, 2, KT])
        s_w, s_bkm = sem("weights_loaded"), sem("masked_bias")
        NLD = 16 * len(loads)
        XN = sb("xn", [P, TPC, D])
        XT = sb("xt", [P, KT, CH])
        CT = sb("ct", [P, KT, CH]) if ctx_dram is not None else None
        QT = sb("qt", [P, KT, CH])
        KTm = sb("ktm", [P, KT, 2, CH])
        KR = sb("kr", [P, KT, CH]) if rope else None
        RT = sb("rt", [P, 2, NJ, CH]) if rope else None
        V = sb("v", [P, TPC, D])
        S = sb("s", [P, TPC, NH, L])
        PT = sb("pt", [P, TPC, NH, L])
        NX = L if over_heads else NH
        MX = sb("mx", [P, TPC, NX])
        SM = sb("sm", [P, TPC, NX])
        RC = sb("rc", [P, TPC, NX])
        O1 = sb("o1", [P, BPT, TPC * KT, L])
        OT = sb("ot", [P, TPC, KT, P])
        ln = layer_norm_buffers(a)
        ln["mhalf"] = g["mhalf"]
        s = layer_norm_semaphores(a, g)
        s_ct = sem("ctx_loaded")
        s_xt, s_xte = sem("x_transposed"), sem("xt_ready")
        s_qp, s_qk = sem("qk_projected"), sem("qk_ready")
        s_r1, s_r2 = sem("rope_products"), sem("rope_summed")
        s_vp, s_v = sem("v_projected"), sem("v_ready")
        s_s, s_m, s_mx, s_sub = sem("scores"), sem("scores_out"), sem("row_max"), sem("shifted")
        s_e, s_sum, s_rc, s_p, s_pt = sem("exps"), sem("sums"), sem("recips"), sem("probs"), sem("probs_t")
        s_o, s_o1, s_ot = sem("pv"), sem("pv_odd"), sem("pv_ready")
        s_y, s_xb, s_x = sem("out_projected"), sem("bias_added"), sem("x_updated")
        pS = [ps(f"psS{j}", [P, 512]) for j in range(4)]
        pO = [ps(f"psO{j}", [P, 512]) for j in range(4)]

        def heads_view(t):
            return S[:, t, :, :].rearrange("p h s -> p s h") if over_heads else S[:, t, :, :]

        def along(T, t):
            v = T[:, t, :]
            return (v.unsqueeze(1) if over_heads else v.unsqueeze(2)).to_broadcast([P, NH, L])

        if rope:
            jobs = [("q", 0), ("qr", 0), ("q", 1), ("qr", 1), ("k", 0), ("kr", 0), ("k", 1), ("kr", 1)]
        else:
            jobs = [("q", 0), ("q", 1), ("k", 0), ("k", 1)]
        NJOB = len(jobs)
        bank = [2, 3, 0, 1, 2, 3, 0, 1]
        NQK = 4 if rope else 6
        FOLDS = BPT * KT

        with nc.Block() as block:
            @block.sync
            def _(sp):
                with nc.allow_non_contiguous_dma(reason="biases onto partitions"):
                    for dst, w_src in loads:
                        sp.dma_start(dst, w_src).then_inc(s_w, 16)
                if ctx_dram is not None:
                    src = ctx_dram.rearrange("(k p) t -> p k t", p=P)
                    sp.dma_start(CT[:, :, :], src[:, :, 0:CH]).then_inc(s_ct, 16)
                    with sp.Fori(1, PASSES) as c:
                        sp.wait_ge(s_vp, c * TPC)
                        sp.dma_start(CT[:, :, :], src[:, :, bass.ds(c * CH, CH)]).then_inc(s_ct, 16)

            @block.tensor
            def _(pe):
                def turn(c):
                    wait(pe, s_qk, c * NQK)
                    wait(pe, s_ot, (c - 1) * FOLDS)
                    if rope:
                        wait(pe, s_r1, c * NJOB)
                    for t in range(TPC):
                        pe.wait_ge(s["xn"], c * TPC + t + 1)
                        for k in range(KT):
                            mm = nc.tensor.transpose(pO[k][:, t * P:(t + 1) * P], XN[:, t, k * P:(k + 1) * P],
                                                     g["ident"][:, :])
                    mm.then_inc(s_xt, 1)

                def source(kind, k):
                    return CT[:, k, :] if kind[0] in "kv" and ctx_dram is not None else XT[:, k, :]

                def project_qk(c):
                    pe.wait_ge(s_xte, c * KT + KT)
                    for n, (kind, f) in enumerate(jobs):
                        if kind == "k" and f == 0 and ctx_dram is not None:
                            pe.wait_ge(s_ct, 16 * (c + 1))
                        if n >= 4:
                            pe.wait_ge(s_r1, c * NJOB + n - 3)
                        for k in range(KT):
                            mm = nc.tensor.matmul(pO[bank[n]][:, :], w[kind][:, k, f * P:(f + 1) * P],
                                                  source(kind, k), start=(k == 0), stop=(k == KT - 1))
                        mm.then_inc(s_qp, 1)

                def project_v(c):
                    wait(pe, s_m, c * QUADS)
                    if ctx_dram is not None:
                        pe.wait_ge(s_ct, 16 * (c + 1))
                    for t in range(TPC):
                        for k in range(KT):
                            mm = nc.tensor.matmul(pS[2 + t // 2][:, (t % 2) * D:(t % 2) * D + D],
                                                  source("v", k)[:, t * P:(t + 1) * P], w["v"][:, k, :],
                                                  start=(k == 0), stop=(k == KT - 1))
                        mm.then_inc(s_vp, 1)

                def scores(c):
                    pe.wait_ge(s_qk, c * NQK + NQK)
                    if rope:
                        pe.wait_ge(s_r2, c * 4 + 4)
                    pe.wait_ge(s_v, c * TPC + TPC)
                    wait(pe, s_x, c * TPC)
                    take_wait_pe(nc, g, pS[0][:, 0:2])
                    for t in range(TPC):
                        for hf in range(KT):
                            for b in range(BPT):
                                for j in range(QUADS):
                                    r = slice(32 * j, 32 * j + 32)
                                    tok = slice(t * P + b * L, t * P + b * L + L)
                                    col = (t * KT + hf) * 2 * L
                                    mm = nc.tensor.matmul(pS[j][b * L:(b + 1) * L, col:col + 2 * L],
                                                          QT[r, hf, tok], KTm[r, hf, :, tok],
                                                          start=True, stop=True)
                    mm.then_inc(s_s, 1)

                def weigh_values(b):
                    pe.wait_ge(s_v, b * TPC + TPC)
                    if rope:
                        pe.wait_ge(s_r1, (b + 1) * NJOB if isinstance(b, int) and b == PASSES - 1
                                   else (b + 2) * NJOB)
                    else:
                        pe.wait_ge(s_qk, (b + 1) * NQK if isinstance(b, int) and b == PASSES - 1
                                   else (b + 2) * NQK)
                    for t in range(TPC):
                        pe.wait_ge(s_pt, b * TPC + t + 1)
                        take_wait_pe(nc, g, pO[0][:, t * P:t * P + 2])
                        for hf in range(KT):
                            for j in range(QUADS):
                                for bb in range(BPT):
                                    r = slice(32 * bb, 32 * bb + 32)
                                    f = hf * P + 32 * j
                                    h = hf * 8 + 2 * j
                                    col = (t * KT + hf) * 2 * L
                                    mm = nc.tensor.matmul(pO[bb][32 * j:32 * j + 32, col:col + 2 * L],
                                                          V[r, t, f:f + 32], PT[r, t, h:h + 2, :],
                                                          start=True, stop=True)
                    mm.then_inc(s_o, 1)

                def project_out(b):
                    pe.wait_ge(s_ot, b * FOLDS + FOLDS)
                    pe.wait_ge(s_m, b * QUADS + QUADS)
                    for t in range(TPC):
                        for k in range(KT):
                            mm = nc.tensor.matmul(pS[t // 2][:, (t % 2) * D:(t % 2) * D + D], OT[:, t, k, :],
                                                  w["o"][:, k, :], start=(k == 0), stop=(k == KT - 1))
                        mm.then_inc(s_y, 1)

                def steps(c, b):
                    if c is not None:
                        turn(c)
                        project_qk(c)
                    if b is not None:
                        weigh_values(b)
                    if c is not None:
                        project_v(c)
                    if b is not None:
                        project_out(b)
                    if c is not None:
                        scores(c)

                pe.wait_ge(s_w, NLD)
                pipelined(nc, pe, steps)

            @block.vector
            def _(dve):
                def transposed(c):
                    dve.wait_ge(s_xt, c + 1)
                    wait(dve, s_vp, c * TPC)
                    for k in range(KT):
                        nc.vector.tensor_copy(XT[:, k, :], pO[k][:, :]).then_inc(s_xte, 1)

                def rope_products(c):
                    wait(dve, s_r2, c * 4)
                    for n, (kind, f) in enumerate(jobs):
                        dve.wait_ge(s_qp, c * NJOB + n + 1)
                        nc.vector.scalar_tensor_tensor(
                            out=RT[:, n % 2, n // 2, :].rearrange("p (b l) -> p b l", l=L),
                            in0=pO[bank[n]][:, :].rearrange("p (b l) -> p b l", l=L),
                            scalar=w["b" + kind][:, f:f + 1],
                            in1=g["sin" if n % 2 else "cos"][:, :].unsqueeze(1).to_broadcast([P, CH // L, L]),
                            op0=ALU.add, op1=ALU.mult).then_inc(s_r1, 1)

                def values(c):
                    wait(dve, s_o, c)
                    for t in range(TPC):
                        if t % 2 == 0:
                            dve.wait_ge(s_vp, c * TPC + t + 2)
                        nc.vector.tensor_tensor(V[:, t, :], pS[2 + t // 2][:, (t % 2) * D:(t % 2) * D + D],
                                                w["bv"][:, :], ALU.add).then_inc(s_v, 1)

                def scores_out(c):
                    dve.wait_ge(s_s, c + 1)
                    wait(dve, s_pt, c * TPC)
                    for j in range(QUADS):
                        i0 = pS[j][:, :].rearrange("p (x e) -> p x e", e=2 * L)
                        o = S[:, :, :, :].rearrange("p t (f j e) s -> p j (t f) (e s)", f=KT, j=QUADS)[:, j]
                        if causal:
                            i0 = i0.rearrange("p x (e s) -> p x e s", e=2)
                            o = o.rearrange("p x (e s) -> p x e s", e=2)
                            msk = g["causal"][:, :].unsqueeze(1).unsqueeze(1).to_broadcast([P, 8, 2, L])
                            nc.vector.tensor_tensor(o, i0, msk, ALU.add).then_inc(s_m, 1)
                        else:
                            nc.vector.tensor_copy(o, i0).then_inc(s_m, 1)
                    dve.wait_ge(s_m, c * QUADS + QUADS)
                    wait(dve, s_sub, c * TPC)
                    for t in range(TPC):
                        nc.vector.tensor_reduce(MX[:, t, :], heads_view(t), AX.X, ALU.max).then_inc(s_mx, 1)

                def softmax_sums(b):
                    wait(dve, s_p, b * TPC)
                    for t in range(TPC):
                        dve.wait_ge(s_e, b * TPC + t + 1)
                        nc.vector.tensor_reduce(SM[:, t, :], heads_view(t), AX.X, ALU.add).then_inc(s_sum, 1)
                        dve.wait_ge(s_sum, b * TPC + t + 1)
                        nc.vector.reciprocal(RC[:, t, :], SM[:, t, :]).then_inc(s_rc, 1)
                    wait(dve, s_o, b)
                    for t in range(TPC):
                        dve.wait_ge(s_p, b * TPC + t + 1)
                        nc.vector.transpose(PT[:, t, :, :], S[:, t, :, :]).then_inc(s_pt, 1)

                def fold_values(b):
                    wait(dve, s_y, b * TPC)
                    for bb in range(BPT):
                        dve.wait_ge(s_o1, b * BPT + bb + 1)
                        for hf in range(KT):
                            src = pO[bb][:, :].rearrange("p (t f e q) -> p f e t q", f=KT, e=2, q=L)[:, hf, 0]
                            odd = O1[:, bb, :, :].rearrange("p (t f) q -> p f t q", f=KT)[:, hf]
                            nc.vector.scalar_tensor_tensor(
                                out=OT[:, :, hf, bb * L:(bb + 1) * L], in0=src, scalar=g["halves"][:, 0:1],
                                in1=odd, op0=ALU.mult, op1=ALU.add).then_inc(s_ot, 1)

                def update(b):
                    for t in range(TPC):
                        dve.wait_ge(s_y, b * TPC + (t // 2) * 2 + 2)
                        dve.wait_ge(s_xb, b * TPC + t + 1)
                        xt = X[:, bass.ds(b * TPC + t, 1), :].rearrange("p a d -> p (a d)")
                        nc.vector.tensor_tensor(xt, pS[t // 2][:, (t % 2) * D:(t % 2) * D + D], xt,
                                                ALU.add).then_inc(s_x, 1)

                def steps(c, b):
                    if c is not None:
                        layer_norm_dve(nc, dve, X, c, s, ln)
                        transposed(c)
                        if rope:
                            rope_products(c)
                    if b is not None:
                        softmax_sums(b)
                        fold_values(b)
                    if c is not None:
                        values(c)
                    if b is not None:
                        update(b)
                    if c is not None:
                        scores_out(c)

                dve.wait_ge(s_w, NLD)
                for e in range(2):
                    nc.vector.tensor_scalar(w["bkm"][:, e, :], w["bk"][:, :], g["halves"][:, e:e + 1], None,
                                            ALU.mult).then_inc(s_bkm, 1)
                pipelined(nc, dve, steps)

            @block.scalar
            def _(act):
                def queries_keys(c):
                    wait(act, s_s, c)
                    if rope:
                        for f in range(KT):
                            act.wait_ge(s_r2, c * 4 + f + 3)
                            for e in range(2):
                                nc.scalar.activation(KTm[:, f, e, :], KR[:, f, :], ACT.Copy,
                                                     scale=g["halves"][:, e:e + 1]).then_inc(s_qk, 1)
                        return
                    for n, (kind, f) in enumerate(jobs):
                        act.wait_ge(s_qp, c * NJOB + n + 1)
                        src = pO[bank[n]][:, :]
                        if kind == "q":
                            nc.scalar.activation(QT[:, f, :], src, ACT.Identity,
                                                 bias=w["bq"][:, f:f + 1]).then_inc(s_qk, 1)
                        else:
                            for e in range(2):
                                nc.scalar.activation(KTm[:, f, e, :], src, ACT.Identity,
                                                     bias=w["bkm"][:, e, f:f + 1],
                                                     scale=g["halves"][:, e:e + 1]).then_inc(s_qk, 1)

                def exps(b):
                    for t in range(TPC):
                        act.wait_ge(s_sub, b * TPC + t + 1)
                        nc.scalar.activation(S[:, t, :, :], S[:, t, :, :], ACT.Exp,
                                             scale=HD ** -0.5).then_inc(s_e, 1)

                def odd_heads(b):
                    act.wait_ge(s_o, b + 1)
                    wait(act, s_ot, b * FOLDS)
                    for bb in range(BPT):
                        src = pO[bb][:, :].rearrange("p (x e q) -> p e x q", e=2, q=L)[:, 1]
                        nc.scalar.activation(O1[:, bb, :, :], src, ACT.Copy,
                                             scale=g["halves"][:, 1:2]).then_inc(s_o1, 1)

                def steps(c, b):
                    if c is not None:
                        layer_norm_act(nc, act, X, XN, c, s, ln, s_xt)
                    if b is not None:
                        exps(b)
                    if c is not None:
                        queries_keys(c)
                    if b is not None:
                        odd_heads(b)

                act.wait_ge(s_w, NLD)
                act.wait_ge(s_bkm, 2)
                pipelined(nc, act, steps)

            @block.gpsimd
            def _(pool):
                def shift(b):
                    for t in range(TPC):
                        pool.wait_ge(s_mx, b * TPC + t + 1)
                        nc.gpsimd.tensor_tensor(S[:, t, :, :], S[:, t, :, :], along(MX, t),
                                                ALU.subtract).then_inc(s_sub, 1)

                def add_bias(c):
                    for t in range(TPC):
                        pool.wait_ge(s["xn"], c * TPC + t + 1)
                        xt = X[:, bass.ds(c * TPC + t, 1), :].rearrange("p a d -> p (a d)")
                        nc.gpsimd.tensor_tensor(xt, xt, w["bo"][:, :], ALU.add).then_inc(s_xb, 1)

                def rope_sums(c):
                    wait(pool, s_s, c)
                    wait(pool, s_qk, c * NQK)
                    for i in range(4):
                        pool.wait_ge(s_r1, c * NJOB + 2 * i + 2)
                        dst = QT[:, i, :] if i < 2 else KR[:, i - 2, :]
                        nc.gpsimd.tensor_tensor(dst, RT[:, 0, i, :], RT[:, 1, i, :], ALU.add).then_inc(s_r2, 1)

                def normalise(b):
                    for t in range(TPC):
                        pool.wait_ge(s_rc, b * TPC + t + 1)
                        nc.gpsimd.tensor_tensor(S[:, t, :, :], S[:, t, :, :], along(RC, t),
                                                ALU.mult).then_inc(s_p, 1)

                def steps(c, b):
                    if c is not None:
                        layer_norm_pool(nc, pool, c, s, ln)
                    if b is not None:
                        shift(b)
                    if c is not None and rope:
                        rope_sums(c)
                    if b is not None:
                        normalise(b)
                    if c is not None:
                        add_bias(c)

                pool.wait_ge(s_w, NLD)
                pipelined(nc, pool, steps)


NE0 = 32
H0 = D // 4
PAIRS = NE0 // 2


def routed_ffn0(nc, tag, X, g, dram):
    with ExitStack() as ctx:
        a = Scope(nc, ctx, tag)
        sb, ps, sem = a.sb, a.ps, a.sem
        W1 = sb("w1", [P, KT, NE0 * H0])
        W2 = sb("w2", [P, PAIRS, D])
        RW = sb("router_w", [P, KT, NE0])
        RB = sb("router_b", [P, NE0])
        B1 = sb("b1", [P, PAIRS])
        B2 = sb("b2", [NE0, D])
        SEL = sb("pair_select", [NE0, PAIRS * P])
        SELh = sb("pair_select_bf", [NE0, PAIRS * P], BF16)
        IOTA = sb("iota", [P, NE0])
        XTall = sb("xt_all", [P, KT, TOK])
        OHall = sb("onehot_t", [NE0, TOK], BF16)
        B2S = sb("b2_selected", [P, TILES, D])
        s_w, s_wb = sem("weights_loaded"), sem("select_ready")
        loads = [(RW[:, :, :], dram["ffn0_rT"].rearrange("(k p) n -> p k n", p=P)),
                 (RB[:, :], dram["ffn0_rb"].partition_broadcast(P)),
                 (IOTA[:, :], dram["iota32"]), (SEL[:, :], dram["pair_select"]), (B2[:, :], dram["ffn0_b2"]),
                 (B1[:, :], dram["ffn0_b1"].rearrange("(j p) -> p j", p=P)),
                 (W1[:, :, :], dram["ffn0_w1"].rearrange("(k p) n -> p k n", p=P)),
                 (W2[:, :, :], dram["ffn0_w2"].rearrange("(j p) n -> p j n", p=P))]
        NLD = 16 * len(loads)

        with ExitStack() as ctx2:
            a2 = Scope(nc, ctx2, tag + "r")
            XN = a2.sb("xn", [P, TPC, D])
            XT = a2.sb("xt", [P, KT, CH])
            LG = a2.sb("logits", [P, TPC, NE0])
            M8 = a2.sb("max8", [P, TPC, 8])
            I8 = a2.sb("idx8", [P, TPC, 8], U32)
            IF = a2.sb("idx", [P, TPC])
            OH = a2.sb("onehot", [P, TPC, NE0])
            OHT = a2.sb("onehot_t", [NE0, CH])
            ln = layer_norm_buffers(a2)
            ln["mhalf"] = g["mhalf"]
            s = layer_norm_semaphores(a2, g)
            s_xt, s_xte, s_xc = a2.sem("x_transposed"), a2.sem("xt_ready"), a2.sem("xt_kept")
            s_lg, s_l, s_m8, s_i8 = a2.sem("logits"), a2.sem("logits_out"), a2.sem("max8"), a2.sem("idx8")
            s_if, s_oh, s_oht, s_ohe = a2.sem("idx"), a2.sem("onehot"), a2.sem("onehot_t"), a2.sem("onehot_out")
            s_ohk = a2.sem("onehot_kept")
            s_b2, s_b2e = a2.sem("b2"), a2.sem("b2_out")
            pT = [a2.ps(f"pT{j}", [P, 512]) for j in range(KT)]
            pL = a2.ps("pL", [P, TPC, NE0])
            pH = a2.ps("pH", [NE0, 512])
            pB = [a2.ps(f"pB{j}", [P, 512]) for j in range(2)]
            with nc.Block() as block:
                @block.sync
                def _(sp):
                    with nc.allow_non_contiguous_dma(reason="biases onto partitions"):
                        for dst, src in loads:
                            sp.dma_start(dst, src).then_inc(s_w, 16)

                @block.tensor
                def _(pe):
                    def select_biases(b):
                        pe.wait_ge(s_oh, b * TPC + TPC)
                        wait(pe, s_ohe, b)
                        wait(pe, s_ohk, b)
                        for t in range(TPC):
                            mm = nc.tensor.transpose(pH[:, t * P:(t + 1) * P], OH[:, t, :], g["ident"][:, :])
                        mm.then_inc(s_oht, 1)
                        pe.wait_ge(s_ohe, b + 1)
                        wait(pe, s_b2e, b * TPC)
                        for t in range(TPC):
                            nc.tensor.matmul(pB[t // 2][:, (t % 2) * D:(t % 2) * D + D], OHT[:, t * P:(t + 1) * P],
                                             B2[:, :], start=True, stop=True).then_inc(s_b2, 1)

                    def logits(c):
                        wait(pe, s_xte, c * KT)
                        wait(pe, s_xc, c * KT)
                        for t in range(TPC):
                            pe.wait_ge(s["xn"], c * TPC + t + 1)
                            for k in range(KT):
                                mm = nc.tensor.transpose(pT[k][:, t * P:(t + 1) * P], XN[:, t, k * P:(k + 1) * P],
                                                         g["ident"][:, :])
                        mm.then_inc(s_xt, 1)
                        pe.wait_ge(s_xte, c * KT + KT)
                        wait(pe, s_l, c)
                        for t in range(TPC):
                            for k in range(KT):
                                mm = nc.tensor.matmul(pL[:, t, :], XT[:, k, t * P:(t + 1) * P], RW[:, k, :],
                                                      start=(k == 0), stop=(k == KT - 1))
                        mm.then_inc(s_lg, 1)

                    def steps(c, b):
                        if b is not None:
                            select_biases(b)
                        if c is not None:
                            logits(c)

                    pe.wait_ge(s_w, NLD)
                    pipelined(nc, pe, steps)

                @block.vector
                def _(dve):
                    def route(b):
                        dve.wait_ge(s_lg, b + 1)
                        nc.vector.tensor_tensor(LG[:, :, :], pL[:, :, :],
                                                RB[:, :].unsqueeze(1).to_broadcast([P, TPC, NE0]),
                                                ALU.add).then_inc(s_l, 1)
                        dve.wait_ge(s_l, b + 1)
                        take_wait(nc, g)
                        for t in range(TPC):
                            nc.vector.max(M8[:, t, :], LG[:, t, :]).then_inc(s_m8, 1)
                        dve.wait_ge(s_m8, b * TPC + TPC)
                        take_wait(nc, g)
                        for t in range(TPC):
                            nc.vector.max_index(I8[:, t, :], M8[:, t, :], LG[:, t, :]).then_inc(s_i8, 1)
                        dve.wait_ge(s_i8, b * TPC + TPC)
                        nc.vector.tensor_copy(IF[:, :], I8[:, :, 0]).then_inc(s_if, 1)
                        wait(dve, s_oht, b)
                        dve.wait_ge(s_if, b + 1)
                        for t in range(TPC):
                            nc.vector.tensor_scalar(OH[:, t, :], IOTA[:, :], IF[:, t:t + 1], None,
                                                    ALU.is_equal).then_inc(s_oh, 1)
                        dve.wait_ge(s_oht, b + 1)
                        wait(dve, s_b2, b * TPC)
                        nc.vector.tensor_copy(OHT[:, :], pH[:, :]).then_inc(s_ohe, 1)
                        for t in range(TPC):
                            if t % 2 == 0:
                                dve.wait_ge(s_b2, b * TPC + t + 2)
                            dst = B2S[:, bass.ds(b * TPC + t, 1), :].rearrange("p a d -> p (a d)")
                            nc.vector.tensor_copy(dst, pB[t // 2][:, (t % 2) * D:(t % 2) * D + D]).then_inc(s_b2e, 1)

                    def transposed(c):
                        dve.wait_ge(s_xt, c + 1)
                        wait(dve, s_lg, c)
                        for k in range(KT):
                            nc.vector.tensor_copy(XT[:, k, :], pT[k][:, :]).then_inc(s_xte, 1)

                    def steps(c, b):
                        if c is not None:
                            layer_norm_dve(nc, dve, X, c, s, ln)
                        if b is not None:
                            route(b)
                        if c is not None:
                            transposed(c)

                    dve.wait_ge(s_w, NLD)
                    nc.vector.tensor_copy(SELh[:, :], SEL[:, :]).then_inc(s_wb, 1)
                    pipelined(nc, dve, steps)

                @block.scalar
                def _(act):
                    def steps(c, b):
                        if b is not None:
                            act.wait_ge(s_ohe, b + 1)
                            nc.scalar.copy(OHall[:, bass.ds(b * CH, CH)], OHT[:, :]).then_inc(s_ohk, 1)
                        if c is not None:
                            layer_norm_act(nc, act, X, XN, c, s, ln, s_xt)
                            act.wait_ge(s_xte, c * KT + KT)
                            for k in range(KT):
                                nc.scalar.copy(XTall[:, k, bass.ds(c * CH, CH)], pT[k][:, :]).then_inc(s_xc, 1)

                    pipelined(nc, act, steps)

                @block.gpsimd
                def _(pool):
                    layer_norm_pool(nc, pool, 0, s, ln)
                    with pool.Fori(1, PASSES) as c:
                        layer_norm_pool(nc, pool, c, s, ln)

        with ExitStack() as ctx3:
            a3 = Scope(nc, ctx3, tag + "e")
            HR = a3.sb("hidden", [P, 2, CH])
            HM = a3.sb("hidden_masked", [P, 2, CH])
            Y = a3.sb("y", [P, TPC, D])
            s_h, s_hr, s_mk, s_hm = a3.sem("hidden"), a3.sem("hidden_out"), a3.sem("mask"), a3.sem("masked")
            s_y2, s_yp, s_y, s_x = a3.sem("pair_summed"), a3.sem("y"), a3.sem("y_out"), a3.sem("x_updated")
            pH = [a3.ps(f"pH{j}", [P, 512]) for j in range(3)]
            pM = [a3.ps(f"pM{j}", [P, 512]) for j in range(3)]
            pY = [a3.ps(f"pY{j}", [P, 512]) for j in range(2)]
            PP = PAIRS

            def passes(eng, body):
                body(0)
                with eng.Fori(1, PASSES) as c:
                    body(c)

            with nc.Block() as block:
                @block.tensor
                def _(pe):
                    def hidden(c, p):
                        wait(pe, s_hr, c * PP + p - 2)
                        wait(pe, s_hm, c * PP + p - 2)
                        for k in range(KT):
                            mm = nc.tensor.matmul(pH[p % 3][:, :], W1[:, k, p * P:(p + 1) * P],
                                                  XTall[:, k, bass.ds(c * CH, CH)],
                                                  start=(k == 0), stop=(k == KT - 1))
                        mm.then_inc(s_h, 1)
                        nc.tensor.matmul(pM[p % 3][:, :], SELh[:, p * P:(p + 1) * P], OHall[:, bass.ds(c * CH, CH)],
                                         start=True, stop=True).then_inc(s_mk, 1)

                    def out(c, p):
                        pe.wait_ge(s_hm, c * PP + p + 1)
                        if p == 0:
                            wait(pe, s_y, c * TPC)
                        for t in range(TPC):
                            mm = nc.tensor.matmul(pY[t // 2][:, (t % 2) * D:(t % 2) * D + D],
                                                  HM[:, p % 2, t * P:(t + 1) * P], W2[:, p, :],
                                                  start=(p == 0 and t % 2 == 0), stop=(p == PP - 1),
                                                  skip_group_check=True)
                        mm.then_inc(s_y2, 1)

                    def body(c):
                        for p in range(PP):
                            hidden(c, p)
                            if p > 0:
                                out(c, p - 1)
                        out(c, PP - 1)

                    passes(pe, body)

                @block.scalar
                def _(act):
                    def body(c):
                        for p in range(PP):
                            act.wait_ge(s_h, c * PP + p + 1)
                            wait(act, s_hm, c * PP + p - 1)
                            nc.scalar.activation(HR[:, p % 2, :], pH[p % 3][:, :], ACT.Relu,
                                                 bias=B1[:, p:p + 1]).then_inc(s_hr, 1)

                    passes(act, body)

                @block.vector
                def _(dve):
                    def body(c):
                        for p in range(PP):
                            dve.wait_ge(s_hr, c * PP + p + 1)
                            dve.wait_ge(s_mk, c * PP + p + 1)
                            wait(dve, s_y2, c * PP + p - 1)
                            nc.vector.tensor_tensor(HM[:, p % 2, :], pM[p % 3][:, :], HR[:, p % 2, :],
                                                    ALU.mult).then_inc(s_hm, 1)
                        dve.wait_ge(s_y2, c * PP + PP)
                        wait(dve, s_x, c * TPC)
                        for t in range(TPC):
                            bs = B2S[:, bass.ds(c * TPC + t, 1), :].rearrange("p a d -> p (a d)")
                            nc.vector.tensor_tensor(Y[:, t, :], pY[t // 2][:, (t % 2) * D:(t % 2) * D + D], bs,
                                                    ALU.add).then_inc(s_y, 1)
                        for t in range(TPC):
                            dve.wait_ge(s_y, c * TPC + t + 1)
                            xt = X[:, bass.ds(c * TPC + t, 1), :].rearrange("p a d -> p (a d)")
                            nc.vector.scalar_tensor_tensor(out=xt, in0=Y[:, t, :], scalar=0.0, in1=xt,
                                                           op0=ALU.max, op1=ALU.add).then_inc(s_x, 1)

                    passes(dve, body)


XW = 1024
XD = XW // NH
SK = 257
SK2 = SK + 1
XCH = 256
XTP = XCH // P
XPASSES = TOK // XCH
XB = XCH // L
ROWS = NH * L
RT4 = ROWS // P
FT = XW // P
PARTS = ((0, 0), (0, 1), (1, 0))


def cross_attention(nc, tag, X, g, dram):
    with ExitStack() as ctx:
        a = Scope(nc, ctx, tag)
        sb, ps, sem = a.sb, a.ps, a.sem
        WQ = sb("wq", [P, KT, XW])
        WKr = sb("wk_parts", [P, 2, FT, D], F32R)
        WV = sb("wv", [P, KT, XW])
        WO = sb("wo", [P, FT, D])
        BQ = sb("bq", [P, FT])
        BV = sb("bv", [P, FT])
        BO = sb("bo", [P, D])
        XN = sb("xn", [P, XTP, D])
        XT = sb("xt", [P, KT, XCH])
        QTr = sb("qt_parts", [P, 2, FT, XCH], F32R)
        Gr = sb("queries_to_context", [P, 2, KT, XB, ROWS], F32R)
        CT = sb("ctx_t", [P, KT, SK])
        CTr = sb("ctx_t_parts", [P, 2, 2, KT, SK2], F32R)
        CX = sb("ctx", [P, KT, D])
        CXr = sb("ctx_parts", [P, 2, 2, KT, D], F32R)
        CL = sb("ctx_last", [3, D])
        CLh = sb("ctx_last_hi", [3, D], F32R)
        CLs = sb("ctx_last_stack", [3, 2, D], F32R)
        zeros = sb("zeros", [3, D])
        LM = sb("stack_masks", [3, 2])
        PR = sb("probs", [P, 2 * RT4 * SK])
        PC = sb("probs_last_parts", [P, RT4, 4], F32R)
        NM = sb("neg_max", [P, 2, RT4])
        SM = sb("sums", [P, 2, RT4])
        RC = sb("recips", [P, 2, RT4])
        PL = sb("probs_last", [4, ROWS], F32R)
        MX = sb("mixed_context", [P, KT, NH, XCH])
        IDr = sb("ident_r", [P, P], F32R)
        PRv = PR[:, :].rearrange("p (i t s) -> p i t s", i=2, t=RT4)
        OT = PR[:, 0:FT * XCH].rearrange("p (f t) -> p f t", f=FT)
        PTr = QTr[:, :, 0:KT * ROWS // XCH, :].rearrange("p i f t -> p i (f t)").rearrange(
            "p i (k r) -> p i k r", k=KT)
        WK = MX[:, 0, :, :].rearrange("p h t -> p (h t)")[:, 0:FT * D].rearrange("p (f d) -> p f d", f=FT)
        ln = layer_norm_buffers(a)
        ln["mhalf"] = g["mhalf"]
        s = layer_norm_semaphores(a, g)
        s_wq, s_wk0, s_w, s_wk = sem("wq_loaded"), sem("wk_loaded"), sem("weights_loaded"), sem("wk_split")
        s_ct, s_cx, s_cl = sem("ctx_t_loaded"), sem("ctx_loaded"), sem("ctx_last_loaded")
        s_cts, s_cxs, s_cls, s_pz = sem("ctx_t_split"), sem("ctx_split"), sem("ctx_last_split"), sem("pads_zeroed")
        s_xt, s_xte = sem("x_transposed"), sem("xt_ready")
        s_qp, s_q, s_ql = sem("q_projected"), sem("q_hi"), sem("q_lo")
        s_gp, s_gh, s_gl = sem("g_projected"), sem("g_hi"), sem("g_lo")
        s_s, s_nm, s_e = sem("scores"), sem("row_max"), sem("exps")
        s_rc, s_p, s_pc = sem("recips"), sem("probs"), sem("probs_last")
        s_t, s_tl = sem("probs_transposed"), sem("last_transposed")
        s_ph, s_plo, s_pl = sem("pt_hi"), sem("pt_lo"), sem("pt_last")
        s_m, s_ma, s_md = sem("mixed"), sem("mix0_ready"), sem("mix1_ready")
        s_o, s_oe = sem("heads_projected"), sem("heads_ready")
        s_y, s_xb, s_x = sem("out_projected"), sem("bias_added"), sem("x_updated")
        pS = [ps(f"pS{j}", [P, 512]) for j in range(RT4)]
        pA = [ps(f"pA{j}", [P, 512]) for j in range(2)]
        pM = [ps(f"pM{j}", [P, 512]) for j in range(2)]
        gbank = [pA[0], pA[1]] + pS
        q_loads = [(WQ[:, :, :], dram["L1x_qT"].rearrange("(k p) n -> p k n", p=P)),
                   (BQ[:, :], dram["L1x_bq"].rearrange("(k p) -> p k", p=P))]
        k_loads = [(WK, dram["L1x_k"].rearrange("(k p) n -> p k n", p=P))]
        loads = [(WV[:, :, :], dram["L1x_vT"].rearrange("(k p) n -> p k n", p=P)),
                 (WO[:, :, :], dram["L1x_oT"].rearrange("(k p) n -> p k n", p=P)),
                 (BV[:, :], dram["L1x_bv"].rearrange("(k p) -> p k", p=P)),
                 (BO[:, :], dram["L1x_bo"].partition_broadcast(P)),
                 (LM[:, :], dram["stack_masks"])]
        NLD = 16 * len(loads)
        FIRST = 0
        AHEAD = XB // 2

        def passes(eng, body):
            body(FIRST, 1)
            with eng.Fori(1, XPASSES - 1) as c:
                body(c, c + 1)
            body(XPASSES - 1, None)

        with nc.Block() as block:
            @block.sync
            def _(sp):
                def body(c, nxt):
                    for b in range(XB):
                        gb = c * XB + b
                        wait(sp, s_cts, gb * 2)
                        sp.dma_start(CT[:, :, :], dram["ctxT"].rearrange("b (k p) s -> b p k s", p=P)
                                     [bass.ds(gb, 1)].rearrange("a p k s -> p (a k) s")).then_inc(s_ct, 16)
                        wait(sp, s_cxs, gb * 2)
                        rows = dram["ctx"][bass.ds(gb, 1)]
                        sp.dma_start(CX[:, :, :], rows[:, 0:KT * P, :].rearrange("a (k p) d -> p (a k) d", p=P)
                                     ).then_inc(s_cx, 16)
                        wait(sp, s_cls, gb * 5)
                        row = dram["ctx_last"][bass.ds(gb, 1), :].partition_broadcast(3).rearrange("q a n -> q (a n)")
                        sp.dma_start(CL[:, :], row).then_inc(s_cl, 16)

                with nc.allow_non_contiguous_dma(reason="biases onto partitions"):
                    for group, loaded in ((q_loads, s_wq), (k_loads, s_wk0)):
                        for dst, src in group:
                            sp.dma_start(dst, src).then_inc(loaded, 16)
                    for dst, src in loads:
                        sp.dma_start(dst, src).then_inc(s_w, 16)
                passes(sp, body)

            @block.tensor
            def _(pe):
                def parts(out, lhs, rhs, first=True, last=True):
                    for n, (x, y) in enumerate(PARTS):
                        mm = nc.tensor.matmul(out, lhs(x), rhs(y), start=(first and n == 0),
                                              stop=(last and n == len(PARTS) - 1))
                    return mm

                def queries(c):
                    wait(pe, s_oe, c * FT)
                    for t in range(XTP):
                        pe.wait_ge(s["xn"], c * XTP + t + 1)
                        for k in range(KT):
                            mm = nc.tensor.transpose(pA[k][:, t * P:(t + 1) * P], XN[:, t, k * P:(k + 1) * P],
                                                     g["ident"][:, :])
                    mm.then_inc(s_xt, 1)
                    pe.wait_ge(s_xte, c * KT + KT)
                    wait(pe, s_e, c * XB * RT4)
                    for f in range(FT):
                        if f >= 6:
                            pe.wait_ge(s_ql, c * FT + f - 5)
                        for k in range(KT):
                            mm = nc.tensor.matmul(gbank[f % 6][:, 0:XCH], WQ[:, k, f * P:(f + 1) * P], XT[:, k, :],
                                                  start=(k == 0), stop=(k == KT - 1))
                        mm.then_inc(s_qp, 1)
                    if isinstance(c, int) and c == FIRST:
                        pe.wait_ge(s_wk, 2)
                    for h in range(NH):
                        r = slice(64 * (h % 2), 64 * (h % 2) + 64)
                        need = max(h // 2 + 1, min(h + FT - 6, FT - 1) + 1 if h < 6 else 0)
                        pe.wait_ge(s_ql, c * FT + min(need, FT))
                        if h >= 6:
                            pe.wait_ge(s_gl, c * NH + h - 5)
                        for m in range(KT):
                            mm = parts(gbank[(h + FT) % 6][:, m * XCH:(m + 1) * XCH],
                                       lambda x: WKr[r, x, h // 2, m * P:(m + 1) * P],
                                       lambda y: QTr[r, y, h // 2, :])
                        mm.then_inc(s_gp, 1)

                def scores(c, b):
                    gb, i = c * XB + b, b % 2
                    pe.wait_ge(s_cts, gb * 2 + 2)
                    if b == 0:
                        pe.wait_ge(s_gl, c * NH + NH)
                    for t in range(RT4):
                        wait(pe, s_e, (gb - 1) * RT4 + t + 1)
                        if t == RT4 - 1 and b > 0:
                            pe.wait_ge(s_pl, gb)
                        for k in range(KT):
                            mm = parts(pS[t][:, 0:SK2], lambda x: Gr[:, x, k, b, t * P:(t + 1) * P],
                                       lambda y: CTr[:, i, y, k, :], k == 0, k == KT - 1)
                        mm.then_inc(s_s, 1)

                def turn(c, b):
                    gb, i = c * XB + b, b % 2
                    wait(pe, s_plo, gb * KT)
                    for k in range(KT):
                        for t in range(RT4):
                            if k == 0:
                                pe.wait_ge(s_p, gb * RT4 + t + 1)
                            mm = nc.tensor.transpose(pA[k][:, t * P:(t + 1) * P], PRv[:, i, t, k * P:(k + 1) * P],
                                                     g["ident"][:, :])
                        mm.then_inc(s_t, 1)
                    pe.wait_ge(s_pc, gb * 3 + 3)
                    for t in range(RT4):
                        mm = nc.tensor.transpose(pS[-1][0:4, t * P:(t + 1) * P].bitcast(F32R), PC[:, t, :],
                                                 IDr[:, :])
                    mm.then_inc(s_tl, 1)

                def mix(c, b):
                    gb, i = c * XB + b, b % 2
                    pe.wait_ge(s_cxs, gb * 2 + 2)
                    pe.wait_ge(s_cls, gb * 5 + 5)
                    wait(pe, s_ma, gb)
                    wait(pe, s_md, gb)
                    if b == 0:
                        wait(pe, s_x, c * XTP)
                    pe.wait_ge(s_pl, gb + 1)
                    for m in range(KT):
                        nc.tensor.matmul(pM[m][:, :], CLs[0:3, i, m * P:(m + 1) * P], PL[0:3, :],
                                         start=True, stop=False)
                    for k in range(KT):
                        pe.wait_ge(s_plo, gb * KT + k + 1)
                        for m in range(KT):
                            mm = parts(pM[m][:, :], lambda x: CXr[:, i, x, k, m * P:(m + 1) * P],
                                       lambda y: PTr[:, y, k, :], False, k == KT - 1)
                    mm.then_inc(s_m, 1)

                def outputs(c):
                    if isinstance(c, int) and c == FIRST:
                        pe.wait_ge(s_w, NLD)
                    pe.wait_ge(s_ma, c * XB + XB)
                    pe.wait_ge(s_md, c * XB + XB)
                    for f in range(FT):
                        if f >= 2:
                            pe.wait_ge(s_oe, c * FT + f - 1)
                        for e in range(2):
                            h = 2 * f + e
                            for k in range(KT):
                                mm = nc.tensor.matmul(pA[f % 2][64 * e:64 * e + 64, 0:XCH],
                                                      WV[:, k, h * XD:(h + 1) * XD], MX[:, k, h, :],
                                                      start=(k == 0), stop=(k == KT - 1))
                        mm.then_inc(s_o, 1)
                    pe.wait_ge(s_oe, c * FT + FT)
                    for t in range(XTP):
                        for f in range(FT):
                            mm = nc.tensor.matmul(pM[t][:, 0:D], OT[:, f, t * P:(t + 1) * P], WO[:, f, :],
                                                  start=(f == 0), stop=(f == FT - 1))
                        mm.then_inc(s_y, 1)

                def body(c, nxt):
                    queries(c)
                    scores(c, 0)
                    turn(c, 0)
                    for b in range(XB):
                        if b + 1 < XB:
                            scores(c, b + 1)
                        mix(c, b)
                        if b + 1 < XB:
                            turn(c, b + 1)
                    outputs(c)

                pe.wait_ge(s_wq, 16 * len(q_loads))
                pe.wait_ge(s_pz, 4)
                passes(pe, body)

            @block.vector
            def _(dve):
                def body(c, nxt):
                    dve.wait_ge(s_xt, c + 1)
                    wait(dve, s_qp, c * FT)
                    for k in range(KT):
                        nc.vector.tensor_copy(XT[:, k, :], pA[k][:, 0:XCH]).then_inc(s_xte, 1)
                    for f in range(FT):
                        dve.wait_ge(s_q, c * FT + f + 1)
                        nc.vector.scalar_tensor_tensor(
                            out=QTr[:, 1, f, :], in0=gbank[f % 6][:, 0:XCH], scalar=BQ[:, f:f + 1],
                            in1=QTr[:, 0, f, :].bitcast(F32), op0=ALU.add, op1=ALU.subtract).then_inc(s_ql, 1)
                    if isinstance(c, int) and c == FIRST:
                        dve.wait_ge(s_wk, 1)
                        nc.vector.tensor_tensor(WKr[:, 1, :, :], WK, WKr[:, 0, :, :].bitcast(F32), ALU.subtract
                                                ).then_inc(s_wk, 1)
                    for h in range(NH):
                        dve.wait_ge(s_gh, c * NH + h + 1)
                        for m in range(KT):
                            src = gbank[(h + FT) % 6][:, m * XCH:(m + 1) * XCH].rearrange("p (b q) -> p b q", q=L)
                            ins = nc.vector.scalar_tensor_tensor(
                                out=Gr[:, 1, m, :, h * L:(h + 1) * L], in0=src, scalar=XD ** -0.5,
                                in1=Gr[:, 0, m, :, h * L:(h + 1) * L].bitcast(F32),
                                op0=ALU.mult, op1=ALU.subtract)
                        ins.then_inc(s_gl, 1)
                    row_maxima(c, 0)
                    probabilities(c, 0)
                    for b in range(XB):
                        across(c, b)
                        if nxt is not None and b == AHEAD - 2:
                            layer_norm_moments(nc, dve, X, nxt, s, ln, XTP)
                        if b + 1 < XB:
                            row_maxima(c, b + 1)
                            probabilities(c, b + 1)
                        if nxt is not None and b == AHEAD:
                            layer_norm_shift(nc, dve, nxt, s, ln, XTP)
                        gb = c * XB + b
                        dve.wait_ge(s_m, gb + 1)
                        nc.vector.tensor_copy(MX[:, 1, :, b * L:(b + 1) * L],
                                              pM[1][:, :].rearrange("p (h q) -> p h q", q=L)).then_inc(s_md, 1)
                    for t in range(XTP):
                        dve.wait_ge(s_y, c * XTP + t + 1)
                        dve.wait_ge(s_xb, c * XTP + t + 1)
                        xt = X[:, bass.ds(c * XTP + t, 1), :].rearrange("p a d -> p (a d)")
                        nc.vector.tensor_tensor(xt, pM[t][:, 0:D], xt, ALU.add).then_inc(s_x, 1)

                def row_maxima(c, b):
                    gb, i = c * XB + b, b % 2
                    for t in range(RT4):
                        dve.wait_ge(s_s, gb * RT4 + t + 1)
                        nc.vector.tensor_reduce(NM[:, i, t:t + 1], pS[t][:, 0:SK], AX.X, ALU.max,
                                                negate=True).then_inc(s_nm, 1)

                def across(c, b):
                    gb, i = c * XB + b, b % 2
                    for k in range(KT):
                        dve.wait_ge(s_ph, gb * KT + k + 1)
                        nc.vector.tensor_tensor(PTr[:, 1, k, :], pA[k][:, :], PTr[:, 0, k, :].bitcast(F32),
                                                ALU.subtract).then_inc(s_plo, 1)
                        if k == 0:
                            dve.wait_ge(s_tl, gb + 1)
                            nc.vector.tensor_copy(PL[0:3, :], pS[-1][0:3, :]).then_inc(s_pl, 1)

                def probabilities(c, b):
                    gb, i = c * XB + b, b % 2
                    dve.wait_ge(s_e, gb * RT4 + RT4)
                    nc.vector.reciprocal(RC[:, i, :], SM[:, i, :]).then_inc(s_rc, 1)
                    dve.wait_ge(s_rc, gb + 1)
                    for t in range(RT4):
                        nc.vector.tensor_scalar(PRv[:, i, t, :], PRv[:, i, t, :], RC[:, i, t:t + 1], None,
                                                ALU.mult).then_inc(s_p, 1)
                    dve.wait_ge(s_p, gb * RT4 + RT4)
                    last = PRv[:, i, :, KT * P]
                    nc.vector.tensor_copy(PC[:, :, 0], last).then_inc(s_pc, 1)
                    nc.vector.tensor_copy(PC[:, :, 2], last).then_inc(s_pc, 1)
                    dve.wait_ge(s_pc, gb * 3 + 2)
                    nc.vector.tensor_tensor(PC[:, :, 1], last, PC[:, :, 0].bitcast(F32), ALU.subtract).then_inc(s_pc, 1)

                layer_norm_dve(nc, dve, X, 0, s, ln, XTP)
                nc.vector.memset(CTr[:, :, :, :, SK:SK2].bitcast(F32), 0.0).then_inc(s_pz, 1)
                nc.vector.memset(zeros[:, :], 0.0).then_inc(s_pz, 1)
                nc.vector.memset(PC[:, :, 3:4].bitcast(F32), 0.0).then_inc(s_pz, 1)
                nc.vector.tensor_copy(IDr[:, :], g["ident"][:, :]).then_inc(s_pz, 1)
                dve.wait_ge(s_wq, 16 * len(q_loads))
                passes(dve, body)

            @block.scalar
            def _(act):
                def body(c, nxt):
                    for f in range(FT):
                        act.wait_ge(s_qp, c * FT + f + 1)
                        wait(act, s_gp, c * NH)
                        nc.scalar.activation(QTr[:, 0, f, :], gbank[f % 6][:, 0:XCH], ACT.Identity,
                                             bias=BQ[:, f:f + 1]).then_inc(s_q, 1)
                    if isinstance(c, int) and c == FIRST:
                        act.wait_ge(s_wk0, 16)
                        nc.scalar.copy(WKr[:, 0, :, :], WK).then_inc(s_wk, 1)
                    for h in range(NH):
                        act.wait_ge(s_gp, c * NH + h + 1)
                        nc.scalar.activation(Gr[:, 0, :, :, h * L:(h + 1) * L],
                                             gbank[(h + FT) % 6][:, :].rearrange("p (m b q) -> p m b q", m=KT, q=L),
                                             ACT.Copy, scale=XD ** -0.5).then_inc(s_gh, 1)
                    exps(c, 0)
                    for b in range(XB):
                        gb, i = c * XB + b, b % 2
                        ahead = nxt is not None or b + 2 < XB
                        for k in range(KT):
                            act.wait_ge(s_t, gb * KT + k + 1)
                            wait(act, s_m, gb)
                            nc.scalar.copy(PTr[:, 0, k, :], pA[k][:, :]).then_inc(s_ph, 1)
                        if b + 1 < XB:
                            exps(c, b + 1)
                        if ahead:
                            round_ctx_t(gb + 2, i)
                        act.wait_ge(s_m, gb + 1)
                        nc.scalar.copy(MX[:, 0, :, b * L:(b + 1) * L],
                                       pM[0][:, :].rearrange("p (h q) -> p h q", q=L)).then_inc(s_ma, 1)
                        if ahead:
                            round_ctx(gb + 2, i)
                        if b == AHEAD and nxt is not None:
                            layer_norm_act(nc, act, X, XN, nxt, s, ln, s_xt, XTP)
                    if isinstance(c, int) and c == FIRST:
                        act.wait_ge(s_w, NLD)
                    for f in range(FT):
                        act.wait_ge(s_o, c * FT + f + 1)
                        nc.scalar.activation(OT[:, f, :], pA[f % 2][:, 0:XCH], ACT.Identity,
                                             bias=BV[:, f:f + 1]).then_inc(s_oe, 1)

                def round_ctx_t(gb, i):
                    act.wait_ge(s_ct, gb * 16 + 16)
                    wait(act, s_s, (gb - 1) * RT4 - RT4)
                    nc.scalar.copy(CTr[:, i, 0, :, 0:SK], CT[:, :, :]).then_inc(s_cts, 1)

                def round_ctx(gb, i):
                    act.wait_ge(s_cx, gb * 16 + 16)
                    wait(act, s_m, gb - 1)
                    nc.scalar.copy(CXr[:, i, 0], CX[:, :, :]).then_inc(s_cxs, 1)

                def exps(c, b):
                    gb, i = c * XB + b, b % 2
                    wait(act, s_t, (gb - 1) * KT)
                    wait(act, s_tl, gb - 1)
                    wait(act, s_rc, gb - 1)
                    if b == 0:
                        wait(act, s_y, c * XTP)
                    for t in range(RT4):
                        act.wait_ge(s_nm, gb * RT4 + t + 1)
                        nc.scalar.activation(PRv[:, i, t, :], pS[t][:, 0:SK], ACT.Exp, bias=NM[:, i, t:t + 1],
                                             accum_out=SM[:, i, t:t + 1]).then_inc(s_e, 1)

                layer_norm_act(nc, act, X, XN, 0, s, ln, s_xt, XTP)
                act.wait_ge(s_pz, 1)
                for gb in range(2):
                    round_ctx_t(gb, gb)
                    round_ctx(gb, gb)
                act.wait_ge(s_wq, 16 * len(q_loads))
                passes(act, body)

            @block.gpsimd
            def _(pool):
                def body(c, nxt):
                    for b in range(XB):
                        gb, i = c * XB + b, b % 2
                        for src, dst, split in ((CT[:, :, :], CTr[:, i, :, :, 0:SK], s_cts),
                                                (CX[:, :, :], CXr[:, i], s_cxs)):
                            pool.wait_ge(split, gb * 2 + 1)
                            nc.gpsimd.tensor_tensor(dst[:, 1], src, dst[:, 0].bitcast(F32),
                                                    ALU.subtract).then_inc(split, 1)
                        last_rows(gb, i)
                        if nxt is not None and b == AHEAD:
                            layer_norm_pool(nc, pool, nxt, s, ln, XTP)
                        if nxt is not None and b == AHEAD + 2:
                            add_bias(nxt)

                def last_rows(gb, i):
                    pool.wait_ge(s_cl, gb * 16 + 16)
                    nc.gpsimd.tensor_tensor(CLh[:, :], CL[:, :], zeros[:, :], ALU.add).then_inc(s_cls, 1)
                    pool.wait_ge(s_cls, gb * 5 + 1)
                    nc.gpsimd.tensor_tensor(CL[:, :], CL[:, :], CLh[:, :].bitcast(F32), ALU.subtract).then_inc(s_cls, 1)
                    pool.wait_ge(s_cls, gb * 5 + 2)
                    nc.gpsimd.tensor_tensor(CL[:, :], CL[:, :], LM[:, 1:2].to_broadcast([3, D]), ALU.mult
                                            ).then_inc(s_cls, 1)
                    nc.gpsimd.tensor_tensor(CLh[:, :], CLh[:, :].bitcast(F32), LM[:, 0:1].to_broadcast([3, D]),
                                            ALU.mult).then_inc(s_cls, 1)
                    pool.wait_ge(s_cls, gb * 5 + 4)
                    wait(pool, s_m, gb - 1)
                    nc.gpsimd.tensor_tensor(CLs[:, i, :], CL[:, :], CLh[:, :].bitcast(F32), ALU.add
                                            ).then_inc(s_cls, 1)

                def add_bias(c):
                    for t in range(XTP):
                        pool.wait_ge(s["xn"], c * XTP + t + 1)
                        xt = X[:, bass.ds(c * XTP + t, 1), :].rearrange("p a d -> p (a d)")
                        nc.gpsimd.tensor_tensor(xt, xt, BO[:, :], ALU.add).then_inc(s_xb, 1)

                layer_norm_pool(nc, pool, 0, s, ln, XTP)
                pool.wait_ge(s_w, NLD)
                for t in range(XTP):
                    pool.wait_ge(s["xn"], t + 1)
                    nc.gpsimd.tensor_tensor(X[:, t, :], X[:, t, :], BO[:, :], ALU.add).then_inc(s_xb, 1)
                pool.wait_ge(s_pz, 2)
                passes(pool, body)


NE1 = 8
F1 = 1024
FT1 = F1 // P
TOP = 2
SLOT_TILES = (TOP * TOK + NE1 * (P - 1)) // P
SLOTS = SLOT_TILES * P


def routed_ffn1(nc, tag, X, g, dram, out):
    with ExitStack() as ctx:
        a = Scope(nc, ctx, tag)
        sb, ps, sem = a.sb, a.ps, a.sem
        GU, WE = KT * 2 * F1, KT * 2 * F1 + FT1 * D
        W = sb("w_experts", [P, NE1 * WE])
        carve = Carve(W[:, (NE1 - 1) * WE:NE1 * WE])
        POS = sb("slots", [P, TOP, TILES], U32)
        WT = sb("weights", [P, TOP, TILES])
        E32 = sb("tile_expert", [1, SLOT_TILES], U32)
        x_mid = nc.dram_tensor("x_mid", (TOK, D), F32, kind="Internal").ap()
        xs = nc.dram_tensor("x_slots", (SLOTS, D), F32, kind="Internal").ap()
        ys = nc.dram_tensor("y_slots", (SLOTS, D), F32, kind="Internal").ap()
        s_we = sem("experts_loaded")
        NWE = 16 * 2 * NE1
        s_sc = sem("rows_scattered")

        def load_expert(sp, e):
            gu = W[:, e * WE:e * WE + GU].rearrange("p (k n) -> p k n", k=KT)
            dn = W[:, e * WE + GU:(e + 1) * WE].rearrange("p (f n) -> p f n", f=FT1)
            sp.dma_start(gu, dram["ffn1_gu"][e].rearrange("(k p) n -> p k n", p=P)).then_inc(s_we, 16)
            sp.dma_start(dn, dram["ffn1_d"][e].rearrange("(f p) n -> p f n", p=P)).then_inc(s_we, 16)

        with ExitStack() as ctx2:
            a2 = Scope(nc, ctx2, tag + "r")
            RW = carve.sb("router_w", [P, KT, NE1])
            TRI = carve.sb("before", [P, P])
            IOTA = carve.sb("iota", [P, NE1])
            LG = carve.sb("logits", [P, TILES, NE1])
            s_w, s_mid, s_zf = a2.sem("weights_loaded"), a2.sem("x_stored"), a2.sem("slots_zeroed")
            with ExitStack() as ctx3:
                a3 = Scope(nc, ctx3, tag + "l")
                XN = carve.sb("xn", [P, TPC, D])
                XT = carve.sb("xt", [P, KT, CH])
                ln = layer_norm_buffers(carve)
                ln["mhalf"] = g["mhalf"]
                s = layer_norm_semaphores(a3, g)
                s_z = a3.sem("zeros")
                s_xt, s_xte, s_xk = a3.sem("x_transposed"), a3.sem("xt_ready"), a3.sem("xn_kept")
                s_lg, s_l = a3.sem("logits"), a3.sem("logits_out")
                ZR = carve.sb("zeros", [P, D])
                pT = [a3.ps(f"pT{j}", [P, 512]) for j in range(KT)]
                pL = a3.ps("pL", [P, TPC, NE1])
                with nc.Block() as block:
                    @block.sync
                    def _(sp):
                        sp.dma_start(RW[:, :, :], dram["ffn1_rT"].rearrange("(k p) n -> p k n", p=P)).then_inc(s_w, 16)
                        sp.dma_start(TRI[:, :], dram["before"]).then_inc(s_w, 16)
                        sp.dma_start(IOTA[:, :], dram["iota32"][:, 0:NE1]).then_inc(s_w, 16)
                        sp.dma_start(x_mid.rearrange("(t p) d -> p t d", p=P), X[:, :, :]).then_inc(s_mid, 16)
                        sp.wait_ge(s_z, 1)
                        sp.dma_start(xs.rearrange("(t p) d -> p t d", p=P),
                                     ZR[:, :].unsqueeze(1).to_broadcast([P, SLOT_TILES, D])).then_inc(s_zf, 16)
                        for e in range(NE1 - 1):
                            load_expert(sp, e)
                        sp.wait_ge(s_zf, 16)
                        sp.wait_ge(s_mid, 16)

                    @block.tensor
                    def _(pe):
                        def body(c):
                            wait(pe, s_xte, c * KT)
                            for t in range(TPC):
                                pe.wait_ge(s["xn"], c * TPC + t + 1)
                                for k in range(KT):
                                    mm = nc.tensor.transpose(pT[k][:, t * P:(t + 1) * P],
                                                             XN[:, t, k * P:(k + 1) * P], g["ident"][:, :])
                            mm.then_inc(s_xt, 1)
                            pe.wait_ge(s_xte, c * KT + KT)
                            wait(pe, s_l, c)
                            for t in range(TPC):
                                for k in range(KT):
                                    mm = nc.tensor.matmul(pL[:, t, :], XT[:, k, t * P:(t + 1) * P], RW[:, k, :],
                                                          start=(k == 0), stop=(k == KT - 1))
                            mm.then_inc(s_lg, 1)

                        pe.wait_ge(s_w, 48)
                        first_then_loop(pe, PASSES, body)

                    @block.vector
                    def _(dve):
                        def body(c):
                            layer_norm_dve(nc, dve, X, c, s, ln)
                            if not isinstance(c, int):
                                logits_out(c - 1)
                            dve.wait_ge(s_xt, c + 1)
                            wait(dve, s_lg, c)
                            for k in range(KT):
                                nc.vector.tensor_copy(XT[:, k, :], pT[k][:, :]).then_inc(s_xte, 1)

                        def logits_out(c):
                            dve.wait_ge(s_lg, c + 1)
                            nc.vector.tensor_copy(LG[:, bass.ds(c * TPC, TPC), :], pL[:, :, :]).then_inc(s_l, 1)

                        nc.vector.memset(ZR[:, :], 0.0).then_inc(s_z, 1)
                        first_then_loop(dve, PASSES, body)
                        logits_out(PASSES - 1)

                    @block.scalar
                    def _(act):
                        def body(c):
                            wait(act, s_xk, c * TPC)
                            layer_norm_act(nc, act, X, XN, c, s, ln, s_xt)

                        first_then_loop(act, PASSES, body)

                    @block.gpsimd
                    def _(pool):
                        def body(c):
                            layer_norm_pool(nc, pool, c, s, ln)
                            for t in range(TPC):
                                pool.wait_ge(s["xn"], c * TPC + t + 1)
                                xt = X[:, bass.ds(c * TPC + t, 1), :].rearrange("p a d -> p (a d)")
                                nc.gpsimd.tensor_copy(xt, XN[:, t, :]).then_inc(s_xk, 1)

                        pool.wait_ge(s_mid, 16)
                        first_then_loop(pool, PASSES, body)

            M8 = carve.sb("max8", [P, TILES, 8])
            I8 = carve.sb("idx8", [P, TILES, 8], U32)
            IX = carve.sb("idx", [P, TILES, TOP])
            OH = carve.sb("onehots", [P, TOP, TILES, NE1])
            CN = carve.sb("chosen", [P, TILES, NE1])
            CP = carve.sb("counted", [P, TILES + 1, NE1])
            NG = carve.sb("more_than", [P, NE1, TILES])
            TH = carve.sb("thresholds", [P, TILES])
            NT = carve.sb("tiles_of", [P, NE1])
            TB = carve.sb("first_tile", [P, NE1 + 1])
            BS = carve.sb("first_slot", [P, TILES, NE1])
            SL = carve.sb("slot_of", [P, TILES, NE1])
            SX = carve.sb("slot_masked", [P, TOP, TILES, NE1])
            PF = carve.sb("slot_f", [P, TOP, TILES])
            EX = carve.sb("exp2", [P, TILES])
            E1 = carve.sb("exp_sum", [P, TILES])
            DF = carve.sb("diff", [P, TILES])
            GE = carve.sb("tile_past", [1, NE1 - 1, SLOT_TILES])
            EF = carve.sb("tile_expert_f", [1, SLOT_TILES])
            ONE = carve.sb("ones", [P, P])
            s_m8, s_i8, s_oh, s_cn = a2.sem("max8"), a2.sem("idx8"), a2.sem("onehots"), a2.sem("chosen")
            s_rk, s_st, s_df, s_ex = a2.sem("ranks"), a2.sem("step"), a2.sem("diff"), a2.sem("exp2")
            s_pos, s_e = a2.sem("slots_known"), a2.sem("experts_known")
            pR = a2.ps("pR", [P, TILES, NE1])
            pC = a2.ps("pC", [P, TILES, NE1])
            with nc.Block() as block:
                @block.vector
                def _(dve):
                    count = [0]

                    def step(ins):
                        count[0] += 1
                        ins.then_inc(s_st, 1)
                        dve.wait_ge(s_st, count[0])

                    nc.vector.memset(ONE[:, :], 1.0)
                    for t in range(TILES):
                        ins = nc.vector.max(M8[:, t, :], LG[:, t, :])
                    step(ins)
                    for t in range(TILES):
                        ins = nc.vector.max_index(I8[:, t, :], M8[:, t, :], LG[:, t, :])
                    step(ins)
                    nc.vector.tensor_tensor(DF[:, :], M8[:, :, 1], M8[:, :, 0], ALU.subtract).then_inc(s_df, 1)
                    step(nc.vector.tensor_copy(IX[:, :, :], I8[:, :, 0:TOP]))
                    for i in range(TOP):
                        ins = nc.vector.tensor_tensor(OH[:, i, :, :],
                                                      IOTA[:, :].unsqueeze(1).to_broadcast([P, TILES, NE1]),
                                                      IX[:, :, i].unsqueeze(2).to_broadcast([P, TILES, NE1]),
                                                      ALU.is_equal)
                    step(ins)
                    nc.vector.tensor_tensor(CN[:, :, :], OH[:, 0], OH[:, 1], ALU.add).then_inc(s_cn, 1)
                    nc.vector.memset(CP[:, 0, :], 0.0)
                    step(nc.vector.memset(TB[:, 0:1], 0.0))
                    for t in range(1, TILES):
                        ins = nc.vector.memset(TH[:, t:t + 1], float(t * P))
                    dve.wait_ge(s_rk, 1)
                    for t in range(TILES):
                        step(nc.vector.tensor_tensor(CP[:, t + 1, :], CP[:, t, :], pC[:, t, :], ALU.add))
                    step(nc.vector.tensor_tensor(
                        NG[:, :, 1:TILES], CP[:, TILES, :].unsqueeze(2).to_broadcast([P, NE1, TILES - 1]),
                        TH[:, 1:TILES].unsqueeze(1).to_broadcast([P, NE1, TILES - 1]), ALU.is_gt))
                    step(nc.vector.tensor_reduce(NT[:, :], NG[:, :, 1:TILES], AX.X, ALU.add))
                    step(nc.vector.tensor_scalar(NT[:, :], NT[:, :], 1.0, None, ALU.add))
                    for e in range(NE1):
                        step(nc.vector.tensor_tensor(TB[:, e + 1:e + 2], TB[:, e:e + 1], NT[:, e:e + 1], ALU.add))
                    step(nc.vector.scalar_tensor_tensor(
                        out=BS[:, :, :], in0=TB[:, 0:NE1].unsqueeze(1).to_broadcast([P, TILES, NE1]), scalar=float(P),
                        in1=CP[:, 0:TILES, :], op0=ALU.mult, op1=ALU.add))
                    step(nc.vector.tensor_tensor(SL[:, :, :], pR[:, :, :], BS[:, :, :], ALU.add))
                    for i in range(TOP):
                        ins = nc.vector.tensor_tensor(SX[:, i], SL[:, :, :], OH[:, i], ALU.mult)
                    step(ins)
                    for i in range(TOP):
                        ins = nc.vector.tensor_reduce(PF[:, i, :], SX[:, i], AX.X, ALU.add)
                    step(ins)
                    nc.vector.tensor_copy(POS[:, :, :], PF[:, :, :]).then_inc(s_pos, 1)
                    for e in range(1, NE1):
                        ins = nc.vector.tensor_scalar(GE[0:1, e - 1, :], g["tile_no"][0:1, :], TB[0:1, e:e + 1], None,
                                                      ALU.is_ge)
                    step(ins)
                    step(nc.vector.tensor_reduce(EF[:, :], GE[:, :, :].rearrange("p e t -> p t e"), AX.X, ALU.add))
                    nc.vector.tensor_copy(E32[:, :], EF[:, :]).then_inc(s_e, 1)
                    dve.wait_ge(s_ex, 1)
                    step(nc.vector.tensor_scalar(E1[:, :], EX[:, :], 1.0, None, ALU.add))
                    step(nc.vector.reciprocal(WT[:, 0, :], E1[:, :]))
                    nc.vector.tensor_tensor(WT[:, 1, :], WT[:, 0, :], EX[:, :], ALU.mult)

                @block.scalar
                def _(act):
                    act.wait_ge(s_df, 1)
                    nc.scalar.activation(EX[:, :], DF[:, :], ACT.Exp).then_inc(s_ex, 1)

                @block.tensor
                def _(pe):
                    pe.wait_ge(s_cn, 1)
                    nc.tensor.matmul(pR[:, :, :], TRI[:, :], CN[:, :, :], start=True, stop=True)
                    nc.tensor.matmul(pC[:, :, :], ONE[:, :], CN[:, :, :], start=True, stop=True).then_inc(s_rk, 1)

                @block.gpsimd
                def _(pool):
                    pool.wait_ge(s_pos, 1)
                    for t in range(TILES):
                        for i in range(TOP):
                            pool.indirect_dma_start(xs, bass.IndirectOffsetOnAxis(ap=POS[:, i, t:t + 1], axis=0),
                                                    X[:, t, :], None).then_inc(s_sc, 16)
                    pool.wait_ge(s_sc, 16 * TILES * TOP)

        with ExitStack() as ctx2:
            a2 = Scope(nc, ctx2, tag + "e")
            XF = X[:, :, :].rearrange("p t d -> p (t d)")
            H = XF[:, 0:2 * F1].rearrange("p (i f) -> p i f", i=2)
            HT = XF[:, 2 * F1:3 * F1].rearrange("p (f t) -> p f t", f=FT1)
            XS = XF[:, 3 * F1:3 * F1 + 2 * D].rearrange("p (i d) -> p i d", i=2)
            XST = XF[:, 3 * F1 + 2 * D:4 * F1].rearrange("p (i k t) -> p i k t", i=2, k=KT)
            Y = a2.sb("y", [P, 2, D])
            s_xs = [a2.sem(f"slots_loaded{i}") for i in range(2)]
            s_ys = [a2.sem(f"y_stored{i}") for i in range(2)]
            s_t, s_te = a2.sem("x_transposed"), a2.sem("xt_ready")
            s_g, s_u, s_ge, s_h = a2.sem("gate"), a2.sem("up"), a2.sem("gelu"), a2.sem("hidden")
            s_ht, s_h0, s_h1 = a2.sem("hidden_transposed"), a2.sem("ht0_ready"), a2.sem("ht1_ready")
            s_y, s_ye = a2.sem("down"), a2.sem("y_ready")
            pX = a2.ps("pX", [P, KT, P])
            pG = [a2.ps(f"pG{j}", [P, 512]) for j in range(2)]
            pU = [a2.ps(f"pU{j}", [P, 512]) for j in range(2)]
            pH = [a2.ps(f"pH{j}", [P, 512]) for j in range(2)]
            pY = a2.ps("pY", [P, D])
            NT_ = SLOT_TILES

            def tiles(eng, step, drain):
                step(0, 0)
                step(1, 1)
                with eng.Fori(1, NT_ // 2) as j:
                    step(j * 2, 0)
                    step(j * 2 + 1, 1)
                if NT_ % 2:
                    step(NT_ - 1, 0)
                drain(NT_ - 1)

            with nc.Block() as block:
                @block.sync
                def _(sp):
                    load_expert(sp, NE1 - 1)

                    def step(t, i):
                        wait(sp, s_t, t - 1)
                        sp.dma_start(XS[:, i, :], xs.rearrange("(t p) d -> p t d", p=P)[:, bass.ds(t, 1), :]
                                     .rearrange("p a d -> p (a d)")).then_inc(s_xs[i], 16)

                    tiles(sp, step, lambda t: None)

                @block.tensor
                def _(pe):
                    def turn(t, i):
                        pe.wait_ge(s_xs[i], half(t, i, 16))
                        wait(pe, s_te, t)
                        for k in range(KT):
                            mm = nc.tensor.transpose(pX[:, k, :], XS[:, i, k * P:(k + 1) * P], g["ident"][:, :])
                        mm.then_inc(s_t, 1)

                    def gate_up(t, i):
                        e = pe.value_load(E32[0:1, bass.ds(t, 1)], min_val=0, max_val=NE1 - 1)
                        pe.wait_ge(s_te, t + 1)
                        for n in range(2):
                            for bank, off, done in ((pG, 0, s_g), (pU, F1, s_u)):
                                wait(pe, s_ge if bank is pG else s_h, 2 * t + n - 1)
                                for k in range(KT):
                                    mm = nc.tensor.matmul(bank[n][:, :], XST[:, i, k, :],
                                                          W[:, bass.ds(e * WE + (k * 2 * F1 + off + n * 512), 512)],
                                                          start=(k == 0), stop=(k == KT - 1))
                                mm.then_inc(done, 1)

                    def hidden_across(t, i):
                        pe.wait_ge(s_h, 2 * t + 2)
                        wait(pe, s_h0, t)
                        wait(pe, s_h1, t)
                        for f in range(FT1):
                            mm = nc.tensor.transpose(pH[f // 4][:, (f % 4) * P:(f % 4) * P + P],
                                                     H[:, i, f * P:(f + 1) * P], g["ident"][:, :])
                            if f % 4 == 3:
                                mm.then_inc(s_ht, 1)

                    def down(t):
                        e = pe.value_load(E32[0:1, bass.ds(t, 1)], min_val=0, max_val=NE1 - 1)
                        pe.wait_ge(s_h0, t + 1)
                        pe.wait_ge(s_h1, t + 1)
                        wait(pe, s_ye, t)
                        for f in range(FT1):
                            mm = nc.tensor.matmul(pY[:, :], HT[:, f, :], W[:, bass.ds(e * WE + (GU + f * D), D)],
                                                  start=(f == 0), stop=(f == FT1 - 1))
                        mm.then_inc(s_y, 1)

                    def step(t, i):
                        gate_up(t, i)
                        first = isinstance(t, int) and t == 0
                        if not first:
                            hidden_across(t - 1, 1 - i)
                        if not (isinstance(t, int) and t == NT_ - 1):
                            turn(t + 1, 1 - i)
                        if not first:
                            down(t - 1)

                    def drain(t):
                        hidden_across(t, t % 2)
                        down(t)

                    pe.wait_ge(s_we, NWE)
                    turn(0, 0)
                    tiles(pe, step, drain)

                @block.scalar
                def _(act):
                    def store(t, i):
                        act.wait_ge(s_ye, t + 1)
                        act.dma_start(ys.rearrange("(t p) d -> p t d", p=P)[:, bass.ds(t, 1), :]
                                      .rearrange("p a d -> p (a d)"), Y[:, i, :]).then_inc(s_ys[i], 16)

                    def step(t, i):
                        for n in range(2):
                            act.wait_ge(s_g, 2 * t + n + 1)
                            if n == 0:
                                wait(act, s_ht, 2 * t - 2)
                            nc.scalar.activation(H[:, i, n * 512:(n + 1) * 512], pG[n][:, :],
                                                 ACT.Gelu).then_inc(s_ge, 1)
                        if not (isinstance(t, int) and t == 0):
                            finish(t - 1, 1 - i)

                    def finish(t, i):
                        act.wait_ge(s_ht, 2 * t + 1)
                        wait(act, s_y, t)
                        nc.scalar.copy(HT[:, 0:4, :], pH[0][:, :].rearrange("p (f t) -> p f t", t=P)).then_inc(s_h0, 1)
                        store(t, i)

                    tiles(act, step, lambda t: finish(t, t % 2))
                    for i in range(2):
                        act.wait_ge(s_ys[i], half(NT_ - 1 if (NT_ - 1) % 2 == i else NT_ - 2, i, 16))

                @block.vector
                def _(dve):
                    def rows_across(t, i):
                        dve.wait_ge(s_t, t + 1)
                        wait(dve, s_u, 2 * t - 2)
                        nc.vector.tensor_copy(XST[:, i, :, :], pX[:, :, :]).then_inc(s_te, 1)

                    def step(t, i):
                        if not (isinstance(t, int) and t == 0):
                            across(t - 1)
                        if not (isinstance(t, int) and t == NT_ - 1):
                            rows_across(t + 1, 1 - i)
                        if not (isinstance(t, int) and t == 0):
                            out_rows(t - 1, 1 - i)
                        gated(t, i)

                    def gated(t, i):
                        for n in range(2):
                            dve.wait_ge(s_ge, 2 * t + n + 1)
                            dve.wait_ge(s_u, 2 * t + n + 1)
                            h = H[:, i, n * 512:(n + 1) * 512]
                            nc.vector.tensor_tensor(h, pU[n][:, :], h, ALU.mult).then_inc(s_h, 1)

                    def across(t):
                        dve.wait_ge(s_ht, 2 * t + 2)
                        wait(dve, s_y, t)
                        nc.vector.tensor_copy(HT[:, 4:8, :], pH[1][:, :].rearrange("p (f t) -> p f t", t=P)
                                              ).then_inc(s_h1, 1)

                    def out_rows(t, i):
                        dve.wait_ge(s_y, t + 1)
                        if not (isinstance(t, int) and t < 2):
                            dve.wait_ge(s_ys[i], half(t - 2, i, 16))
                        nc.vector.tensor_copy(Y[:, i, :], pY[:, :]).then_inc(s_ye, 1)

                    def drain(t):
                        across(t)
                        out_rows(t, t % 2)

                    rows_across(0, 0)
                    tiles(dve, step, drain)

        with ExitStack() as ctx2:
            a2 = Scope(nc, ctx2, tag + "c")
            XM = X
            YG = a2.sb("y_gathered", [P, 2, TOP, D])
            s_xm, s_yg = a2.sem("x_loaded"), [a2.sem(f"rows_gathered{i}") for i in range(2)]
            s_a, s_o, s_st = a2.sem("first_added"), a2.sem("out_ready"), a2.sem("out_stored")
            with nc.Block() as block:
                @block.sync
                def _(sp):
                    sp.dma_start(XM[:, :, :], x_mid.rearrange("(t p) d -> p t d", p=P)).then_inc(s_xm, 16)
                    for t in range(0, TILES, TPC):
                        sp.wait_ge(s_o, t + TPC)
                        sp.dma_start(out.rearrange("(t p) d -> p t d", p=P)[:, t:t + TPC, :],
                                     XM[:, t:t + TPC, :]).then_inc(s_st, 16)
                    sp.wait_ge(s_st, 16 * (TILES // TPC))

                @block.gpsimd
                def _(pool):
                    for t in range(TILES):
                        if t >= 2:
                            pool.wait_ge(s_o, t - 1)
                        for i in range(TOP):
                            pool.indirect_dma_start(YG[:, t % 2, i, :], None, ys,
                                                    bass.IndirectOffsetOnAxis(ap=POS[:, i, t:t + 1], axis=0)
                                                    ).then_inc(s_yg[t % 2], 16)

                @block.vector
                def _(dve):
                    dve.wait_ge(s_xm, 16)
                    for t in range(TILES):
                        dve.wait_ge(s_yg[t % 2], 32 * (t // 2 + 1))
                        nc.vector.scalar_tensor_tensor(out=XM[:, t, :], in0=YG[:, t % 2, 0, :],
                                                       scalar=WT[:, 0, t:t + 1], in1=XM[:, t, :],
                                                       op0=ALU.mult, op1=ALU.add).then_inc(s_a, 1)
                        dve.wait_ge(s_a, t + 1)
                        nc.vector.scalar_tensor_tensor(out=XM[:, t, :], in0=YG[:, t % 2, 1, :],
                                                       scalar=WT[:, 1, t:t + 1], in1=XM[:, t, :],
                                                       op0=ALU.mult, op1=ALU.add).then_inc(s_o, 1)


SMALL = {"L0x": ("L0_xattn_", "Wo", "bo"), "L0a": ("L0_attn_", "Wp", "bp"), "L1a": ("L1_attn_", "Wo", "bo")}


def load_phase(nc, dram, X, g):
    loads = [(X[:, :, :], dram["x"].rearrange("(t p) d -> p t d", p=P))]
    loads += [(g[k][:, :], dram[k]) for k in ("ident", "causal", "halves", "cos", "sin", "tile_no")]
    with nc.Block() as block:
        @block.sync
        def _(sp):
            for dst, src in loads:
                sp.dma_start(dst, src).then_inc(g["loaded"], 16)
            sp.wait_ge(g["loaded"], 16 * len(loads))

        @block.gpsimd
        def _(pool):
            nc.gpsimd.memset(g["mhalf"][:, :], -0.5).then_inc(g["made"], 1)
            nc.gpsimd.memset(g["eps"][:, :], EPS).then_inc(g["made"], 1)


def build_program(nc, dram, out, phases=(1, 2, 3, 4, 5, 6)):
    with ExitStack() as ctx:
        a = Scope(nc, ctx, "all")
        X = a.sb("x", [P, TILES, D])
        g = {"ident": a.sb("ident", [P, P]), "causal": a.sb("causal", [P, L]), "halves": a.sb("halves", [P, 2]),
             "cos": a.sb("cos", [P, L]), "sin": a.sb("sin", [P, L]), "mhalf": a.sb("mhalf", [P, TPC]), "eps": a.sb("eps", [P, TPC]), "tile_no": a.sb("tile_no", [1, SLOT_TILES]), "spare": a.sb("spare", [P, 1]),
             "loaded": a.sem("loaded"), "made": a.sem("made")}
        load_phase(nc, dram, X, g)
        if 1 in phases:
            small_attention(nc, "L0x", X, g, dram, True, False, False, dram["ctx_head"])
        if 2 in phases:
            small_attention(nc, "L0a", X, g, dram, True, True, False, None)
        if 3 in phases:
            routed_ffn0(nc, "L0f", X, g, dram)
        if 4 in phases:
            cross_attention(nc, "L1x", X, g, dram)
        if 5 in phases:
            small_attention(nc, "L1a", X, g, dram, False, False, True, None)
        if 6 in phases:
            routed_ffn1(nc, "L1f", X, g, dram, out)
            return
        s_out = a.sem("out_stored")
        with nc.Block() as block:
            @block.sync
            def _(sp):
                sp.dma_start(out.rearrange("(t p) d -> p t d", p=P), X[:, :, :]).then_inc(s_out, 16)
                sp.wait_ge(s_out, 16)


def lay_out(inputs):
    f = {k: np.asarray(v) for k, v in inputs.items()}
    arr = {"x": f["x"].reshape(TOK, D)}
    arr["ctx_head"] = f["ctx_1024"][:, :L, :].reshape(TOK, D).T
    perm = np.array([h * HD + (d + HD // 2) % HD for h in range(NH) for d in range(HD)])
    for tag, (pre, wo, bo) in SMALL.items():
        for kind in "qkv":
            arr[f"{tag}_{kind}T"] = f[f"{pre}W{kind}"].T
            arr[f"{tag}_b{kind}"] = f[f"{pre}b{kind}"]
        arr[f"{tag}_oT"] = f[pre + wo].T
        arr[f"{tag}_bo"] = f[pre + bo]
        if tag == "L0a":
            for kind in "qk":
                arr[f"{tag}_{kind}rT"] = f[f"{pre}W{kind}"].T[:, perm]
                arr[f"{tag}_b{kind}r"] = f[f"{pre}b{kind}"][perm]
    arr["ctx"], arr["ctxT"] = f["ctx_1024"], f["ctx_1024"].transpose(0, 2, 1)
    arr["ctx_last"] = f["ctx_1024"][:, -1, :]
    arr["stack_masks"] = np.array([[1, 0], [1, 0], [0, 1]], np.float32)
    for kind in "qvo":
        arr[f"L1x_{kind}T"] = f[f"L1_xattn_W{kind}"].T
        arr[f"L1x_b{kind}"] = f[f"L1_xattn_b{kind}"]
    arr["L1x_k"] = f["L1_xattn_Wk"]
    arr["ffn1_rT"] = f["L1_ffn_gate_w"].T
    arr["ffn1_gu"] = f["L1_ffn_gate_up_w"].transpose(0, 2, 1)
    arr["ffn1_d"] = f["L1_ffn_down_w"].transpose(0, 2, 1)
    arr["tile_no"] = np.arange(SLOT_TILES, dtype=np.float32)[None, :]
    arr["before"] = np.triu(np.ones((P, P), np.float32), 1)
    arr["ffn0_rT"], arr["ffn0_rb"] = f["L0_ffn_router_w"].T, f["L0_ffn_router_b"]
    arr["ffn0_w1"] = f["L0_ffn_weights1"].transpose(1, 0, 2).reshape(D, NE0 * H0)
    arr["ffn0_b1"] = f["L0_ffn_bias1"].reshape(NE0 * H0)
    arr["ffn0_w2"] = f["L0_ffn_weights2"].reshape(NE0 * H0, D)
    arr["ffn0_b2"] = f["L0_ffn_bias2"]
    arr["iota32"] = np.tile(np.arange(NE0, dtype=np.float32), (P, 1))
    arr["pair_select"] = (np.arange(NE0)[:, None] == np.arange(NE0 * H0)[None, :] // H0).astype(np.float32)
    cos, sin = rope_tables()
    q = np.arange(P) % L
    arr.update(ident=np.eye(P, dtype=np.float32), cos=cos, sin=sin,
               causal=np.where(np.arange(L)[None, :] > q[:, None], NEG, 0.0).astype(np.float32),
               halves=np.stack([(np.arange(P) // HD) % 2 == e for e in range(2)], 1).astype(np.float32))
    return {k: np.ascontiguousarray(v) for k, v in arr.items()}


def kernel(**inputs):
    import concourse.bacc as bacc
    from concourse.bass_utils import run_bass_kernel_spmd

    arr = lay_out(inputs)
    nc = bacc.Bacc("TRN2", target_bir_lowering=False, num_devices=1, dynamic_dma_scratch_size=8192)
    dram = {k: nc.dram_tensor(f"in_{k}", v.shape, mybir.dt.from_np(v.dtype), kind="ExternalInput").ap()
            for k, v in arr.items()}
    out = nc.dram_tensor("out", (TOK, D), F32, kind="ExternalOutput").ap()
    build_program(nc, dram, out)
    r = run_bass_kernel_spmd(nc, [{f"in_{k}": v for k, v in arr.items()}], core_ids=[0])
    return r.results[0]["out"].reshape(B, L, D)
```

```python
from contextlib import ExitStack

import numpy as np

import concourse.bass as bass
from concourse import mybir

F32 = mybir.dt.float32
U32 = mybir.dt.uint32
BF16 = mybir.dt.bfloat16
F32R = mybir.dt.float32r
ACT = mybir.ActivationFunctionType
ALU = mybir.AluOpType
AX = mybir.AxisListType

P = 128
D = 256
KT = D // P
B, L = 64, 32
TOK = B * L
TILES = TOK // P
BPT = P // L
CH = 512
PASSES = TOK // CH
TPC = CH // P
NH = 16
HD = D // NH
NEG = -1.0e30
EPS = 1e-5
PARTS = ((0, 0), (0, 1), (1, 0))


class Scope:

    def __init__(self, nc, ctx, tag):
        self.nc, self.ctx, self.tag, self.sems = nc, ctx, tag, []
        ctx.callback(self.free_semaphores)

    def sb(self, name, shape, dt=F32):
        return self.ctx.enter_context(self.nc.sbuf_tensor(f"{self.tag}_{name}", shape, dt))

    def ps(self, name, shape, dt=F32):
        return self.ctx.enter_context(self.nc.psum_tensor(f"{self.tag}_{name}", shape, dt))

    def sem(self, name):
        self.sems.append(self.nc.alloc_semaphore(name=f"{self.tag}_{name}"))
        return self.sems[-1]

    def free_semaphores(self):
        if self.sems:
            self.nc.clear_and_free_semaphores(self.sems)
            self.nc.all_engine_barrier()


class Carve:

    def __init__(self, region):
        self.region, self.at = region, 0

    def sb(self, name, shape, dt=F32):
        n = int(np.prod(shape[1:]))
        assert self.at + n <= self.region.shape[1], name
        v = self.region[0:shape[0], self.at:self.at + n]
        self.at += n
        if dt is not F32:
            v = v.bitcast(dt)
        if len(shape) == 2:
            return v
        names = "abcd"[:len(shape) - 1]
        return v.rearrange(f"p ({' '.join(names)}) -> p {' '.join(names)}",
                           **{k: size for k, size in zip(names, shape[1:])})


def is_first(c):
    return isinstance(c, int) and c == 0


def wait(eng, sem, value):
    if not isinstance(value, int) or value > 0:
        eng.wait_ge(sem, value)


def take_wait(nc, g):
    nc.vector.memset(g["spare"][:, :], 0.0)


def pipelined(eng, steps):
    steps(0, None, 1)
    steps(1, 0, 2)
    with eng.Fori(2, PASSES - 1) as c:
        steps(c, c - 1, c + 1)
    steps(PASSES - 1, PASSES - 2, None)
    steps(None, PASSES - 1, None)


def first_then_loop(eng, n, body):
    body(0)
    with eng.Fori(1, n) as c:
        body(c)


def half(t, i, by):
    if isinstance(t, int):
        return (t // 2 + 1) * by
    return (t - i) * (by // 2) + by


def rope_tables():
    half = HD // 2
    inv = (1.0 / np.float32(10000.0) ** (np.arange(0, HD, 2, dtype=np.float32) / np.float32(HD))).astype(np.float32)
    freqs = np.arange(L, dtype=np.float32)[:, None] * inv[None, :]
    emb = np.concatenate((freqs, freqs), axis=-1)
    sign = np.where(np.arange(HD) < half, -1.0, 1.0).astype(np.float32)
    cos = np.cos(emb).astype(np.float32)
    sin = np.sin(emb).astype(np.float32) * sign[None, :]
    return np.tile(cos, (BPT, 1)).copy(), np.tile(sin, (BPT, 1)).copy()


def layer_norm_moments(nc, dve, X, c, s, buf, n=TPC, at=None):
    at = c if at is None else at
    for t in range(n):
        nc.vector.bn_stats(buf["st"][:, t, :], X[:, bass.ds(at * n + t, 1), :]).then_inc(s["st"], 1)
    dve.wait_ge(s["st"], c * n + n)
    take_wait(nc, s["g"])
    for t in range(n):
        nc.vector.bn_aggr(buf["mv"][:, t, :], buf["st"][:, t, :]).then_inc(s["mv"], 1)


def layer_norm_shift(nc, dve, c, s, buf, n=TPC):
    dve.wait_ge(s["rs"], c + 1)
    nc.vector.scalar_tensor_tensor(out=buf["nb"][:, 0:n], in0=buf["mv"][:, 0:n, 0], scalar=-1.0,
                                   in1=buf["rs"][:, 0:n], op0=ALU.mult, op1=ALU.mult).then_inc(s["nb"], 1)


def layer_norm_dve(nc, dve, X, c, s, buf, n=TPC):
    layer_norm_moments(nc, dve, X, c, s, buf, n)
    layer_norm_shift(nc, dve, c, s, buf, n)


def layer_norm_pool(nc, pool, c, s, buf, n=TPC):
    pool.wait_ge(s["mv"], c * n + n)
    nc.gpsimd.tensor_tensor(buf["ve"][:, 0:n], buf["mv"][:, 0:n, 1], s["g"]["eps"][:, 0:n], ALU.add).then_inc(s["ve"], 1)
    pool.wait_ge(s["ve"], c + 1)
    nc.gpsimd.tensor_tensor(buf["rs"][:, 0:n], buf["ve"][:, 0:n], buf["mhalf"][:, 0:n], ALU.pow).then_inc(s["rs"], 1)


def layer_norm_act(nc, act, X, XN, c, s, buf, xn_free, n=TPC, at=None):
    at = c if at is None else at
    act.wait_ge(s["nb"], c + 1)
    wait(act, xn_free, c)
    for t in range(n):
        nc.scalar.activation(XN[:, t, :], X[:, bass.ds(at * n + t, 1), :], ACT.Identity,
                             bias=buf["nb"][:, t:t + 1], scale=buf["rs"][:, t:t + 1]).then_inc(s["xn"], 1)


def layer_norm_buffers(a):
    return {"st": a.sb("ln_stats", [P, TPC, 6]), "mv": a.sb("ln_mean_var", [P, TPC, 2]),
            "ve": a.sb("ln_var_eps", [P, TPC]), "rs": a.sb("ln_rstd", [P, TPC]),
            "nb": a.sb("ln_shift", [P, TPC]), "mhalf": None}


def layer_norm_semaphores(a, g):
    return {"g": g, **{k: a.sem("ln_" + k) for k in ("st", "mv", "ve", "rs", "nb", "xn")}}


class Layer:

    def __init__(self, tag, first, causal, rope, ctx):
        self.tag, self.first, self.causal, self.rope, self.ctx = tag, first, causal, rope, ctx


class Pass:

    def __init__(self, ly, x):
        self.ly, self.x, self.n = ly, x, ly.first + x if ly.first else x

    def starts_layer(self, act):
        if is_first(self.x):
            act()


def pipelined_layers(eng, layers, steps):
    for i, ly in enumerate(layers):
        last = Pass(layers[i - 1], PASSES - 1) if i > 0 else None
        following = Pass(layers[i + 1], 0) if i + 1 < len(layers) else None
        steps(Pass(ly, 0), last, Pass(ly, 1))
        steps(Pass(ly, 1), Pass(ly, 0), Pass(ly, 2))
        with eng.Fori(2, PASSES - 1) as x:
            steps(Pass(ly, x), Pass(ly, x - 1), Pass(ly, x + 1))
        steps(Pass(ly, PASSES - 1), Pass(ly, PASSES - 2), following)
    steps(None, Pass(layers[-1], PASSES - 1), None)


def small_attentions(nc, tag, X, g, dram, over_heads, layers, x_rest=None):
    PAIR = 2 * HD
    NP = D // PAIR
    with ExitStack() as ctx:
        a = Scope(nc, ctx, tag)
        sb, ps, sem = a.sb, a.ps, a.sem
        for ly in layers:
            ly.w, ly.loads, ly.s_w = {}, [], sem(f"{ly.tag}_weights_loaded")
            for kind in "qkvo":
                ly.w[kind] = sb(f"{ly.tag}_w{kind}", [P, KT, D])
                ly.w["b" + kind] = sb(f"{ly.tag}_b{kind}", [P, D])
                ly.loads.append((ly.w[kind][:, :, :], dram[f"{ly.tag}_{kind}T"].rearrange("(k p) n -> p k n", p=P)))
                ly.loads.append((ly.w["b" + kind][:, :], dram[f"{ly.tag}_b{kind}"].partition_broadcast(P)))
            ly.all_loaded = 16 * len(ly.loads)
        s_z = sem("zeroed")
        rope = any(ly.rope for ly in layers)
        has_ctx = any(ly.ctx is not None for ly in layers)
        XN = sb("xn", [P, TPC, D])
        XT = sb("xt", [P, KT, CH])
        CT = sb("ct", [P, KT, CH]) if has_ctx else None
        Q = sb("q", [P, TPC * D])
        K = sb("k", [P, TPC * D])
        V = sb("v", [P, TPC * D])
        R1 = {"q": sb("q_cos", [P, TPC * D]), "k": sb("k_cos", [P, TPC * D])} if rope else None
        R2 = {"q": sb("q_sin", [P, TPC * D]), "k": sb("k_sin", [P, TPC * D])} if rope else None
        QT = sb("q_t", [P, TPC * NP, L])
        KTt = sb("k_t", [P, TPC * NP, L])
        QD = sb("q_blocks", [P, TPC * NP, P])
        KM = sb("k_masked", [P, TPC * NP, 2, L])
        S = sb("s", [P, TPC, NH, L])
        PT = sb("probs_t", [P, TPC, NH, L])
        VD = sb("v_blocks", [P, TPC * NP, P])
        U = sb("heads_turned", [P, TPC, NH, PAIR])
        NX = L if over_heads else NH
        MX = sb("mx", [P, TPC, NX])
        SM = sb("sm", [P, TPC, NX])
        RC = sb("rc", [P, TPC, NX])
        O = sb("o", [P, TPC, D])
        OT = sb("o_t", [P, KT, CH])
        ln = layer_norm_buffers(a)
        ln["mhalf"] = g["mhalf"]
        s = layer_norm_semaphores(a, g)
        s_ct = sem("ctx_loaded")
        s_xt, s_xte = sem("x_transposed"), sem("xt_ready")
        s_qp, s_kp, s_vp = sem("q_projected"), sem("k_projected"), sem("v_projected")
        s_q, s_k, s_v = sem("q_ready"), sem("k_ready"), sem("v_ready")
        s_r1, s_r2, s_r = sem("cos_products"), sem("sin_products"), sem("rotated")
        s_qt, s_kt, s_qd, s_km = sem("q_turned"), sem("k_turned"), sem("q_blocks_ready"), sem("k_masked_ready")
        s_s, s_m, s_mx, s_sub = sem("scores"), sem("scores_out"), sem("row_max"), sem("shifted")
        s_e, s_sum, s_rc, s_p = sem("exps"), sem("sums"), sem("recips"), sem("probs")
        s_pt, s_vd = sem("probs_turned"), sem("v_blocks_ready")
        s_u = sem("heads_turned")
        s_pv, s_o, s_tr, s_ot = sem("values_weighed"), sem("heads_ready"), sem("heads_transposed"), sem("heads_t_ready")
        s_y, s_xb, s_x = sem("out_projected"), sem("bias_added"), sem("x_updated")
        pA = [ps(f"psA{j}", [P, 512]) for j in range(2)]
        pB = [ps(f"psB{j}", [P, 512]) for j in range(2)]
        pS = [ps(f"psS{j}", [P, 512]) for j in range(TPC)]

        def half_bank(banks, t):
            return banks[t // 2][:, (t % 2) * D:(t % 2) * D + D]

        def heads_view(t):
            return S[:, t, :, :].rearrange("p h s -> p s h") if over_heads else S[:, t, :, :]

        def along(T, t):
            v = T[:, t, :]
            return (v.unsqueeze(1) if over_heads else v.unsqueeze(2)).to_broadcast([P, NH, L])

        with nc.Block() as block:
            @block.sync
            def _(sp):
                for ly in layers:
                    for dst, w_src in ly.loads:
                        sp.dma_start(dst, w_src).then_inc(ly.s_w, 16)
                    if ly.ctx is not None:
                        assert ly.first == 0
                        src = ly.ctx.rearrange("(k p) t -> p k t", p=P)
                        sp.dma_start(CT[:, :, :], src[:, :, 0:CH]).then_inc(s_ct, 16)
                        if x_rest is not None:
                            sp.dma_start(*x_rest).then_inc(g["x_rest"], 16)
                        with sp.Fori(1, PASSES) as c:
                            sp.wait_ge(s_vp, c * TPC)
                            sp.dma_start(CT[:, :, :], src[:, :, bass.ds(c * CH, CH)]).then_inc(s_ct, 16)

            @block.tensor
            def _(pe):
                def turn(c):
                    wait(pe, s_k, c.n * TPC)
                    for t in range(TPC):
                        pe.wait_ge(s["xn"], c.n * TPC + t + 1)
                        for k in range(KT):
                            mm = nc.tensor.transpose(pB[k][:, t * P:(t + 1) * P], XN[:, t, k * P:(k + 1) * P],
                                                     g["ident"][:, :])
                    mm.then_inc(s_xt, 1)

                def project(w, banks, src, kind, done):
                    for t in range(TPC):
                        for k in range(KT):
                            mm = nc.tensor.matmul(half_bank(banks, t), src[:, k, t * P:(t + 1) * P], w[kind][:, k, :],
                                                  start=(k == 0), stop=(k == KT - 1))
                        mm.then_inc(done, 1)

                def projections(c):
                    pe.wait_ge(s_xte, c.n * KT + KT)
                    project(c.ly.w, pA, XT, "q", s_qp)
                    wait(pe, s_x, (c.n - 1) * TPC)
                    src = XT
                    if c.ly.ctx is not None:
                        src = CT
                        pe.wait_ge(s_ct, 16 * (c.x + 1))
                    project(c.ly.w, pB, src, "k", s_kp)
                    wait(pe, s_m, c.n * TPC)
                    project(c.ly.w, pS[2:], src, "v", s_vp)

                def weigh_values(b, c):
                    pe.wait_ge(s_m, b.n * TPC + TPC)
                    pe.wait_ge(s_vd, b.n * BPT + BPT)
                    for t in range(TPC):
                        if t == 2 and c is not None:
                            pe.wait_ge(s_v, c.n * TPC + TPC)
                        pe.wait_ge(s_pt, b.n * TPC + t + 1)
                        for j in range(NP):
                            mm = nc.tensor.matmul(pS[t][:, j * 2 * L:(j + 1) * 2 * L], VD[:, t * NP + j, :],
                                                  PT[:, t, 2 * j:2 * j + 2, :], start=True, stop=True)
                        mm.then_inc(s_pv, 1)

                def project_out(b, c, n):
                    if c is not None:
                        pe.wait_ge(s_q, c.n * TPC + TPC)
                    for t in range(TPC):
                        pe.wait_ge(s_o, (b.n * TPC + t) * 2 + 2)
                        for k in range(KT):
                            mm = nc.tensor.transpose(pA[k][:, t * P:(t + 1) * P], O[:, t, k * P:(k + 1) * P],
                                                     g["ident"][:, :])
                    mm.then_inc(s_tr, 1)
                    if n is not None:
                        pe.wait_ge(s_xte, n.n * KT + KT)
                    elif c is not None:
                        pe.wait_ge(s_k, c.n * TPC + TPC)
                    pe.wait_ge(s_ot, b.n * KT + KT)
                    project(b.ly.w, pB, OT, "o", s_y)

                def scores(c, b):
                    pe.wait_ge(s_v, c.n * TPC + TPC)
                    if b is not None:
                        pe.wait_ge(s_u, b.n * TPC + TPC)
                    pe.wait_ge(s_km, c.n * 2 + 2)
                    pe.wait_ge(s_qd, c.n * BPT + BPT)
                    for t in range(TPC):
                        for j in range(NP):
                            mm = nc.tensor.matmul(pS[t][:, j * 2 * L:(j + 1) * 2 * L], QD[:, t * NP + j, :],
                                                  KM[:, t * NP + j, :, :], start=True, stop=True)
                        mm.then_inc(s_s, 1)

                def steps(c, b, n):
                    if c is not None:
                        c.starts_layer(lambda: pe.wait_ge(c.ly.s_w, c.ly.all_loaded))
                        projections(c)
                    if b is not None:
                        weigh_values(b, c)
                    if n is not None:
                        turn(n)
                    if b is not None:
                        project_out(b, c, n)
                    if c is not None:
                        scores(c, b)

                turn(Pass(layers[0], 0))
                pipelined_layers(pe, layers, steps)

            @block.vector
            def _(dve):
                def take(c, banks, dst, kind, made, done):
                    for t in range(TPC):
                        if t % 2 == 0:
                            dve.wait_ge(made, c.n * TPC + t + 2)
                        nc.vector.tensor_tensor(dst[:, t * D:(t + 1) * D], half_bank(banks, t),
                                                c.ly.w["b" + kind][:, :], ALU.add).then_inc(done, 1)

                def cos_product(c, kind, src, ready, order):
                    dve.wait_ge(ready, c.n * TPC + TPC)
                    wait(dve, (s_qt, s_kt)[order], c.n)
                    nc.vector.tensor_tensor(
                        R1[kind][:, :].rearrange("p (x d) -> p x d", d=HD),
                        src[:, :].rearrange("p (x d) -> p x d", d=HD),
                        g["cos"][:, :].unsqueeze(1).to_broadcast([P, TPC * NH, HD]), ALU.mult).then_inc(s_r1, 1)

                def turned(c, src, ready, count, dst, free, per, done):
                    dve.wait_ge(ready, count)
                    wait(dve, free, c.n * per)
                    nc.vector.transpose(dst[:, :, :], src[:, :].rearrange("p (x d) -> p x d", d=PAIR)).then_inc(done, 1)

                def turn_probs(b, tiles):
                    for t in tiles:
                        if over_heads:
                            dve.wait_ge(s_p, b.n * TPC + t + 1)
                        else:
                            dve.wait_ge(s_e, b.n * TPC + t + 1)
                        wait(dve, s_pv, (b.n - 1) * TPC + t + 1)
                        nc.vector.transpose(PT[:, t, :, :], S[:, t, :, :]).then_inc(s_pt, 1)

                def sums(b, tiles=range(TPC)):
                    for t in tiles:
                        dve.wait_ge(s_e, b.n * TPC + t + 1)
                        if over_heads:
                            wait(dve, s_p, b.n * TPC)
                        nc.vector.tensor_reduce(SM[:, t, :], heads_view(t), AX.X, ALU.add).then_inc(s_sum, 1)
                        dve.wait_ge(s_sum, b.n * TPC + t + 1)
                        nc.vector.reciprocal(RC[:, t, :], SM[:, t, :]).then_inc(s_rc, 1)

                def take_heads(b):
                    dve.wait_ge(s_rc, b.n * TPC + TPC)
                    wait(dve, s_tr, b.n)
                    for t in range(TPC + 1):
                        if t < TPC:
                            dve.wait_ge(s_pv, b.n * TPC + t + 1)
                            nc.vector.transpose(U[:, t, :, :], pS[t][:, :].rearrange("p (h q) -> p h q", q=L)
                                                ).then_inc(s_u, 1)
                        if t > 0:
                            own_features(b, t - 1)

                def own_features(b, t):
                    dve.wait_ge(s_u, b.n * TPC + t + 1)
                    for e in range(2):
                        dst = O[:, t, :].rearrange("p (j e d) -> p j e d", e=2, d=HD)[:, :, e, :]
                        src = U[:, t, :, :].rearrange("p (j e) f -> p j e f", e=2)[:, :, e, e * HD:(e + 1) * HD]
                        if over_heads:
                            nc.vector.tensor_copy(dst, src).then_inc(s_o, 1)
                        else:
                            rc = RC[:, t, :].rearrange("p (j e) -> p j e", e=2)[:, :, e]
                            nc.vector.tensor_tensor(dst, src, rc.unsqueeze(2).to_broadcast([P, NP, HD]),
                                                    ALU.mult).then_inc(s_o, 1)

                def update(b):
                    for t in range(TPC):
                        if t % 2 == 0:
                            dve.wait_ge(s_y, b.n * TPC + t + 2)
                        dve.wait_ge(s_xb, b.n * TPC + t + 1)
                        xt = X[:, bass.ds(b.x * TPC + t, 1), :].rearrange("p a d -> p (a d)")
                        nc.vector.tensor_tensor(xt, half_bank(pB, t), xt, ALU.add).then_inc(s_x, 1)

                def scores_out(c):
                    wait(dve, s_pt, c.n * TPC)
                    wait(dve, s_sum, c.n * TPC)
                    wait(dve, s_sub, c.n * TPC)
                    for t in range(TPC):
                        dve.wait_ge(s_s, c.n * TPC + t + 1)
                        src = pS[t][:, :].rearrange("p (h s) -> p h s", s=L)
                        if c.ly.causal:
                            nc.vector.tensor_tensor(S[:, t, :, :], src,
                                                    g["causal"][:, :].unsqueeze(1).to_broadcast([P, NH, L]),
                                                    ALU.add).then_inc(s_m, 1)
                        else:
                            nc.vector.tensor_copy(S[:, t, :, :], src).then_inc(s_m, 1)
                        dve.wait_ge(s_m, c.n * TPC + t + 1)
                        nc.vector.tensor_reduce(MX[:, t, :], heads_view(t), AX.X, ALU.max).then_inc(s_mx, 1)

                def steps(c, b, n):
                    if c is not None:
                        c.starts_layer(lambda: dve.wait_ge(c.ly.s_w, c.ly.all_loaded))
                        take(c, pA, Q, "q", s_qp, s_q)
                        if c.ly.rope:
                            cos_product(c, "q", Q, s_q, 0)
                        else:
                            turned(c, Q, s_q, c.n * TPC + TPC, QT, s_qd, BPT, s_qt)
                    if b is not None:
                        if over_heads:
                            sums(b)
                        turn_probs(b, range(2))
                    if c is not None:
                        take(c, pB, K, "k", s_kp, s_k)
                        if c.ly.rope:
                            cos_product(c, "k", K, s_k, 1)
                        else:
                            turned(c, K, s_k, c.n * TPC + TPC, KTt, s_km, 2, s_kt)
                    if b is not None:
                        turn_probs(b, range(2, TPC))
                    if c is not None:
                        wait(dve, s_vd, c.n * BPT)
                        take(c, pS[2:], V, "v", s_vp, s_v)
                    if c is not None and c.ly.rope:
                        turned(c, R1["q"], s_r, c.x * 2 + 1, QT, s_qd, BPT, s_qt)
                        turned(c, R1["k"], s_r, c.x * 2 + 2, KTt, s_km, 2, s_kt)
                    if n is not None:
                        if x_rest is not None and isinstance(n.n, int) and n.n == 1:
                            dve.wait_ge(g["x_rest"], 16)
                        if n.ly.first > 0:
                            dve.wait_ge(s_x, (n.n - PASSES + 1) * TPC)
                        layer_norm_moments(nc, dve, X, n.n, s, ln, at=n.x)
                    if b is not None and not over_heads:
                        sums(b, range(2))
                    if n is not None:
                        layer_norm_shift(nc, dve, n.n, s, ln)
                    if b is not None and not over_heads:
                        sums(b, range(2, TPC))
                    if b is not None:
                        take_heads(b)
                    if b is not None:
                        update(b)
                    if c is not None:
                        scores_out(c)

                layer_norm_dve(nc, dve, X, 0, s, ln)
                nc.vector.memset(QD[:, :, :], 0.0).then_inc(s_z, 1)
                pipelined_layers(dve, layers, steps)

            @block.scalar
            def _(act):
                def exps(b, t):
                    act.wait_ge(s_sub, b.n * TPC + t + 1)
                    nc.scalar.activation(S[:, t, :, :], S[:, t, :, :], ACT.Exp, scale=HD ** -0.5).then_inc(s_e, 1)

                def value_blocks(c):
                    act.wait_ge(s_v, c.n * TPC + TPC)
                    wait(act, s_pv, c.n * TPC)
                    v = V[:, :].rearrange("p (x f) -> p x f", f=PAIR)
                    for bb in range(BPT):
                        r = slice(bb * L, (bb + 1) * L)
                        nc.scalar.copy(VD[r, :, r], v[r]).then_inc(s_vd, 1)

                def query_blocks(c):
                    act.wait_ge(s_qt, c.n + 1)
                    wait(act, s_s, c.n * TPC)
                    for bb in range(BPT):
                        r = slice(bb * L, (bb + 1) * L)
                        nc.scalar.copy(QD[r, :, r], QT[r, :, :]).then_inc(s_qd, 1)

                def across(banks, count, value, dst, done, used=None, used_value=0):
                    act.wait_ge(count, value)
                    if used is not None:
                        wait(act, used, used_value)
                    for k in range(KT):
                        nc.scalar.copy(dst[:, k, :], banks[k][:, :]).then_inc(done, 1)

                def steps(c, b, n):
                    if b is not None:
                        for t in range(TPC):
                            exps(b, t)
                    if c is not None:
                        query_blocks(c)
                    if n is not None:
                        layer_norm_act(nc, act, X, XN, n.n, s, ln, s_xt, at=n.x)
                    if n is not None:
                        across(pB, s_xt, n.n + 1, XT, s_xte, s_vp, n.n * TPC)
                    if b is not None:
                        across(pA, s_tr, b.n + 1, OT, s_ot, s_y, b.n * TPC)
                    if c is not None:
                        value_blocks(c)

                layer_norm_act(nc, act, X, XN, 0, s, ln, s_xt)
                across(pB, s_xt, 1, XT, s_xte)
                act.wait_ge(s_z, 2)
                pipelined_layers(act, layers, steps)

            @block.gpsimd
            def _(pool):
                def shift(b):
                    for t in range(TPC):
                        pool.wait_ge(s_mx, b.n * TPC + t + 1)
                        nc.gpsimd.tensor_tensor(S[:, t, :, :], S[:, t, :, :], along(MX, t),
                                                ALU.subtract).then_inc(s_sub, 1)

                def normalise(b):
                    for t in range(TPC):
                        pool.wait_ge(s_rc, b.n * TPC + t + 1)
                        nc.gpsimd.tensor_tensor(S[:, t, :, :], S[:, t, :, :], along(RC, t),
                                                ALU.mult).then_inc(s_p, 1)

                def sin_products(c, kind, src, ready, order):
                    pool.wait_ge(ready, c.n * TPC + TPC)
                    wait(pool, s_r, (c.x - 1) * 2 + order + 1)
                    h = HD // 2
                    x = src[:, :].rearrange("p (x d) -> p x d", d=HD)
                    y = R2[kind][:, :].rearrange("p (x d) -> p x d", d=HD)
                    sin = g["sin"][:, :].unsqueeze(1).to_broadcast([P, TPC * NH, HD])
                    nc.gpsimd.tensor_tensor(y[:, :, 0:h], x[:, :, h:HD], sin[:, :, 0:h], ALU.mult).then_inc(s_r2, 1)
                    nc.gpsimd.tensor_tensor(y[:, :, h:HD], x[:, :, 0:h], sin[:, :, h:HD], ALU.mult).then_inc(s_r2, 1)

                def rotated(c, kind, order):
                    pool.wait_ge(s_r1, c.x * 2 + order + 1)
                    pool.wait_ge(s_r2, (c.x * 2 + order) * 2 + 2)
                    nc.gpsimd.tensor_tensor(R1[kind][:, :], R1[kind][:, :], R2[kind][:, :], ALU.add).then_inc(s_r, 1)

                def masked_keys(c):
                    pool.wait_ge(s_kt, c.n + 1)
                    wait(pool, s_s, c.n * TPC)
                    for e in range(2):
                        own = g["halves"][:, e:e + 1].unsqueeze(2).to_broadcast([P, TPC * NP, L])
                        nc.gpsimd.tensor_tensor(KM[:, :, e, :], KTt[:, :, :], own, ALU.mult).then_inc(s_km, 1)

                def add_bias(c):
                    c.starts_layer(lambda: pool.wait_ge(c.ly.s_w, c.ly.all_loaded))
                    for t in range(TPC):
                        pool.wait_ge(s["xn"], c.n * TPC + t + 1)
                        xt = X[:, bass.ds(c.x * TPC + t, 1), :].rearrange("p a d -> p (a d)")
                        nc.gpsimd.tensor_tensor(xt, xt, c.ly.w["bo"][:, :], ALU.add).then_inc(s_xb, 1)

                def steps(c, b, n):
                    if b is not None:
                        shift(b)
                    if c is not None and c.ly.rope:
                        sin_products(c, "q", Q, s_q, 0)
                        rotated(c, "q", 0)
                        sin_products(c, "k", K, s_k, 1)
                        rotated(c, "k", 1)
                    if b is not None and over_heads:
                        normalise(b)
                    if n is not None:
                        layer_norm_pool(nc, pool, n.n, s, ln)
                    if c is not None:
                        masked_keys(c)
                    if n is not None:
                        add_bias(n)

                layer_norm_pool(nc, pool, 0, s, ln)
                nc.gpsimd.memset(VD[:, :, :], 0.0).then_inc(s_z, 1)
                add_bias(Pass(layers[0], 0))
                pipelined_layers(pool, layers, steps)


NE0 = 32
H0 = D // 4
PAIRS = NE0 // 2


def routed_ffn0(nc, tag, X, g, dram):
    with ExitStack() as ctx:
        a = Scope(nc, ctx, tag)
        sb, ps, sem = a.sb, a.ps, a.sem
        W1 = sb("w1", [P, KT, NE0 * H0])
        W2 = sb("w2", [P, PAIRS, D])
        RW = sb("router_w", [P, KT, NE0])
        RB = sb("router_b", [P, NE0])
        B1 = sb("b1", [P, PAIRS])
        B2 = sb("b2", [NE0, D])
        SEL = sb("pair_select", [NE0, PAIRS * P])
        SELh = sb("pair_select_bf", [NE0, PAIRS * P], BF16)
        IOTA = sb("iota", [P, NE0])
        W1r = sb("w1_parts", [P, 2, KT, NE0 * H0], F32R)
        W2r = sb("w2_parts", [P, 2, PAIRS, D], F32R)
        XTr = sb("xt_parts", [P, 2, KT, TOK], F32R)
        OHall = sb("onehot_t", [NE0, TOK], BF16)
        B2S = sb("b2_selected", [P, TILES, D])
        s_w, s_wb, s_we = sem("router_loaded"), sem("select_ready"), sem("experts_loaded")
        s_wr, s_wl = sem("experts_rounded"), sem("experts_low_parts")
        loads = [(RW[:, :, :], dram["ffn0_rT"].rearrange("(k p) n -> p k n", p=P)),
                 (RB[:, :], dram["ffn0_rb"].partition_broadcast(P)),
                 (IOTA[:, :], dram["iota32"]), (SEL[:, :], dram["pair_select"]), (B2[:, :], dram["ffn0_b2"])]
        e_loads = [(B1[:, :], dram["ffn0_b1"].rearrange("(j p) -> p j", p=P)),
                   (W1[:, :, :], dram["ffn0_w1"].rearrange("(k p) n -> p k n", p=P)),
                   (W2[:, :, :], dram["ffn0_w2"].rearrange("(j p) n -> p j n", p=P))]
        NLD = 16 * len(loads)

        with ExitStack() as ctx2:
            a2 = Scope(nc, ctx2, tag + "r")
            XN = a2.sb("xn", [P, TPC, D])
            XT = a2.sb("xt", [P, KT, CH])
            LG = a2.sb("logits", [P, TPC, NE0])
            M8 = a2.sb("max8", [P, TPC, 8])
            I8 = a2.sb("idx8", [P, TPC, 8], U32)
            IF = a2.sb("idx", [P, TPC])
            OH = a2.sb("onehot", [P, TPC, NE0])
            OHT = a2.sb("onehot_t", [NE0, CH])
            ln = layer_norm_buffers(a2)
            ln["mhalf"] = g["mhalf"]
            s = layer_norm_semaphores(a2, g)
            s_xt, s_xte, s_xc = a2.sem("x_transposed"), a2.sem("xt_ready"), a2.sem("xt_rounded")
            s_xl = a2.sem("xt_low_parts")
            s_lg, s_l, s_m8, s_i8 = a2.sem("logits"), a2.sem("logits_out"), a2.sem("max8"), a2.sem("idx8")
            s_if, s_oh, s_oht, s_ohe = a2.sem("idx"), a2.sem("onehot"), a2.sem("onehot_t"), a2.sem("onehot_out")
            s_ohk = a2.sem("onehot_kept")
            s_b2, s_b2e = a2.sem("b2"), a2.sem("b2_out")
            pT = [a2.ps(f"pT{j}", [P, 512]) for j in range(KT)]
            pL = a2.ps("pL", [P, TPC, NE0])
            pH = a2.ps("pH", [NE0, 512])
            pB = [a2.ps(f"pB{j}", [P, 512]) for j in range(2)]
            with nc.Block() as block:
                @block.sync
                def _(sp):
                    with nc.allow_non_contiguous_dma(reason="biases onto partitions"):
                        for dst, src in loads:
                            sp.dma_start(dst, src).then_inc(s_w, 16)
                        for dst, src in e_loads:
                            sp.dma_start(dst, src).then_inc(s_we, 16)

                @block.tensor
                def _(pe):
                    def select_biases(b):
                        pe.wait_ge(s_oh, b * TPC + TPC)
                        wait(pe, s_ohe, b)
                        wait(pe, s_ohk, b)
                        for t in range(TPC):
                            mm = nc.tensor.transpose(pH[:, t * P:(t + 1) * P], OH[:, t, :], g["ident"][:, :])
                        mm.then_inc(s_oht, 1)
                        pe.wait_ge(s_ohe, b + 1)
                        wait(pe, s_b2e, b * TPC)
                        for t in range(TPC):
                            nc.tensor.matmul(pB[t // 2][:, (t % 2) * D:(t % 2) * D + D], OHT[:, t * P:(t + 1) * P],
                                             B2[:, :], start=True, stop=True).then_inc(s_b2, 1)

                    def turn(c):
                        wait(pe, s_xte, c * KT)
                        wait(pe, s_xc, c * KT)
                        for t in range(TPC):
                            pe.wait_ge(s["xn"], c * TPC + t + 1)
                            for k in range(KT):
                                mm = nc.tensor.transpose(pT[k][:, t * P:(t + 1) * P], XN[:, t, k * P:(k + 1) * P],
                                                         g["ident"][:, :])
                        mm.then_inc(s_xt, 1)

                    def logits(c):
                        pe.wait_ge(s_xte, c * KT + KT)
                        wait(pe, s_l, c)
                        for t in range(TPC):
                            for k in range(KT):
                                mm = nc.tensor.matmul(pL[:, t, :], XT[:, k, t * P:(t + 1) * P], RW[:, k, :],
                                                      start=(k == 0), stop=(k == KT - 1))
                        mm.then_inc(s_lg, 1)

                    def steps(c, b, n):
                        if c is not None:
                            turn(c)
                            logits(c)
                        if b is not None:
                            select_biases(b)

                    pe.wait_ge(s_w, NLD)
                    pipelined(pe, steps)

                @block.vector
                def _(dve):
                    def route(b):
                        dve.wait_ge(s_lg, b + 1)
                        nc.vector.tensor_tensor(LG[:, :, :], pL[:, :, :],
                                                RB[:, :].unsqueeze(1).to_broadcast([P, TPC, NE0]),
                                                ALU.add).then_inc(s_l, 1)
                        dve.wait_ge(s_l, b + 1)
                        take_wait(nc, g)
                        for t in range(TPC):
                            nc.vector.max(M8[:, t, :], LG[:, t, :]).then_inc(s_m8, 1)
                        dve.wait_ge(s_m8, b * TPC + TPC)
                        take_wait(nc, g)
                        for t in range(TPC):
                            nc.vector.max_index(I8[:, t, :], M8[:, t, :], LG[:, t, :]).then_inc(s_i8, 1)
                        dve.wait_ge(s_i8, b * TPC + TPC)
                        nc.vector.tensor_copy(IF[:, :], I8[:, :, 0]).then_inc(s_if, 1)
                        wait(dve, s_oht, b)
                        dve.wait_ge(s_if, b + 1)
                        for t in range(TPC):
                            nc.vector.tensor_scalar(OH[:, t, :], IOTA[:, :], IF[:, t:t + 1], None,
                                                    ALU.is_equal).then_inc(s_oh, 1)

                    def biases(b):
                        dve.wait_ge(s_oht, b + 1)
                        wait(dve, s_b2, b * TPC)
                        nc.vector.tensor_copy(OHT[:, :], pH[:, :]).then_inc(s_ohe, 1)
                        for t in range(TPC):
                            if t % 2 == 0:
                                dve.wait_ge(s_b2, b * TPC + t + 2)
                            dst = B2S[:, bass.ds(b * TPC + t, 1), :].rearrange("p a d -> p (a d)")
                            nc.vector.tensor_copy(dst, pB[t // 2][:, (t % 2) * D:(t % 2) * D + D]).then_inc(s_b2e, 1)

                    def transposed(c):
                        dve.wait_ge(s_xt, c + 1)
                        wait(dve, s_lg, c)
                        wait(dve, s_xl, c * KT)
                        wait(dve, s_xc, c * KT)
                        for k in range(KT):
                            nc.vector.tensor_copy(XT[:, k, :], pT[k][:, :]).then_inc(s_xte, 1)

                    def low_parts(c):
                        for k in range(KT):
                            dve.wait_ge(s_xc, c * KT + k + 1)
                            tok = bass.ds(c * CH, CH)
                            nc.vector.tensor_tensor(XTr[:, 1, k, tok], XT[:, k, :], XTr[:, 0, k, tok].bitcast(F32),
                                                    ALU.subtract).then_inc(s_xl, 1)

                    def steps(c, b, n):
                        if c is not None:
                            transposed(c)
                        if n is not None:
                            layer_norm_moments(nc, dve, X, n, s, ln)
                        if b is not None:
                            route(b)
                        if n is not None:
                            layer_norm_shift(nc, dve, n, s, ln)
                        if b is not None:
                            biases(b)
                        if c is not None:
                            low_parts(c)

                    layer_norm_dve(nc, dve, X, 0, s, ln)
                    dve.wait_ge(s_w, NLD)
                    nc.vector.tensor_copy(SELh[:, :], SEL[:, :]).then_inc(s_wb, 1)
                    pipelined(dve, steps)

                @block.scalar
                def _(act):
                    def steps(c, b, n):
                        if c is not None:
                            act.wait_ge(s_xte, c * KT + KT)
                            for k in range(KT):
                                nc.scalar.copy(XTr[:, 0, k, bass.ds(c * CH, CH)], XT[:, k, :]).then_inc(s_xc, 1)
                        if isinstance(c, int) and c == 1:
                            act.wait_ge(s_we, 16 * len(e_loads))
                            nc.scalar.copy(W1r[:, 0], W1[:, :, :]).then_inc(s_wr, 1)
                            nc.scalar.copy(W2r[:, 0], W2[:, :, :]).then_inc(s_wr, 1)
                        if b is not None:
                            act.wait_ge(s_ohe, b + 1)
                            nc.scalar.copy(OHall[:, bass.ds(b * CH, CH)], OHT[:, :]).then_inc(s_ohk, 1)
                        if n is not None:
                            layer_norm_act(nc, act, X, XN, n, s, ln, s_xt)

                    layer_norm_act(nc, act, X, XN, 0, s, ln, s_xt)
                    pipelined(act, steps)

                @block.gpsimd
                def _(pool):
                    def low_part(W, Wr, n):
                        pool.wait_ge(s_wr, n)
                        nc.gpsimd.tensor_tensor(Wr[:, 1], W[:, :, :], Wr[:, 0].bitcast(F32),
                                                ALU.subtract).then_inc(s_wl, 1)

                    for c in range(PASSES - 1):
                        layer_norm_pool(nc, pool, c, s, ln)
                    low_part(W1, W1r, 1)
                    layer_norm_pool(nc, pool, PASSES - 1, s, ln)
                    low_part(W2, W2r, 2)

        with ExitStack() as ctx3:
            a3 = Scope(nc, ctx3, tag + "e")
            HR = a3.sb("hidden", [P, 2, CH])
            HM = a3.sb("hidden_masked", [P, 2, CH])
            HMr = a3.sb("hidden_parts", [P, 2, 2, CH], F32R)
            Y = a3.sb("y", [P, TPC, D])
            s_h, s_hr, s_mk, s_hm = a3.sem("hidden"), a3.sem("hidden_out"), a3.sem("mask"), a3.sem("masked")
            s_hi, s_lo = a3.sem("hidden_hi"), a3.sem("hidden_lo")
            s_y2, s_y, s_x = a3.sem("pair_summed"), a3.sem("y_out"), a3.sem("x_updated")
            pH = [a3.ps(f"pH{j}", [P, 512]) for j in range(3)]
            pM = [a3.ps(f"pM{j}", [P, 512]) for j in range(3)]
            pY = [a3.ps(f"pY{j}", [P, 512]) for j in range(2)]
            PP = PAIRS

            def passes(eng, body):
                body(0)
                with eng.Fori(1, PASSES) as c:
                    body(c)

            with nc.Block() as block:
                @block.tensor
                def _(pe):
                    def hidden(c, p):
                        wait(pe, s_hr, c * PP + p - 2)
                        wait(pe, s_hm, c * PP + p - 2)
                        for k in range(KT):
                            for n, (x, y) in enumerate(PARTS):
                                mm = nc.tensor.matmul(pH[p % 3][:, :], W1r[:, x, k, p * P:(p + 1) * P],
                                                      XTr[:, y, k, bass.ds(c * CH, CH)], start=(k == 0 and n == 0),
                                                      stop=(k == KT - 1 and n == len(PARTS) - 1))
                        mm.then_inc(s_h, 1)
                        nc.tensor.matmul(pM[p % 3][:, :], SELh[:, p * P:(p + 1) * P], OHall[:, bass.ds(c * CH, CH)],
                                         start=True, stop=True).then_inc(s_mk, 1)

                    def out(c, p):
                        pe.wait_ge(s_lo, c * PP + p + 1)
                        if p == 0:
                            wait(pe, s_y, c * TPC)
                        for t in range(TPC):
                            for n, (x, y) in enumerate(PARTS):
                                mm = nc.tensor.matmul(pY[t // 2][:, (t % 2) * D:(t % 2) * D + D],
                                                      HMr[:, p % 2, x, t * P:(t + 1) * P], W2r[:, y, p, :],
                                                      start=(p == 0 and t % 2 == 0 and n == 0),
                                                      stop=(p == PP - 1 and n == len(PARTS) - 1),
                                                      skip_group_check=True)
                        mm.then_inc(s_y2, 1)

                    def body(c):
                        for p in range(PP):
                            hidden(c, p)
                            if p > 1:
                                out(c, p - 2)
                        out(c, PP - 2)
                        out(c, PP - 1)

                    passes(pe, body)

                @block.scalar
                def _(act):
                    def body(c):
                        for p in range(PP):
                            act.wait_ge(s_h, c * PP + p + 1)
                            wait(act, s_hm, c * PP + p - 1)
                            nc.scalar.activation(HR[:, p % 2, :], pH[p % 3][:, :], ACT.Relu,
                                                 bias=B1[:, p:p + 1]).then_inc(s_hr, 1)
                            if p > 0:
                                rounded(c, p - 1)
                        rounded(c, PP - 1)

                    def rounded(c, p):
                        act.wait_ge(s_hm, c * PP + p + 1)
                        wait(act, s_y2, c * PP + p - 1)
                        nc.scalar.copy(HMr[:, p % 2, 0, :], HM[:, p % 2, :]).then_inc(s_hi, 1)

                    passes(act, body)

                @block.vector
                def _(dve):
                    def body(c):
                        for p in range(PP):
                            dve.wait_ge(s_hr, c * PP + p + 1)
                            dve.wait_ge(s_mk, c * PP + p + 1)
                            wait(dve, s_hi, c * PP + p - 1)
                            wait(dve, s_lo, c * PP + p - 1)
                            nc.vector.tensor_tensor(HM[:, p % 2, :], pM[p % 3][:, :], HR[:, p % 2, :],
                                                    ALU.mult).then_inc(s_hm, 1)
                            if p > 0:
                                rest(c, p - 1)
                        rest(c, PP - 1)
                        dve.wait_ge(s_y2, c * PP + PP)
                        wait(dve, s_x, c * TPC)
                        for t in range(TPC):
                            bs = B2S[:, bass.ds(c * TPC + t, 1), :].rearrange("p a d -> p (a d)")
                            nc.vector.tensor_tensor(Y[:, t, :], pY[t // 2][:, (t % 2) * D:(t % 2) * D + D], bs,
                                                    ALU.add).then_inc(s_y, 1)
                        for t in range(TPC):
                            dve.wait_ge(s_y, c * TPC + t + 1)
                            xt = X[:, bass.ds(c * TPC + t, 1), :].rearrange("p a d -> p (a d)")
                            nc.vector.scalar_tensor_tensor(out=xt, in0=Y[:, t, :], scalar=0.0, in1=xt,
                                                           op0=ALU.max, op1=ALU.add).then_inc(s_x, 1)

                    def rest(c, p):
                        dve.wait_ge(s_hi, c * PP + p + 1)
                        wait(dve, s_y2, c * PP + p - 1)
                        nc.vector.tensor_tensor(HMr[:, p % 2, 1, :], HM[:, p % 2, :],
                                                HMr[:, p % 2, 0, :].bitcast(F32), ALU.subtract).then_inc(s_lo, 1)

                    passes(dve, body)


XW = 1024
XD = XW // NH
SK = 257
SK2 = SK + 1
XCH = 256
XTP = XCH // P
XPASSES = TOK // XCH
XB = XCH // L
ROWS = NH * L
RT4 = ROWS // P
FT = XW // P


def cross_attention(nc, tag, X, g, dram):
    with ExitStack() as ctx:
        a = Scope(nc, ctx, tag)
        sb, ps, sem = a.sb, a.ps, a.sem
        WQ = sb("wq", [P, KT, XW])
        WKr = sb("wk_parts", [P, 2, FT, D], F32R)
        WV = sb("wv", [P, KT, XW])
        WO = sb("wo", [P, FT, D])
        BQ = sb("bq", [P, FT])
        BV = sb("bv", [P, FT])
        BO = sb("bo", [P, D])
        XN = sb("xn", [P, XTP, D])
        XT = sb("xt", [P, KT, XCH])
        QTr = sb("qt_parts", [P, 2, FT, XCH], F32R)
        Gr = sb("queries_to_context", [P, 2, KT, XB, ROWS], F32R)
        CT = sb("ctx_t", [P, KT, SK])
        CTr = sb("ctx_t_parts", [P, 2, 2, KT, SK2], F32R)
        CX = sb("ctx", [P, KT, D])
        CXr = sb("ctx_parts", [P, 2, 2, KT, D], F32R)
        CL = sb("ctx_last", [3, D])
        CLh = sb("ctx_last_hi", [3, D], F32R)
        CLs = sb("ctx_last_stack", [3, 2, D], F32R)
        zeros = sb("zeros", [3, D])
        LM = sb("stack_masks", [3, 2])
        PR = sb("probs", [P, 2 * RT4 * SK])
        PC = sb("probs_last_parts", [P, RT4, 4], F32R)
        NM = sb("neg_max", [P, 2, RT4])
        SM = sb("sums", [P, 2, RT4])
        RC = sb("recips", [P, 2, RT4])
        PL = sb("probs_last", [4, ROWS], F32R)
        MX = sb("mixed_context", [P, KT, NH, XCH])
        IDr = sb("ident_r", [P, P], F32R)
        PRv = PR[:, :].rearrange("p (i t s) -> p i t s", i=2, t=RT4)
        OT = PR[:, 0:FT * XCH].rearrange("p (f t) -> p f t", f=FT)
        PTr = QTr[:, :, 0:KT * ROWS // XCH, :].rearrange("p i f t -> p i (f t)").rearrange(
            "p i (k r) -> p i k r", k=KT)
        WK = MX[:, 0, :, :].rearrange("p h t -> p (h t)")[:, 0:FT * D].rearrange("p (f d) -> p f d", f=FT)
        ln = layer_norm_buffers(a)
        ln["mhalf"] = g["mhalf"]
        s = layer_norm_semaphores(a, g)
        s_wq, s_wk0, s_w, s_wk = sem("wq_loaded"), sem("wk_loaded"), sem("weights_loaded"), sem("wk_split")
        s_ct, s_cx, s_cl = sem("ctx_t_loaded"), sem("ctx_loaded"), sem("ctx_last_loaded")
        s_cts, s_cxs, s_cls, s_pz = sem("ctx_t_split"), sem("ctx_split"), sem("ctx_last_split"), sem("pads_zeroed")
        s_xt, s_xte = sem("x_transposed"), sem("xt_ready")
        s_qp, s_q, s_ql = sem("q_projected"), sem("q_hi"), sem("q_lo")
        s_gp, s_gh, s_gl = sem("g_projected"), sem("g_hi"), sem("g_lo")
        s_s, s_nm, s_e = sem("scores"), sem("row_max"), sem("exps")
        s_rc, s_p, s_pc = sem("recips"), sem("probs"), sem("probs_last")
        s_t, s_tl = sem("probs_transposed"), sem("last_transposed")
        s_ph, s_plo, s_pl = sem("pt_hi"), sem("pt_lo"), sem("pt_last")
        s_m, s_ma, s_md = sem("mixed"), sem("mix0_ready"), sem("mix1_ready")
        s_o, s_oe = sem("heads_projected"), sem("heads_ready")
        s_y, s_xb, s_x = sem("out_projected"), sem("bias_added"), sem("x_updated")
        pS = [ps(f"pS{j}", [P, 512]) for j in range(RT4)]
        pA = [ps(f"pA{j}", [P, 512]) for j in range(2)]
        pM = [ps(f"pM{j}", [P, 512]) for j in range(2)]
        last_g = [max((t + 1) * NH // RT4 - 1, max(h for h in range(NH) if (h + FT) % 6 == 2 + t)) for t in range(RT4)]
        gbank = [pA[0], pA[1]] + pS
        q_loads = [(WQ[:, :, :], dram["L1x_qT"].rearrange("(k p) n -> p k n", p=P)),
                   (BQ[:, :], dram["L1x_bq"].rearrange("(k p) -> p k", p=P))]
        k_loads = [(WK, dram["L1x_k"].rearrange("(k p) n -> p k n", p=P))]
        loads = [(WV[:, :, :], dram["L1x_vT"].rearrange("(k p) n -> p k n", p=P)),
                 (WO[:, :, :], dram["L1x_oT"].rearrange("(k p) n -> p k n", p=P)),
                 (BV[:, :], dram["L1x_bv"].rearrange("(k p) -> p k", p=P)),
                 (BO[:, :], dram["L1x_bo"].partition_broadcast(P)),
                 (LM[:, :], dram["stack_masks"])]
        NLD = 16 * len(loads)
        AHEAD = XB // 2

        def passes(eng, body):
            body(0, 1)
            with eng.Fori(1, XPASSES - 1) as c:
                body(c, c + 1)
            body(XPASSES - 1, None)

        with nc.Block() as block:
            @block.sync
            def _(sp):
                def body(c, nxt):
                    for b in range(XB):
                        gb = c * XB + b
                        wait(sp, s_cts, gb * 2)
                        sp.dma_start(CT[:, :, :], dram["ctxT"].rearrange("b (k p) s -> b p k s", p=P)
                                     [bass.ds(gb, 1)].rearrange("a p k s -> p (a k) s")).then_inc(s_ct, 16)
                        wait(sp, s_cxs, gb * 2)
                        rows = dram["ctx"][bass.ds(gb, 1)]
                        sp.dma_start(CX[:, :, :], rows[:, 0:KT * P, :].rearrange("a (k p) d -> p (a k) d", p=P)
                                     ).then_inc(s_cx, 16)
                        wait(sp, s_cls, gb * 5)
                        row = dram["ctx_last"][bass.ds(gb, 1), :].partition_broadcast(3).rearrange("q a n -> q (a n)")
                        sp.dma_start(CL[:, :], row).then_inc(s_cl, 16)

                with nc.allow_non_contiguous_dma(reason="biases onto partitions"):
                    for dst, src in q_loads:
                        sp.dma_start(dst, src).then_inc(s_wq, 16)
                    for dst, src in loads:
                        sp.dma_start(dst, src).then_inc(s_w, 16)
                passes(sp, body)

            @block.tensor
            def _(pe):
                def parts(out, lhs, rhs, first=True, last=True):
                    for n, (x, y) in enumerate(PARTS):
                        mm = nc.tensor.matmul(out, lhs(x), rhs(y), start=(first and n == 0),
                                              stop=(last and n == len(PARTS) - 1))
                    return mm

                def turn_x(c):
                    wait(pe, s_e, c * XB * RT4)
                    for t in range(XTP):
                        pe.wait_ge(s["xn"], c * XTP + t + 1)
                        for k in range(KT):
                            mm = nc.tensor.transpose(pS[k][:, t * P:(t + 1) * P], XN[:, t, k * P:(k + 1) * P],
                                                     g["ident"][:, :])
                    mm.then_inc(s_xt, 1)

                def queries(c):
                    wait(pe, s_oe, c * FT)
                    pe.wait_ge(s_xte, c * KT + KT)
                    for f in range(FT):
                        if f >= 6:
                            pe.wait_ge(s_ql, c * FT + f - 5)
                        for k in range(KT):
                            mm = nc.tensor.matmul(gbank[f % 6][:, 0:XCH], WQ[:, k, f * P:(f + 1) * P], XT[:, k, :],
                                                  start=(k == 0), stop=(k == KT - 1))
                        mm.then_inc(s_qp, 1)
                    if is_first(c):
                        pe.wait_ge(s_wk, 2)
                    for h in range(NH):
                        r = slice(64 * (h % 2), 64 * (h % 2) + 64)
                        need = max(h // 2 + 1, min(h + FT - 6, FT - 1) + 1 if h < 6 else 0)
                        pe.wait_ge(s_ql, c * FT + min(need, FT))
                        if h >= 6:
                            pe.wait_ge(s_gl, c * NH + h - 5)
                        for m in range(KT):
                            mm = parts(gbank[(h + FT) % 6][:, m * XCH:(m + 1) * XCH],
                                       lambda x: WKr[r, x, h // 2, m * P:(m + 1) * P],
                                       lambda y: QTr[r, y, h // 2, :])
                        mm.then_inc(s_gp, 1)

                def scores(c, b):
                    gb, i = c * XB + b, b % 2
                    pe.wait_ge(s_cts, gb * 2 + 2)
                    for t in range(RT4):
                        if b == 0:
                            pe.wait_ge(s_gl, c * NH + last_g[t] + 1)
                        wait(pe, s_e, (gb - 1) * RT4 + t + 1)
                        if t == RT4 - 1 and b > 0:
                            pe.wait_ge(s_pl, gb)
                        for k in range(KT):
                            mm = parts(pS[t][:, 0:SK2], lambda x: Gr[:, x, k, b, t * P:(t + 1) * P],
                                       lambda y: CTr[:, i, y, k, :], k == 0, k == KT - 1)
                        mm.then_inc(s_s, 1)

                def turn(c, b):
                    gb, i = c * XB + b, b % 2
                    wait(pe, s_plo, gb * KT)
                    for k in range(KT):
                        for t in range(RT4):
                            if k == 0:
                                pe.wait_ge(s_p, gb * RT4 + t + 1)
                            mm = nc.tensor.transpose(pA[k][:, t * P:(t + 1) * P], PRv[:, i, t, k * P:(k + 1) * P],
                                                     g["ident"][:, :])
                        mm.then_inc(s_t, 1)
                    pe.wait_ge(s_pc, gb * 3 + 3)
                    for t in range(RT4):
                        mm = nc.tensor.transpose(pS[-1][0:4, t * P:(t + 1) * P].bitcast(F32R), PC[:, t, :],
                                                 IDr[:, :])
                    mm.then_inc(s_tl, 1)

                def mix(c, b):
                    gb, i = c * XB + b, b % 2
                    pe.wait_ge(s_cxs, gb * 2 + 2)
                    pe.wait_ge(s_cls, gb * 5 + 5)
                    wait(pe, s_ma, gb)
                    wait(pe, s_md, gb)
                    if b == 0:
                        wait(pe, s_x, c * XTP)
                    pe.wait_ge(s_pl, gb + 1)
                    for m in range(KT):
                        nc.tensor.matmul(pM[m][:, :], CLs[0:3, i, m * P:(m + 1) * P], PL[0:3, :],
                                         start=True, stop=False)
                    for k in range(KT):
                        pe.wait_ge(s_plo, gb * KT + k + 1)
                        for m in range(KT):
                            mm = parts(pM[m][:, :], lambda x: CXr[:, i, x, k, m * P:(m + 1) * P],
                                       lambda y: PTr[:, y, k, :], False, k == KT - 1)
                    mm.then_inc(s_m, 1)

                def outputs(c):
                    if is_first(c):
                        pe.wait_ge(s_w, NLD)
                    pe.wait_ge(s_ma, c * XB + XB)
                    pe.wait_ge(s_md, c * XB + XB)
                    for f in range(FT):
                        if f >= 2:
                            pe.wait_ge(s_oe, c * FT + f - 1)
                        for e in range(2):
                            h = 2 * f + e
                            for k in range(KT):
                                mm = nc.tensor.matmul(pA[f % 2][64 * e:64 * e + 64, 0:XCH],
                                                      WV[:, k, h * XD:(h + 1) * XD], MX[:, k, h, :],
                                                      start=(k == 0), stop=(k == KT - 1))
                        mm.then_inc(s_o, 1)
                    for t in range(XTP):
                        for f in range(FT):
                            if t == 0:
                                pe.wait_ge(s_oe, c * FT + f + 1)
                            mm = nc.tensor.matmul(pM[t][:, 0:D], OT[:, f, t * P:(t + 1) * P], WO[:, f, :],
                                                  start=(f == 0), stop=(f == FT - 1))
                        mm.then_inc(s_y, 1)

                def body(c, nxt):
                    queries(c)
                    scores(c, 0)
                    turn(c, 0)
                    for b in range(XB):
                        if b + 1 < XB:
                            scores(c, b + 1)
                        elif nxt is not None:
                            turn_x(nxt)
                        mix(c, b)
                        if b + 1 < XB:
                            turn(c, b + 1)
                    outputs(c)

                pe.wait_ge(s_wq, 16 * len(q_loads))
                pe.wait_ge(s_pz, 4)
                turn_x(0)
                passes(pe, body)

            @block.vector
            def _(dve):
                def take_x(c):
                    dve.wait_ge(s_xt, c + 1)
                    wait(dve, s_qp, c * FT)
                    for k in range(KT):
                        nc.vector.tensor_copy(XT[:, k, :], pS[k][:, 0:XCH]).then_inc(s_xte, 1)

                def body(c, nxt):
                    for f in range(FT):
                        dve.wait_ge(s_q, c * FT + f + 1)
                        nc.vector.scalar_tensor_tensor(
                            out=QTr[:, 1, f, :], in0=gbank[f % 6][:, 0:XCH], scalar=BQ[:, f:f + 1],
                            in1=QTr[:, 0, f, :].bitcast(F32), op0=ALU.add, op1=ALU.subtract).then_inc(s_ql, 1)
                    if is_first(c):
                        dve.wait_ge(s_wk, 1)
                        nc.vector.tensor_tensor(WKr[:, 1, :, :], WK, WKr[:, 0, :, :].bitcast(F32), ALU.subtract
                                                ).then_inc(s_wk, 1)
                    for h in range(NH):
                        dve.wait_ge(s_gh, c * NH + h + 1)
                        for m in range(KT):
                            src = gbank[(h + FT) % 6][:, m * XCH:(m + 1) * XCH].rearrange("p (b q) -> p b q", q=L)
                            ins = nc.vector.scalar_tensor_tensor(
                                out=Gr[:, 1, m, :, h * L:(h + 1) * L], in0=src, scalar=XD ** -0.5,
                                in1=Gr[:, 0, m, :, h * L:(h + 1) * L].bitcast(F32),
                                op0=ALU.mult, op1=ALU.subtract)
                        ins.then_inc(s_gl, 1)
                    row_maxima(c, 0)
                    probabilities(c, 0)
                    for b in range(XB):
                        across(c, b)
                        if nxt is not None and b == AHEAD - 2:
                            layer_norm_moments(nc, dve, X, nxt, s, ln, XTP)
                        if b + 1 < XB:
                            row_maxima(c, b + 1)
                            probabilities(c, b + 1)
                        if nxt is not None and b == AHEAD:
                            layer_norm_shift(nc, dve, nxt, s, ln, XTP)
                        gb = c * XB + b
                        dve.wait_ge(s_m, gb + 1)
                        nc.vector.tensor_copy(MX[:, 1, :, b * L:(b + 1) * L],
                                              pM[1][:, :].rearrange("p (h q) -> p h q", q=L)).then_inc(s_md, 1)
                    if nxt is not None:
                        take_x(nxt)
                    for t in range(XTP):
                        dve.wait_ge(s_y, c * XTP + t + 1)
                        dve.wait_ge(s_xb, c * XTP + t + 1)
                        xt = X[:, bass.ds(c * XTP + t, 1), :].rearrange("p a d -> p (a d)")
                        nc.vector.tensor_tensor(xt, pM[t][:, 0:D], xt, ALU.add).then_inc(s_x, 1)

                def row_maxima(c, b):
                    gb, i = c * XB + b, b % 2
                    for t in range(RT4):
                        dve.wait_ge(s_s, gb * RT4 + t + 1)
                        nc.vector.tensor_reduce(NM[:, i, t:t + 1], pS[t][:, 0:SK], AX.X, ALU.max,
                                                negate=True).then_inc(s_nm, 1)

                def across(c, b):
                    gb, i = c * XB + b, b % 2
                    for k in range(KT):
                        dve.wait_ge(s_ph, gb * KT + k + 1)
                        nc.vector.tensor_tensor(PTr[:, 1, k, :], pA[k][:, :], PTr[:, 0, k, :].bitcast(F32),
                                                ALU.subtract).then_inc(s_plo, 1)
                        if k == 0:
                            dve.wait_ge(s_tl, gb + 1)
                            nc.vector.tensor_copy(PL[0:3, :], pS[-1][0:3, :]).then_inc(s_pl, 1)

                def probabilities(c, b):
                    gb, i = c * XB + b, b % 2
                    dve.wait_ge(s_e, gb * RT4 + RT4)
                    nc.vector.reciprocal(RC[:, i, :], SM[:, i, :]).then_inc(s_rc, 1)
                    dve.wait_ge(s_rc, gb + 1)
                    for t in range(RT4):
                        nc.vector.tensor_scalar(PRv[:, i, t, :], PRv[:, i, t, :], RC[:, i, t:t + 1], None,
                                                ALU.mult).then_inc(s_p, 1)
                    dve.wait_ge(s_p, gb * RT4 + RT4)
                    last = PRv[:, i, :, KT * P]
                    nc.vector.tensor_copy(PC[:, :, 0], last).then_inc(s_pc, 1)
                    nc.vector.tensor_copy(PC[:, :, 2], last).then_inc(s_pc, 1)
                    dve.wait_ge(s_pc, gb * 3 + 2)
                    nc.vector.tensor_tensor(PC[:, :, 1], last, PC[:, :, 0].bitcast(F32), ALU.subtract).then_inc(s_pc, 1)

                layer_norm_dve(nc, dve, X, 0, s, ln, XTP)
                nc.vector.memset(CTr[:, :, :, :, SK:SK2].bitcast(F32), 0.0).then_inc(s_pz, 1)
                nc.vector.memset(zeros[:, :], 0.0).then_inc(s_pz, 1)
                nc.vector.memset(PC[:, :, 3:4].bitcast(F32), 0.0).then_inc(s_pz, 1)
                nc.vector.tensor_copy(IDr[:, :], g["ident"][:, :]).then_inc(s_pz, 1)
                dve.wait_ge(s_wq, 16 * len(q_loads))
                take_x(0)
                passes(dve, body)

            @block.scalar
            def _(act):
                def body(c, nxt):
                    for f in range(FT):
                        act.wait_ge(s_qp, c * FT + f + 1)
                        wait(act, s_gp, c * NH)
                        nc.scalar.activation(QTr[:, 0, f, :], gbank[f % 6][:, 0:XCH], ACT.Identity,
                                             bias=BQ[:, f:f + 1]).then_inc(s_q, 1)
                    if is_first(c):
                        act.wait_ge(s_wk0, 16)
                        nc.scalar.copy(WKr[:, 0, :, :], WK).then_inc(s_wk, 1)
                    for h in range(NH):
                        act.wait_ge(s_gp, c * NH + h + 1)
                        nc.scalar.activation(Gr[:, 0, :, :, h * L:(h + 1) * L],
                                             gbank[(h + FT) % 6][:, :].rearrange("p (m b q) -> p m b q", m=KT, q=L),
                                             ACT.Copy, scale=XD ** -0.5).then_inc(s_gh, 1)
                    exps(c, 0)
                    for b in range(XB):
                        gb, i = c * XB + b, b % 2
                        ahead = nxt is not None or b + 2 < XB
                        for k in range(KT):
                            act.wait_ge(s_t, gb * KT + k + 1)
                            wait(act, s_m, gb)
                            nc.scalar.copy(PTr[:, 0, k, :], pA[k][:, :]).then_inc(s_ph, 1)
                        if b + 1 < XB:
                            exps(c, b + 1)
                        if ahead:
                            round_ctx_t(gb + 2, i)
                        act.wait_ge(s_m, gb + 1)
                        nc.scalar.copy(MX[:, 0, :, b * L:(b + 1) * L],
                                       pM[0][:, :].rearrange("p (h q) -> p h q", q=L)).then_inc(s_ma, 1)
                        if ahead:
                            round_ctx(gb + 2, i)
                        if b == AHEAD and nxt is not None:
                            layer_norm_act(nc, act, X, XN, nxt, s, ln, s_xt, XTP)
                    if is_first(c):
                        act.wait_ge(s_w, NLD)
                    for f in range(FT):
                        act.wait_ge(s_o, c * FT + f + 1)
                        nc.scalar.activation(OT[:, f, :], pA[f % 2][:, 0:XCH], ACT.Identity,
                                             bias=BV[:, f:f + 1]).then_inc(s_oe, 1)

                def round_ctx_t(gb, i):
                    act.wait_ge(s_ct, gb * 16 + 16)
                    wait(act, s_s, (gb - 1) * RT4 - RT4)
                    nc.scalar.copy(CTr[:, i, 0, :, 0:SK], CT[:, :, :]).then_inc(s_cts, 1)

                def round_ctx(gb, i):
                    act.wait_ge(s_cx, gb * 16 + 16)
                    wait(act, s_m, gb - 1)
                    nc.scalar.copy(CXr[:, i, 0], CX[:, :, :]).then_inc(s_cxs, 1)

                def exps(c, b):
                    gb, i = c * XB + b, b % 2
                    wait(act, s_t, (gb - 1) * KT)
                    wait(act, s_tl, gb - 1)
                    wait(act, s_rc, gb - 1)
                    if b == 0:
                        wait(act, s_y, c * XTP)
                    for t in range(RT4):
                        act.wait_ge(s_nm, gb * RT4 + t + 1)
                        nc.scalar.activation(PRv[:, i, t, :], pS[t][:, 0:SK], ACT.Exp, bias=NM[:, i, t:t + 1],
                                             accum_out=SM[:, i, t:t + 1]).then_inc(s_e, 1)

                for dst, src in k_loads:
                    act.dma_start(dst, src).then_inc(s_wk0, 16)
                layer_norm_act(nc, act, X, XN, 0, s, ln, s_xt, XTP)
                act.wait_ge(s_pz, 1)
                for gb in range(2):
                    round_ctx_t(gb, gb)
                    round_ctx(gb, gb)
                act.wait_ge(s_wq, 16 * len(q_loads))
                passes(act, body)

            @block.gpsimd
            def _(pool):
                def body(c, nxt):
                    for b in range(XB):
                        gb, i = c * XB + b, b % 2
                        for src, dst, split in ((CT[:, :, :], CTr[:, i, :, :, 0:SK], s_cts),
                                                (CX[:, :, :], CXr[:, i], s_cxs)):
                            pool.wait_ge(split, gb * 2 + 1)
                            nc.gpsimd.tensor_tensor(dst[:, 1], src, dst[:, 0].bitcast(F32),
                                                    ALU.subtract).then_inc(split, 1)
                        last_rows(gb, i)
                        if nxt is not None and b == AHEAD:
                            layer_norm_pool(nc, pool, nxt, s, ln, XTP)
                        if nxt is not None and b == AHEAD + 2:
                            add_bias(nxt)

                def last_rows(gb, i):
                    pool.wait_ge(s_cl, gb * 16 + 16)
                    nc.gpsimd.tensor_tensor(CLh[:, :], CL[:, :], zeros[:, :], ALU.add).then_inc(s_cls, 1)
                    pool.wait_ge(s_cls, gb * 5 + 1)
                    nc.gpsimd.tensor_tensor(CL[:, :], CL[:, :], CLh[:, :].bitcast(F32), ALU.subtract).then_inc(s_cls, 1)
                    pool.wait_ge(s_cls, gb * 5 + 2)
                    nc.gpsimd.tensor_tensor(CL[:, :], CL[:, :], LM[:, 1:2].to_broadcast([3, D]), ALU.mult
                                            ).then_inc(s_cls, 1)
                    nc.gpsimd.tensor_tensor(CLh[:, :], CLh[:, :].bitcast(F32), LM[:, 0:1].to_broadcast([3, D]),
                                            ALU.mult).then_inc(s_cls, 1)
                    pool.wait_ge(s_cls, gb * 5 + 4)
                    wait(pool, s_m, gb - 1)
                    nc.gpsimd.tensor_tensor(CLs[:, i, :], CL[:, :], CLh[:, :].bitcast(F32), ALU.add
                                            ).then_inc(s_cls, 1)

                def add_bias(c):
                    for t in range(XTP):
                        pool.wait_ge(s["xn"], c * XTP + t + 1)
                        xt = X[:, bass.ds(c * XTP + t, 1), :].rearrange("p a d -> p (a d)")
                        nc.gpsimd.tensor_tensor(xt, xt, BO[:, :], ALU.add).then_inc(s_xb, 1)

                layer_norm_pool(nc, pool, 0, s, ln, XTP)
                pool.wait_ge(s_w, NLD)
                for t in range(XTP):
                    pool.wait_ge(s["xn"], t + 1)
                    nc.gpsimd.tensor_tensor(X[:, t, :], X[:, t, :], BO[:, :], ALU.add).then_inc(s_xb, 1)
                pool.wait_ge(s_pz, 2)
                passes(pool, body)


NE1 = 8
F1 = 1024
FT1 = F1 // P
TOP = 2
SLOT_TILES = (TOP * TOK + NE1 * (P - 1)) // P
SLOTS = SLOT_TILES * P


def routed_ffn1(nc, tag, X, g, dram, out):
    with ExitStack() as ctx:
        a = Scope(nc, ctx, tag)
        sb, ps, sem = a.sb, a.ps, a.sem
        GU, WE = KT * 2 * F1, KT * 2 * F1 + FT1 * D
        W = sb("w_experts", [P, NE1 * WE])
        carve = Carve(W[:, (NE1 - 1) * WE:NE1 * WE])
        POS = sb("slots", [P, TOP, TILES], U32)
        WT = sb("weights", [P, TOP, TILES])
        E32 = sb("tile_expert", [1, SLOT_TILES], U32)
        x_mid = nc.dram_tensor("x_mid", (TOK, D), F32, kind="Internal").ap()
        xs = nc.dram_tensor("x_slots", (SLOTS, D), F32, kind="Internal").ap()
        ys = nc.dram_tensor("y_slots", (SLOTS, D), F32, kind="Internal").ap()
        s_we = sem("experts_loaded")
        NWE = 16 * 2 * NE1
        s_sc = sem("rows_scattered")

        def load_expert(sp, e):
            gu = W[:, e * WE:e * WE + GU].rearrange("p (k n) -> p k n", k=KT)
            dn = W[:, e * WE + GU:(e + 1) * WE].rearrange("p (f n) -> p f n", f=FT1)
            sp.dma_start(gu, dram["ffn1_gu"][e].rearrange("(k p) n -> p k n", p=P)).then_inc(s_we, 16)
            sp.dma_start(dn, dram["ffn1_d"][e].rearrange("(f p) n -> p f n", p=P)).then_inc(s_we, 16)

        with ExitStack() as ctx2:
            a2 = Scope(nc, ctx2, tag + "r")
            RW = carve.sb("router_w", [P, KT, NE1])
            TRI = carve.sb("before", [P, P])
            IOTA = carve.sb("iota", [P, NE1])
            LG = carve.sb("logits", [P, TILES, NE1])
            s_w, s_mid, s_zf = a2.sem("weights_loaded"), a2.sem("x_stored"), a2.sem("slots_zeroed")
            with ExitStack() as ctx3:
                a3 = Scope(nc, ctx3, tag + "l")
                XN = carve.sb("xn", [P, TPC, D])
                XT = carve.sb("xt", [P, KT, CH])
                ln = layer_norm_buffers(carve)
                ln["mhalf"] = g["mhalf"]
                s = layer_norm_semaphores(a3, g)
                s_z = a3.sem("zeros")
                s_xt, s_xte, s_xk = a3.sem("x_transposed"), a3.sem("xt_ready"), a3.sem("xn_kept")
                s_lg, s_l = a3.sem("logits"), a3.sem("logits_out")
                ZR = carve.sb("zeros", [P, D])
                pT = [a3.ps(f"pT{j}", [P, 512]) for j in range(KT)]
                pL = a3.ps("pL", [P, TPC, NE1])
                with nc.Block() as block:
                    @block.sync
                    def _(sp):
                        sp.dma_start(RW[:, :, :], dram["ffn1_rT"].rearrange("(k p) n -> p k n", p=P)).then_inc(s_w, 16)
                        sp.dma_start(TRI[:, :], dram["before"]).then_inc(s_w, 16)
                        sp.dma_start(IOTA[:, :], dram["iota32"][:, 0:NE1]).then_inc(s_w, 16)
                        sp.dma_start(x_mid.rearrange("(t p) d -> p t d", p=P), X[:, :, :]).then_inc(s_mid, 16)
                        sp.wait_ge(s_z, 1)
                        sp.dma_start(xs.rearrange("(t p) d -> p t d", p=P),
                                     ZR[:, :].unsqueeze(1).to_broadcast([P, SLOT_TILES, D])).then_inc(s_zf, 16)
                        for e in range(NE1 - 1):
                            load_expert(sp, e)
                        sp.wait_ge(s_zf, 16)
                        sp.wait_ge(s_mid, 16)

                    @block.tensor
                    def _(pe):
                        def body(c):
                            wait(pe, s_xte, c * KT)
                            for t in range(TPC):
                                pe.wait_ge(s["xn"], c * TPC + t + 1)
                                for k in range(KT):
                                    mm = nc.tensor.transpose(pT[k][:, t * P:(t + 1) * P],
                                                             XN[:, t, k * P:(k + 1) * P], g["ident"][:, :])
                            mm.then_inc(s_xt, 1)
                            pe.wait_ge(s_xte, c * KT + KT)
                            wait(pe, s_l, c)
                            for t in range(TPC):
                                for k in range(KT):
                                    mm = nc.tensor.matmul(pL[:, t, :], XT[:, k, t * P:(t + 1) * P], RW[:, k, :],
                                                          start=(k == 0), stop=(k == KT - 1))
                            mm.then_inc(s_lg, 1)

                        pe.wait_ge(s_w, 48)
                        first_then_loop(pe, PASSES, body)

                    @block.vector
                    def _(dve):
                        def body(c):
                            layer_norm_dve(nc, dve, X, c, s, ln)
                            if not isinstance(c, int):
                                logits_out(c - 1)
                            dve.wait_ge(s_xt, c + 1)
                            wait(dve, s_lg, c)
                            for k in range(KT):
                                nc.vector.tensor_copy(XT[:, k, :], pT[k][:, :]).then_inc(s_xte, 1)

                        def logits_out(c):
                            dve.wait_ge(s_lg, c + 1)
                            nc.vector.tensor_copy(LG[:, bass.ds(c * TPC, TPC), :], pL[:, :, :]).then_inc(s_l, 1)

                        nc.vector.memset(ZR[:, :], 0.0).then_inc(s_z, 1)
                        first_then_loop(dve, PASSES, body)
                        logits_out(PASSES - 1)

                    @block.scalar
                    def _(act):
                        def body(c):
                            wait(act, s_xk, c * TPC)
                            layer_norm_act(nc, act, X, XN, c, s, ln, s_xt)

                        first_then_loop(act, PASSES, body)

                    @block.gpsimd
                    def _(pool):
                        def body(c):
                            layer_norm_pool(nc, pool, c, s, ln)
                            if is_first(c):
                                pool.wait_ge(s_mid, 16)
                            for t in range(TPC):
                                pool.wait_ge(s["xn"], c * TPC + t + 1)
                                xt = X[:, bass.ds(c * TPC + t, 1), :].rearrange("p a d -> p (a d)")
                                nc.gpsimd.tensor_copy(xt, XN[:, t, :]).then_inc(s_xk, 1)

                        first_then_loop(pool, PASSES, body)

            M8 = carve.sb("max8", [P, TILES, 8])
            I8 = carve.sb("idx8", [P, TILES, 8], U32)
            IX = carve.sb("idx", [P, TILES, TOP])
            OH = carve.sb("onehots", [P, TOP, TILES, NE1])
            CN = carve.sb("chosen", [P, TILES, NE1])
            CP = carve.sb("counted", [P, TILES + 1, NE1])
            NG = carve.sb("more_than", [P, NE1, TILES])
            TH = carve.sb("thresholds", [P, TILES])
            NT = carve.sb("tiles_of", [P, NE1])
            TB = carve.sb("first_tile", [P, NE1 + 1])
            BS = carve.sb("first_slot", [P, TILES, NE1])
            SL = carve.sb("slot_of", [P, TILES, NE1])
            SX = carve.sb("slot_masked", [P, TOP, TILES, NE1])
            PF = carve.sb("slot_f", [P, TOP, TILES])
            EX = carve.sb("exp2", [P, TILES])
            E1 = carve.sb("exp_sum", [P, TILES])
            DF = carve.sb("diff", [P, TILES])
            GE = carve.sb("tile_past", [1, NE1 - 1, SLOT_TILES])
            EF = carve.sb("tile_expert_f", [1, SLOT_TILES])
            ONE = carve.sb("ones", [P, P])
            s_m8, s_i8, s_oh, s_cn = a2.sem("max8"), a2.sem("idx8"), a2.sem("onehots"), a2.sem("chosen")
            s_rk, s_st, s_df, s_ex = a2.sem("ranks"), a2.sem("step"), a2.sem("diff"), a2.sem("exp2")
            s_pos, s_e = a2.sem("slots_known"), a2.sem("experts_known")
            pR = a2.ps("pR", [P, TILES, NE1])
            pC = a2.ps("pC", [P, TILES, NE1])
            with nc.Block() as block:
                @block.vector
                def _(dve):
                    count = [0]

                    def step(ins):
                        count[0] += 1
                        ins.then_inc(s_st, 1)
                        dve.wait_ge(s_st, count[0])

                    nc.vector.memset(ONE[:, :], 1.0)
                    for t in range(TILES):
                        ins = nc.vector.max(M8[:, t, :], LG[:, t, :])
                    step(ins)
                    for t in range(TILES):
                        ins = nc.vector.max_index(I8[:, t, :], M8[:, t, :], LG[:, t, :])
                    step(ins)
                    nc.vector.tensor_tensor(DF[:, :], M8[:, :, 1], M8[:, :, 0], ALU.subtract).then_inc(s_df, 1)
                    step(nc.vector.tensor_copy(IX[:, :, :], I8[:, :, 0:TOP]))
                    for i in range(TOP):
                        ins = nc.vector.tensor_tensor(OH[:, i, :, :],
                                                      IOTA[:, :].unsqueeze(1).to_broadcast([P, TILES, NE1]),
                                                      IX[:, :, i].unsqueeze(2).to_broadcast([P, TILES, NE1]),
                                                      ALU.is_equal)
                    step(ins)
                    nc.vector.tensor_tensor(CN[:, :, :], OH[:, 0], OH[:, 1], ALU.add).then_inc(s_cn, 1)
                    nc.vector.memset(CP[:, 0, :], 0.0)
                    step(nc.vector.memset(TB[:, 0:1], 0.0))
                    for t in range(1, TILES):
                        ins = nc.vector.memset(TH[:, t:t + 1], float(t * P))
                    dve.wait_ge(s_rk, 1)
                    for t in range(TILES):
                        step(nc.vector.tensor_tensor(CP[:, t + 1, :], CP[:, t, :], pC[:, t, :], ALU.add))
                    step(nc.vector.tensor_tensor(
                        NG[:, :, 1:TILES], CP[:, TILES, :].unsqueeze(2).to_broadcast([P, NE1, TILES - 1]),
                        TH[:, 1:TILES].unsqueeze(1).to_broadcast([P, NE1, TILES - 1]), ALU.is_gt))
                    step(nc.vector.tensor_reduce(NT[:, :], NG[:, :, 1:TILES], AX.X, ALU.add))
                    step(nc.vector.tensor_scalar(NT[:, :], NT[:, :], 1.0, None, ALU.add))
                    for e in range(NE1):
                        step(nc.vector.tensor_tensor(TB[:, e + 1:e + 2], TB[:, e:e + 1], NT[:, e:e + 1], ALU.add))
                    step(nc.vector.scalar_tensor_tensor(
                        out=BS[:, :, :], in0=TB[:, 0:NE1].unsqueeze(1).to_broadcast([P, TILES, NE1]), scalar=float(P),
                        in1=CP[:, 0:TILES, :], op0=ALU.mult, op1=ALU.add))
                    step(nc.vector.tensor_tensor(SL[:, :, :], pR[:, :, :], BS[:, :, :], ALU.add))
                    for i in range(TOP):
                        ins = nc.vector.tensor_tensor(SX[:, i], SL[:, :, :], OH[:, i], ALU.mult)
                    step(ins)
                    for i in range(TOP):
                        ins = nc.vector.tensor_reduce(PF[:, i, :], SX[:, i], AX.X, ALU.add)
                    step(ins)
                    nc.vector.tensor_copy(POS[:, :, :], PF[:, :, :]).then_inc(s_pos, 1)
                    for e in range(1, NE1):
                        ins = nc.vector.tensor_scalar(GE[0:1, e - 1, :], g["tile_no"][0:1, :], TB[0:1, e:e + 1], None,
                                                      ALU.is_ge)
                    step(ins)
                    step(nc.vector.tensor_reduce(EF[:, :], GE[:, :, :].rearrange("p e t -> p t e"), AX.X, ALU.add))
                    nc.vector.tensor_copy(E32[:, :], EF[:, :]).then_inc(s_e, 1)
                    dve.wait_ge(s_ex, 1)
                    step(nc.vector.tensor_scalar(E1[:, :], EX[:, :], 1.0, None, ALU.add))
                    step(nc.vector.reciprocal(WT[:, 0, :], E1[:, :]))
                    nc.vector.tensor_tensor(WT[:, 1, :], WT[:, 0, :], EX[:, :], ALU.mult)

                @block.scalar
                def _(act):
                    act.wait_ge(s_df, 1)
                    nc.scalar.activation(EX[:, :], DF[:, :], ACT.Exp).then_inc(s_ex, 1)

                @block.tensor
                def _(pe):
                    pe.wait_ge(s_cn, 1)
                    nc.tensor.matmul(pR[:, :, :], TRI[:, :], CN[:, :, :], start=True, stop=True)
                    nc.tensor.matmul(pC[:, :, :], ONE[:, :], CN[:, :, :], start=True, stop=True).then_inc(s_rk, 1)

                @block.gpsimd
                def _(pool):
                    pool.wait_ge(s_pos, 1)
                    for t in range(TILES):
                        for i in range(TOP):
                            pool.indirect_dma_start(xs, bass.IndirectOffsetOnAxis(ap=POS[:, i, t:t + 1], axis=0),
                                                    X[:, t, :], None).then_inc(s_sc, 16)
                    pool.wait_ge(s_sc, 16 * TILES * TOP)

        with ExitStack() as ctx2:
            a2 = Scope(nc, ctx2, tag + "e")
            XF = X[:, :, :].rearrange("p t d -> p (t d)")
            H = XF[:, 0:2 * F1].rearrange("p (i f) -> p i f", i=2)
            HT = XF[:, 2 * F1:3 * F1].rearrange("p (f t) -> p f t", f=FT1)
            XS = XF[:, 3 * F1:3 * F1 + 2 * D].rearrange("p (i d) -> p i d", i=2)
            XST = XF[:, 3 * F1 + 2 * D:4 * F1].rearrange("p (i k t) -> p i k t", i=2, k=KT)
            Y = a2.sb("y", [P, 2, D])
            s_xs = [a2.sem(f"slots_loaded{i}") for i in range(2)]
            s_ys = [a2.sem(f"y_stored{i}") for i in range(2)]
            s_t, s_te = a2.sem("x_transposed"), a2.sem("xt_ready")
            s_g, s_u, s_ge, s_h = a2.sem("gate"), a2.sem("up"), a2.sem("gelu"), a2.sem("hidden")
            s_ht, s_h0, s_h1 = a2.sem("hidden_transposed"), a2.sem("ht0_ready"), a2.sem("ht1_ready")
            s_y, s_ye = a2.sem("down"), a2.sem("y_ready")
            pX = a2.ps("pX", [P, KT, P])
            pG = [a2.ps(f"pG{j}", [P, 512]) for j in range(2)]
            pU = [a2.ps(f"pU{j}", [P, 512]) for j in range(2)]
            pH = [a2.ps(f"pH{j}", [P, 512]) for j in range(2)]
            pY = a2.ps("pY", [P, D])
            NT_ = SLOT_TILES

            def tiles(eng, step, drain, between=lambda: None):
                step(0, 0)
                step(1, 1)
                between()
                with eng.Fori(1, NT_ // 2) as j:
                    step(j * 2, 0)
                    step(j * 2 + 1, 1)
                if NT_ % 2:
                    step(NT_ - 1, 0)
                drain(NT_ - 1)

            with nc.Block() as block:
                @block.sync
                def _(sp):
                    def step(t, i):
                        wait(sp, s_t, t - 1)
                        sp.dma_start(XS[:, i, :], xs.rearrange("(t p) d -> p t d", p=P)[:, bass.ds(t, 1), :]
                                     .rearrange("p a d -> p (a d)")).then_inc(s_xs[i], 16)

                    tiles(sp, step, lambda t: None, lambda: load_expert(sp, NE1 - 1))

                @block.tensor
                def _(pe):
                    def turn(t, i):
                        pe.wait_ge(s_xs[i], half(t, i, 16))
                        wait(pe, s_te, t)
                        for k in range(KT):
                            mm = nc.tensor.transpose(pX[:, k, :], XS[:, i, k * P:(k + 1) * P], g["ident"][:, :])
                        mm.then_inc(s_t, 1)

                    def gate_up(t, i):
                        e = pe.value_load(E32[0:1, bass.ds(t, 1)], min_val=0, max_val=NE1 - 1)
                        pe.wait_ge(s_te, t + 1)
                        for n in range(2):
                            for bank, off, done in ((pG, 0, s_g), (pU, F1, s_u)):
                                wait(pe, s_ge if bank is pG else s_h, 2 * t + n - 1)
                                for k in range(KT):
                                    mm = nc.tensor.matmul(bank[n][:, :], XST[:, i, k, :],
                                                          W[:, bass.ds(e * WE + (k * 2 * F1 + off + n * 512), 512)],
                                                          start=(k == 0), stop=(k == KT - 1))
                                mm.then_inc(done, 1)

                    def hidden_across(t, i):
                        pe.wait_ge(s_h, 2 * t + 2)
                        wait(pe, s_h0, t)
                        wait(pe, s_h1, t)
                        for f in range(FT1):
                            mm = nc.tensor.transpose(pH[f // 4][:, (f % 4) * P:(f % 4) * P + P],
                                                     H[:, i, f * P:(f + 1) * P], g["ident"][:, :])
                            if f % 4 == 3:
                                mm.then_inc(s_ht, 1)

                    def down(t):
                        e = pe.value_load(E32[0:1, bass.ds(t, 1)], min_val=0, max_val=NE1 - 1)
                        wait(pe, s_ye, t)
                        for f in range(FT1):
                            if f == 0:
                                pe.wait_ge(s_h0, t + 1)
                            if f == FT1 // 2:
                                pe.wait_ge(s_h1, t + 1)
                            mm = nc.tensor.matmul(pY[:, :], HT[:, f, :], W[:, bass.ds(e * WE + (GU + f * D), D)],
                                                  start=(f == 0), stop=(f == FT1 - 1))
                        mm.then_inc(s_y, 1)

                    def step(t, i):
                        gate_up(t, i)
                        first = is_first(t)
                        if not first:
                            hidden_across(t - 1, 1 - i)
                        if not (isinstance(t, int) and t == NT_ - 1):
                            turn(t + 1, 1 - i)
                        if not first:
                            down(t - 1)

                    def drain(t):
                        hidden_across(t, t % 2)
                        down(t)

                    pe.wait_ge(s_we, NWE - 32)
                    turn(0, 0)
                    tiles(pe, step, drain, lambda: pe.wait_ge(s_we, NWE))

                @block.scalar
                def _(act):
                    def store(t, i):
                        act.wait_ge(s_ye, t + 1)
                        act.dma_start(ys.rearrange("(t p) d -> p t d", p=P)[:, bass.ds(t, 1), :]
                                      .rearrange("p a d -> p (a d)"), Y[:, i, :]).then_inc(s_ys[i], 16)

                    def step(t, i):
                        for n in range(2):
                            act.wait_ge(s_g, 2 * t + n + 1)
                            if n == 0:
                                wait(act, s_ht, 2 * t - 2)
                            nc.scalar.activation(H[:, i, n * 512:(n + 1) * 512], pG[n][:, :],
                                                 ACT.Gelu).then_inc(s_ge, 1)
                        if not is_first(t):
                            finish(t - 1, 1 - i)

                    def finish(t, i):
                        act.wait_ge(s_ht, 2 * t + 1)
                        wait(act, s_y, t)
                        nc.scalar.copy(HT[:, 0:4, :], pH[0][:, :].rearrange("p (f t) -> p f t", t=P)).then_inc(s_h0, 1)
                        store(t, i)

                    tiles(act, step, lambda t: finish(t, t % 2))
                    for i in range(2):
                        act.wait_ge(s_ys[i], half(NT_ - 1 if (NT_ - 1) % 2 == i else NT_ - 2, i, 16))

                @block.vector
                def _(dve):
                    def rows_across(t, i):
                        dve.wait_ge(s_t, t + 1)
                        wait(dve, s_u, 2 * t - 2)
                        nc.vector.tensor_copy(XST[:, i, :, :], pX[:, :, :]).then_inc(s_te, 1)

                    def step(t, i):
                        if not is_first(t):
                            across(t - 1)
                        if not (isinstance(t, int) and t == NT_ - 1):
                            rows_across(t + 1, 1 - i)
                        if not is_first(t):
                            out_rows(t - 1, 1 - i)
                        gated(t, i)

                    def gated(t, i):
                        for n in range(2):
                            dve.wait_ge(s_ge, 2 * t + n + 1)
                            dve.wait_ge(s_u, 2 * t + n + 1)
                            h = H[:, i, n * 512:(n + 1) * 512]
                            nc.vector.tensor_tensor(h, pU[n][:, :], h, ALU.mult).then_inc(s_h, 1)

                    def across(t):
                        dve.wait_ge(s_ht, 2 * t + 2)
                        wait(dve, s_y, t)
                        nc.vector.tensor_copy(HT[:, 4:8, :], pH[1][:, :].rearrange("p (f t) -> p f t", t=P)
                                              ).then_inc(s_h1, 1)

                    def out_rows(t, i):
                        dve.wait_ge(s_y, t + 1)
                        if not (isinstance(t, int) and t < 2):
                            dve.wait_ge(s_ys[i], half(t - 2, i, 16))
                        nc.vector.tensor_copy(Y[:, i, :], pY[:, :]).then_inc(s_ye, 1)

                    def drain(t):
                        across(t)
                        out_rows(t, t % 2)

                    rows_across(0, 0)
                    tiles(dve, step, drain)

        with ExitStack() as ctx2:
            a2 = Scope(nc, ctx2, tag + "c")
            XM = X
            YG = W[:, 0:TILES * TOP * D].rearrange("p (t i d) -> p t i d", t=TILES, i=TOP)
            GT = 2
            s_xm, s_yg = a2.sem("x_loaded"), [a2.sem(f"rows_gathered{q}") for q in range(TILES // GT)]
            s_a, s_o, s_st = a2.sem("first_added"), a2.sem("out_ready"), a2.sem("out_stored")
            with nc.Block() as block:
                @block.sync
                def _(sp):
                    sp.dma_start(XM[:, :, :], x_mid.rearrange("(t p) d -> p t d", p=P)).then_inc(s_xm, 16)
                    for t in range(0, TILES, GT):
                        sp.wait_ge(s_o, t + GT)
                        sp.dma_start(out.rearrange("(t p) d -> p t d", p=P)[:, t:t + GT, :],
                                     XM[:, t:t + GT, :]).then_inc(s_st, 16)
                    sp.wait_ge(s_st, 16 * (TILES // GT))

                @block.gpsimd
                def _(pool):
                    for t in range(TILES):
                        for i in range(TOP):
                            pool.indirect_dma_start(YG[:, t, i, :], None, ys,
                                                    bass.IndirectOffsetOnAxis(ap=POS[:, i, t:t + 1], axis=0)
                                                    ).then_inc(s_yg[t // GT], 16)

                @block.vector
                def _(dve):
                    dve.wait_ge(s_xm, 16)
                    for t in range(TILES):
                        if t % GT == 0:
                            dve.wait_ge(s_yg[t // GT], 16 * GT * TOP)
                        nc.vector.scalar_tensor_tensor(out=XM[:, t, :], in0=YG[:, t, 0, :],
                                                       scalar=WT[:, 0, t:t + 1], in1=XM[:, t, :],
                                                       op0=ALU.mult, op1=ALU.add).then_inc(s_a, 1)
                        dve.wait_ge(s_a, t + 1)
                        nc.vector.scalar_tensor_tensor(out=XM[:, t, :], in0=YG[:, t, 1, :],
                                                       scalar=WT[:, 1, t:t + 1], in1=XM[:, t, :],
                                                       op0=ALU.mult, op1=ALU.add).then_inc(s_o, 1)


SMALL = {"L0x": ("L0_xattn_", "Wo", "bo"), "L0a": ("L0_attn_", "Wp", "bp"), "L1a": ("L1_attn_", "Wo", "bo")}


def load_phase(nc, dram, X, g):
    x = dram["x"].rearrange("(t p) d -> p t d", p=P)
    loads = [(X[:, 0:TPC, :], x[:, 0:TPC, :])]
    loads += [(g[k][:, :], dram[k]) for k in ("ident", "causal", "halves", "cos", "sin", "tile_no")]
    with nc.Block() as block:
        @block.sync
        def _(sp):
            for dst, src in loads:
                sp.dma_start(dst, src).then_inc(g["loaded"], 16)
            sp.wait_ge(g["loaded"], 16 * len(loads))

        @block.gpsimd
        def _(pool):
            nc.gpsimd.memset(g["mhalf"][:, :], -0.5).then_inc(g["made"], 1)
            nc.gpsimd.memset(g["eps"][:, :], EPS).then_inc(g["made"], 1)


def build_program(nc, dram, out):
    with ExitStack() as ctx:
        a = Scope(nc, ctx, "all")
        X = a.sb("x", [P, TILES, D])
        shapes = {"ident": [P, P], "causal": [P, L], "halves": [P, 2], "cos": [P, HD], "sin": [P, HD],
                  "mhalf": [P, TPC], "eps": [P, TPC], "tile_no": [1, SLOT_TILES], "spare": [P, 1]}
        g = {name: a.sb(name, shape) for name, shape in shapes.items()}
        g.update(loaded=a.sem("loaded"), x_rest=a.sem("x_rest_loaded"), made=a.sem("made"))
        load_phase(nc, dram, X, g)
        x = dram["x"].rearrange("(t p) d -> p t d", p=P)
        small_attentions(nc, "L0", X, g, dram, False,
                         [Layer("L0x", 0, True, False, dram["ctx_head"]), Layer("L0a", PASSES, True, True, None)],
                         x_rest=(X[:, TPC:TILES, :], x[:, TPC:TILES, :]))
        routed_ffn0(nc, "L0f", X, g, dram)
        cross_attention(nc, "L1x", X, g, dram)
        small_attentions(nc, "L1", X, g, dram, True, [Layer("L1a", 0, False, False, None)])
        routed_ffn1(nc, "L1f", X, g, dram, out)


def lay_out(inputs):
    f = {k: np.asarray(v) for k, v in inputs.items()}
    arr = {"x": f["x"].reshape(TOK, D)}
    arr["ctx_head"] = f["ctx_1024"][:, :L, :].reshape(TOK, D).T
    for tag, (pre, wo, bo) in SMALL.items():
        for kind in "qkv":
            arr[f"{tag}_{kind}T"] = f[f"{pre}W{kind}"].T
            arr[f"{tag}_b{kind}"] = f[f"{pre}b{kind}"]
        arr[f"{tag}_oT"] = f[pre + wo].T
        arr[f"{tag}_bo"] = f[pre + bo]
    arr["ctx"], arr["ctxT"] = f["ctx_1024"], f["ctx_1024"].transpose(0, 2, 1)
    arr["ctx_last"] = f["ctx_1024"][:, -1, :]
    arr["stack_masks"] = np.array([[1, 0], [1, 0], [0, 1]], np.float32)
    for kind in "qvo":
        arr[f"L1x_{kind}T"] = f[f"L1_xattn_W{kind}"].T
        arr[f"L1x_b{kind}"] = f[f"L1_xattn_b{kind}"]
    arr["L1x_k"] = f["L1_xattn_Wk"]
    arr["ffn1_rT"] = f["L1_ffn_gate_w"].T
    arr["ffn1_gu"] = f["L1_ffn_gate_up_w"].transpose(0, 2, 1)
    arr["ffn1_d"] = f["L1_ffn_down_w"].transpose(0, 2, 1)
    arr["tile_no"] = np.arange(SLOT_TILES, dtype=np.float32)[None, :]
    arr["before"] = np.triu(np.ones((P, P), np.float32), 1)
    arr["ffn0_rT"], arr["ffn0_rb"] = f["L0_ffn_router_w"].T, f["L0_ffn_router_b"]
    arr["ffn0_w1"] = f["L0_ffn_weights1"].transpose(1, 0, 2).reshape(D, NE0 * H0)
    arr["ffn0_b1"] = f["L0_ffn_bias1"].reshape(NE0 * H0)
    arr["ffn0_w2"] = f["L0_ffn_weights2"].reshape(NE0 * H0, D)
    arr["ffn0_b2"] = f["L0_ffn_bias2"]
    arr["iota32"] = np.tile(np.arange(NE0, dtype=np.float32), (P, 1))
    arr["pair_select"] = (np.arange(NE0)[:, None] == np.arange(NE0 * H0)[None, :] // H0).astype(np.float32)
    cos, sin = rope_tables()
    q = np.arange(P) % L
    arr.update(ident=np.eye(P, dtype=np.float32), cos=cos, sin=sin,
               causal=np.where(np.arange(L)[None, :] > q[:, None], NEG, 0.0).astype(np.float32),
               halves=np.stack([(np.arange(P) // HD) % 2 == e for e in range(2)], 1).astype(np.float32))
    return {k: np.ascontiguousarray(v) for k, v in arr.items()}


def kernel(**inputs):
    import concourse.bacc as bacc
    from concourse.bass_utils import run_bass_kernel_spmd

    arr = lay_out(inputs)
    nc = bacc.Bacc("TRN2", target_bir_lowering=False, num_devices=1, dynamic_dma_scratch_size=8192)
    dram = {k: nc.dram_tensor(f"in_{k}", v.shape, mybir.dt.from_np(v.dtype), kind="ExternalInput").ap()
            for k, v in arr.items()}
    out = nc.dram_tensor("out", (TOK, D), F32, kind="ExternalOutput").ap()
    build_program(nc, dram, out)
    r = run_bass_kernel_spmd(nc, [{f"in_{k}": v for k, v in arr.items()}], core_ids=[0])
    return r.results[0]["out"].reshape(B, L, D)
```
